# Optimizing a Trainium2 kernel written in Bass

```python
import numpy as np
import jax
import jax.numpy as jnp

def _softmax(x, axis=-1):
    return jax.nn.softmax(x, axis=axis)

def _gelu(x):
    return jax.nn.gelu(x, approximate=True)

def _silu(x):
    return jax.nn.silu(x)

def _sigmoid(x):
    return jax.nn.sigmoid(x)

def _layernorm(x, axis=-1, eps=1e-05):
    m = jnp.mean(x, axis=axis, keepdims=True)
    v = jnp.var(x, axis=axis, keepdims=True)
    return (x - m) / jnp.sqrt(v + eps)

def _scatter_add(tgt, idx, src, axis=0):
    return tgt.at[idx].add(src)

def _segment_sum(src, seg, n):
    return jax.ops.segment_sum(src, seg, n)
kernel_name = 'mk_xattn_seq_d2_seqx_r2_fe99fa'

def setup_inputs(seed: int=0):
    np.random.seed(seed)
    _w = jnp.asarray

    def _rec_inputs():
        import jax
        import jax.numpy as jnp
        _rk = jax.random.key(seed)
        x = -0.0002928 + 1 * jax.random.normal(jax.random.fold_in(_rk, 1), (8, 512, 512), jnp.float32)
        _lenS = 512 - jax.random.randint(jax.random.fold_in(_rk, 7), (8,), 0, max(1, 512 // 4) + 1, jnp.int32)
        _lenS2 = 77 - jax.random.randint(jax.random.fold_in(_rk, 8), (8,), 0, max(1, 77 // 4) + 1, jnp.int32)
        _ctx_768P = jax.random.normal(jax.random.fold_in(_rk, 11), (8, 16, 384), jnp.float32)
        _ctx_768c = jax.random.dirichlet(jax.random.fold_in(_rk, 511), 0.3 * jnp.ones((16,), jnp.float32), (8, 77))
        _ctx_768t = jnp.einsum('bsk,bkd->bsd', _ctx_768c, _ctx_768P)
        _ctx_768t = _ctx_768t * jax.lax.rsqrt(jnp.mean(jnp.square(_ctx_768t)) + 1e-12) * 0.953939
        ctx_768 = 2.09791e-05 + 1.00001 * (_ctx_768t + 0.3 * jax.random.normal(jax.random.fold_in(_rk, 611), (8, 77, 384), jnp.float32))
        return (x, ctx_768)
    x, ctx_768 = _rec_inputs()

    def _L0_xattn_setup():
        import jax, jax.numpy as jnp
        import numpy as np
        DIM1, DIM2, H = (512, 384, 16)
        HID = 4 * DIM1
        EPS = 1e-05

        def layernorm(x, w, b):
            mu = jnp.mean(x, axis=-1, keepdims=True)
            var = jnp.mean((x - mu) ** 2, axis=-1, keepdims=True)
            return (x - mu) * jax.lax.rsqrt(var + EPS) * w + b
        key = jax.random.key(seed)
        ks = jax.random.split(key, 12)
        s1 = 1.0 / np.sqrt(DIM1)
        s2 = 1.0 / np.sqrt(DIM2)
        sh = 1.0 / np.sqrt(HID)
        return {'x': jax.random.normal(ks[0], (4, 512, DIM1), jnp.float32), 'y': jax.random.normal(ks[1], (4, 512, DIM2), jnp.float32), 'ln1_w': jnp.ones((DIM1,), jnp.float32), 'ln1_b': jnp.zeros((DIM1,), jnp.float32), 'ln2_w': jnp.ones((DIM2,), jnp.float32), 'ln2_b': jnp.zeros((DIM2,), jnp.float32), 'ln3_w': jnp.ones((DIM1,), jnp.float32), 'ln3_b': jnp.zeros((DIM1,), jnp.float32), 'Wq': jax.random.uniform(ks[2], (DIM1, DIM1), jnp.float32, -s1, s1), 'Wkv': jax.random.uniform(ks[3], (DIM2, 2 * DIM1), jnp.float32, -s2, s2), 'Wproj': jax.random.uniform(ks[4], (DIM1, DIM1), jnp.float32, -s1, s1), 'bproj': jnp.zeros((DIM1,), jnp.float32), 'W1': jax.random.uniform(ks[5], (DIM1, HID), jnp.float32, -s1, s1), 'b1': jnp.zeros((HID,), jnp.float32), 'W2': jax.random.uniform(ks[6], (HID, DIM1), jnp.float32, -sh, sh), 'b2': jnp.zeros((DIM1,), jnp.float32)}
    _L0_xattn_all = _L0_xattn_setup()
    _L0_xattn_in = {k: v for k, v in _L0_xattn_all.items() if k in ('ln1_w', 'ln1_b', 'ln2_w', 'ln2_b', 'ln3_w', 'ln3_b', 'Wq', 'Wkv', 'Wproj', 'bproj', 'W1', 'b1', 'W2', 'b2')}
    del _L0_xattn_all

    def _L1_xattn_setup():
        import jax, jax.numpy as jnp
        import numpy as np
        B, S, L = (2, 1024, 256)
        WIDTH, HEADS, CTX = (512, 16, 384)
        HD = WIDTH // HEADS
        EPS = 1e-05

        def _layernorm(x, g, b):
            m = jnp.mean(x, axis=-1, keepdims=True)
            v = jnp.mean(jnp.square(x - m), axis=-1, keepdims=True)
            return (x - m) * jax.lax.rsqrt(v + EPS) * g + b

        def _mha(q_in, kv_in, wq, bq, wk, bk, wv, bv, wo, bo):
            b = q_in.shape[0]
            q = (q_in @ wq.T + bq).reshape(b, -1, HEADS, HD).transpose(0, 2, 1, 3)
            k = (kv_in @ wk.T + bk).reshape(b, -1, HEADS, HD).transpose(0, 2, 1, 3)
            v = (kv_in @ wv.T + bv).reshape(b, -1, HEADS, HD).transpose(0, 2, 1, 3)
            scores = jnp.einsum('bhqd,bhkd->bhqk', q, k) * HD ** (-0.5)
            p = jax.nn.softmax(scores, axis=-1)
            o = jnp.einsum('bhqk,bhkd->bhqd', p, v)
            o = o.transpose(0, 2, 1, 3).reshape(b, -1, WIDTH)
            return o @ wo.T + bo
        key = jax.random.key(seed)
        ks = jax.random.split(key, 32)

        def xav(k, shape, gain=1.0):
            fan_out, fan_in = shape
            a = gain * np.sqrt(6.0 / (fan_in + fan_out))
            return jax.random.uniform(k, shape, jnp.float32, -a, a)
        g2 = 1.0 / np.sqrt(2.0)
        inp = {'x': jax.random.normal(ks[0], (B, S, WIDTH), jnp.float32), 'context': jax.random.normal(ks[1], (B, L, CTX), jnp.float32), 'ln1_g': jnp.ones((WIDTH,), jnp.float32), 'ln1_b': jnp.zeros((WIDTH,), jnp.float32), 'ln2_g': jnp.ones((WIDTH,), jnp.float32), 'ln2_b': jnp.zeros((WIDTH,), jnp.float32), 'ln3_g': jnp.ones((WIDTH,), jnp.float32), 'ln3_b': jnp.zeros((WIDTH,), jnp.float32), 'sa_wq': xav(ks[2], (WIDTH, WIDTH), g2), 'sa_bq': jnp.zeros((WIDTH,), jnp.float32), 'sa_wk': xav(ks[3], (WIDTH, WIDTH), g2), 'sa_bk': jnp.zeros((WIDTH,), jnp.float32), 'sa_wv': xav(ks[4], (WIDTH, WIDTH), g2), 'sa_bv': jnp.zeros((WIDTH,), jnp.float32), 'sa_wo': xav(ks[5], (WIDTH, WIDTH), 1.0), 'sa_bo': jnp.zeros((WIDTH,), jnp.float32), 'ca_wq': xav(ks[6], (WIDTH, WIDTH), g2), 'ca_bq': jnp.zeros((WIDTH,), jnp.float32), 'ca_wk': xav(ks[7], (WIDTH, CTX), g2), 'ca_bk': jnp.zeros((WIDTH,), jnp.float32), 'ca_wv': xav(ks[8], (WIDTH, CTX), g2), 'ca_bv': jnp.zeros((WIDTH,), jnp.float32), 'ca_wo': xav(ks[9], (WIDTH, WIDTH), 1.0), 'ca_bo': jnp.zeros((WIDTH,), jnp.float32), 'mlp_w1': 0.02 * jax.random.normal(ks[10], (4 * WIDTH, WIDTH), jnp.float32), 'mlp_b1': jnp.zeros((4 * WIDTH,), jnp.float32), 'mlp_w2': 0.02 * jax.random.normal(ks[11], (WIDTH, 4 * WIDTH), jnp.float32), 'mlp_b2': jnp.zeros((WIDTH,), jnp.float32)}
        return inp
    _L1_xattn_all = _L1_xattn_setup()
    _L1_xattn_in = {k: v for k, v in _L1_xattn_all.items() if k in ('ln1_g', 'ln1_b', 'ln2_g', 'ln2_b', 'ln3_g', 'ln3_b', 'sa_wq', 'sa_bq', 'sa_wk', 'sa_bk', 'sa_wv', 'sa_bv', 'sa_wo', 'sa_bo', 'ca_wq', 'ca_bq', 'ca_wk', 'ca_bk', 'ca_wv', 'ca_bv', 'ca_wo', 'ca_bo', 'mlp_w1', 'mlp_b1', 'mlp_w2', 'mlp_b2')}
    del _L1_xattn_all
    return {'x': x, 'ctx_768': ctx_768, 'L0_xattn_ln1_w': _L0_xattn_in['ln1_w'], 'L0_xattn_ln1_b': _L0_xattn_in['ln1_b'], 'L0_xattn_ln2_w': _L0_xattn_in['ln2_w'], 'L0_xattn_ln2_b': _L0_xattn_in['ln2_b'], 'L0_xattn_ln3_w': _L0_xattn_in['ln3_w'], 'L0_xattn_ln3_b': _L0_xattn_in['ln3_b'], 'L0_xattn_Wq': _L0_xattn_in['Wq'], 'L0_xattn_Wkv': _L0_xattn_in['Wkv'], 'L0_xattn_Wproj': _L0_xattn_in['Wproj'], 'L0_xattn_bproj': _L0_xattn_in['bproj'], 'L0_xattn_W1': _L0_xattn_in['W1'], 'L0_xattn_b1': _L0_xattn_in['b1'], 'L0_xattn_W2': _L0_xattn_in['W2'], 'L0_xattn_b2': _L0_xattn_in['b2'], 'L1_xattn_ln1_g': _L1_xattn_in['ln1_g'], 'L1_xattn_ln1_b': _L1_xattn_in['ln1_b'], 'L1_xattn_ln2_g': _L1_xattn_in['ln2_g'], 'L1_xattn_ln2_b': _L1_xattn_in['ln2_b'], 'L1_xattn_ln3_g': _L1_xattn_in['ln3_g'], 'L1_xattn_ln3_b': _L1_xattn_in['ln3_b'], 'L1_xattn_sa_wq': _L1_xattn_in['sa_wq'], 'L1_xattn_sa_bq': _L1_xattn_in['sa_bq'], 'L1_xattn_sa_wk': _L1_xattn_in['sa_wk'], 'L1_xattn_sa_bk': _L1_xattn_in['sa_bk'], 'L1_xattn_sa_wv': _L1_xattn_in['sa_wv'], 'L1_xattn_sa_bv': _L1_xattn_in['sa_bv'], 'L1_xattn_sa_wo': _L1_xattn_in['sa_wo'], 'L1_xattn_sa_bo': _L1_xattn_in['sa_bo'], 'L1_xattn_ca_wq': _L1_xattn_in['ca_wq'], 'L1_xattn_ca_bq': _L1_xattn_in['ca_bq'], 'L1_xattn_ca_wk': _L1_xattn_in['ca_wk'], 'L1_xattn_ca_bk': _L1_xattn_in['ca_bk'], 'L1_xattn_ca_wv': _L1_xattn_in['ca_wv'], 'L1_xattn_ca_bv': _L1_xattn_in['ca_bv'], 'L1_xattn_ca_wo': _L1_xattn_in['ca_wo'], 'L1_xattn_ca_bo': _L1_xattn_in['ca_bo'], 'L1_xattn_mlp_w1': _L1_xattn_in['mlp_w1'], 'L1_xattn_mlp_b1': _L1_xattn_in['mlp_b1'], 'L1_xattn_mlp_w2': _L1_xattn_in['mlp_w2'], 'L1_xattn_mlp_b2': _L1_xattn_in['mlp_b2']}

def reference(x, ctx_768, L0_xattn_ln1_w, L0_xattn_ln1_b, L0_xattn_ln2_w, L0_xattn_ln2_b, L0_xattn_ln3_w, L0_xattn_ln3_b, L0_xattn_Wq, L0_xattn_Wkv, L0_xattn_Wproj, L0_xattn_bproj, L0_xattn_W1, L0_xattn_b1, L0_xattn_W2, L0_xattn_b2, L1_xattn_ln1_g, L1_xattn_ln1_b, L1_xattn_ln2_g, L1_xattn_ln2_b, L1_xattn_ln3_g, L1_xattn_ln3_b, L1_xattn_sa_wq, L1_xattn_sa_bq, L1_xattn_sa_wk, L1_xattn_sa_bk, L1_xattn_sa_wv, L1_xattn_sa_bv, L1_xattn_sa_wo, L1_xattn_sa_bo, L1_xattn_ca_wq, L1_xattn_ca_bq, L1_xattn_ca_wk, L1_xattn_ca_bk, L1_xattn_ca_wv, L1_xattn_ca_bv, L1_xattn_ca_wo, L1_xattn_ca_bo, L1_xattn_mlp_w1, L1_xattn_mlp_b1, L1_xattn_mlp_w2, L1_xattn_mlp_b2):
    import jax
    import jax.numpy as jnp

    def _L0_xattn_ref(x, y, ln1_w, ln1_b, ln2_w, ln2_b, ln3_w, ln3_b, Wq, Wkv, Wproj, bproj, W1, b1, W2, b2):
        import jax, jax.numpy as jnp
        import numpy as np
        DIM1, DIM2, H = (512, 384, 16)
        HID = 4 * DIM1
        EPS = 1e-05

        def layernorm(x, w, b):
            mu = jnp.mean(x, axis=-1, keepdims=True)
            var = jnp.mean((x - mu) ** 2, axis=-1, keepdims=True)
            return (x - mu) * jax.lax.rsqrt(var + EPS) * w + b
        B, N1, C1 = x.shape
        hd = C1 // H
        scale = hd ** (-0.5)
        xn = layernorm(x, ln1_w, ln1_b)
        yn = layernorm(y, ln2_w, ln2_b)
        q = (xn @ Wq).reshape(B, N1, H, hd).transpose(0, 2, 1, 3)
        kv = (yn @ Wkv).reshape(B, y.shape[1], 2, H, hd)
        k = kv[:, :, 0].transpose(0, 2, 1, 3)
        v = kv[:, :, 1].transpose(0, 2, 1, 3)
        attn = jax.nn.softmax(jnp.einsum('bhqd,bhkd->bhqk', q, k) * scale, axis=-1)
        o = jnp.einsum('bhqk,bhkd->bhqd', attn, v).transpose(0, 2, 1, 3).reshape(B, N1, C1)
        x = x + (o @ Wproj + bproj)
        h = jax.nn.gelu(layernorm(x, ln3_w, ln3_b) @ W1 + b1, approximate=False)
        x = x + (h @ W2 + b2)
        return x

    def _L1_xattn_ref(x, context, ln1_g, ln1_b, ln2_g, ln2_b, ln3_g, ln3_b, sa_wq, sa_bq, sa_wk, sa_bk, sa_wv, sa_bv, sa_wo, sa_bo, ca_wq, ca_bq, ca_wk, ca_bk, ca_wv, ca_bv, ca_wo, ca_bo, mlp_w1, mlp_b1, mlp_w2, mlp_b2):
        import jax, jax.numpy as jnp
        import numpy as np
        B, S, L = (2, 1024, 256)
        WIDTH, HEADS, CTX = (512, 16, 384)
        HD = WIDTH // HEADS
        EPS = 1e-05

        def _layernorm(x, g, b):
            m = jnp.mean(x, axis=-1, keepdims=True)
            v = jnp.mean(jnp.square(x - m), axis=-1, keepdims=True)
            return (x - m) * jax.lax.rsqrt(v + EPS) * g + b

        def _mha(q_in, kv_in, wq, bq, wk, bk, wv, bv, wo, bo):
            b = q_in.shape[0]
            q = (q_in @ wq.T + bq).reshape(b, -1, HEADS, HD).transpose(0, 2, 1, 3)
            k = (kv_in @ wk.T + bk).reshape(b, -1, HEADS, HD).transpose(0, 2, 1, 3)
            v = (kv_in @ wv.T + bv).reshape(b, -1, HEADS, HD).transpose(0, 2, 1, 3)
            scores = jnp.einsum('bhqd,bhkd->bhqk', q, k) * HD ** (-0.5)
            p = jax.nn.softmax(scores, axis=-1)
            o = jnp.einsum('bhqk,bhkd->bhqd', p, v)
            o = o.transpose(0, 2, 1, 3).reshape(b, -1, WIDTH)
            return o @ wo.T + bo
        h = _layernorm(x, ln1_g, ln1_b)
        x = x + _mha(h, h, sa_wq, sa_bq, sa_wk, sa_bk, sa_wv, sa_bv, sa_wo, sa_bo)
        h = _layernorm(x, ln2_g, ln2_b)
        x = x + _mha(h, context, ca_wq, ca_bq, ca_wk, ca_bk, ca_wv, ca_bv, ca_wo, ca_bo)
        h = _layernorm(x, ln3_g, ln3_b)
        h = jax.nn.gelu(h @ mlp_w1.T + mlp_b1, approximate=False) @ mlp_w2.T + mlp_b2
        return x + h
    x = _L0_xattn_ref(x, ctx_768, L0_xattn_ln1_w, L0_xattn_ln1_b, L0_xattn_ln2_w, L0_xattn_ln2_b, L0_xattn_ln3_w, L0_xattn_ln3_b, L0_xattn_Wq, L0_xattn_Wkv, L0_xattn_Wproj, L0_xattn_bproj, L0_xattn_W1, L0_xattn_b1, L0_xattn_W2, L0_xattn_b2)
    x = _L1_xattn_ref(x, ctx_768, L1_xattn_ln1_g, L1_xattn_ln1_b, L1_xattn_ln2_g, L1_xattn_ln2_b, L1_xattn_ln3_g, L1_xattn_ln3_b, L1_xattn_sa_wq, L1_xattn_sa_bq, L1_xattn_sa_wk, L1_xattn_sa_bk, L1_xattn_sa_wv, L1_xattn_sa_bv, L1_xattn_sa_wo, L1_xattn_sa_bo, L1_xattn_ca_wq, L1_xattn_ca_bq, L1_xattn_ca_wk, L1_xattn_ca_bk, L1_xattn_ca_wv, L1_xattn_ca_bv, L1_xattn_ca_wo, L1_xattn_ca_bo, L1_xattn_mlp_w1, L1_xattn_mlp_b1, L1_xattn_mlp_w2, L1_xattn_mlp_b2)
    return x

_drawn_inputs = setup_inputs


def setup_inputs(seed=0):
    import zlib

    import numpy as np

    out = dict(_drawn_inputs(seed))
    spreads = {'L0_xattn_ln1_w': (1.0, 0.6),
     'L0_xattn_ln1_b': (0.0, 0.8),
     'L0_xattn_ln2_w': (1.0, 0.2),
     'L0_xattn_ln2_b': (0.0, 0.1),
     'L0_xattn_ln3_w': (1.0, 0.2),
     'L0_xattn_ln3_b': (0.0, 0.367),
     'L0_xattn_bproj': (0.0, 0.1),
     'L0_xattn_b1': (0.0, 0.1),
     'L0_xattn_b2': (0.0, 0.1),
     'L1_xattn_ln1_g': (1.0, 0.2),
     'L1_xattn_ln1_b': (0.0, 0.1),
     'L1_xattn_ln2_g': (1.0, 0.6),
     'L1_xattn_ln2_b': (0.0, 0.8),
     'L1_xattn_ln3_g': (1.0, 0.2),
     'L1_xattn_ln3_b': (0.0, 0.431),
     'L1_xattn_sa_bq': (0.0, 2.0),
     'L1_xattn_sa_bk': (0.0, 2.0),
     'L1_xattn_sa_bv': (0.0, 0.1),
     'L1_xattn_sa_bo': (0.0, 0.1),
     'L1_xattn_ca_bq': (0.0, 0.8),
     'L1_xattn_ca_bk': (0.0, 2.0),
     'L1_xattn_ca_bv': (0.0, 0.1),
     'L1_xattn_ca_bo': (0.0, 0.1),
     'L1_xattn_mlp_b1': (0.0, 0.1),
     'L1_xattn_mlp_b2': (0.0, 0.1)}
    factors = {'L0_xattn_Wq': 2.895}
    for name, (base, spread) in spreads.items():
        noise = np.random.default_rng([zlib.crc32(name.encode()), seed]).standard_normal(out[name].shape)
        drawn = base * np.exp(spread * noise) if base else spread * noise
        out[name] = jnp.asarray(drawn.astype(out[name].dtype))
    for name, factor in factors.items():
        out[name] = (out[name] * factor).astype(out[name].dtype)
    return out
```

```python
from contextlib import ExitStack

import numpy as np

import concourse.bass as bass
from concourse import mybir

F32 = mybir.dt.float32
F32R = mybir.dt.float32r
ACT = mybir.ActivationFunctionType
ALU = mybir.AluOpType
AX = mybir.AxisListType

P = 128
B, S, D = 8, 512, 512
L, CTX = 77, 384
H, HD = 16, 32
HID = 4 * D
KT = D // P
CT = CTX // P
TT = S // P
G = H // 4
JT = HID // P
GL = 4 * L
SCALE = HD ** -0.5
EPS = 1e-5

S_BANK = [0, 1, 2, 0]
S_STEP = {0: [0, 1], 1: [2, 3], 2: [], 3: []}
S_BEFORE = {0: 1, 1: TT, 2: TT, 3: 3}

COLS = [("L0_ln1_w", D), ("L0_ln1_b", D), ("L0_ln2_w", CTX), ("L0_ln2_b", CTX), ("L0_ln3_w", D), ("L0_ln3_b", D),
        ("L0_b1", HID), ("L1_ln1_g", D), ("L1_ln1_b", D), ("L1_ln2_g", D), ("L1_ln2_b", D), ("L1_ln3_g", D),
        ("L1_ln3_b", D), ("L1_sa_bq", D), ("L1_sa_bk", D), ("L1_sa_bv", D), ("L1_ca_bq", D), ("L1_ca_bk", D),
        ("L1_ca_bv", D), ("L1_mlp_b1", HID)]
COL_AT, NCOL = {}, 0
for _name, _n in COLS:
    COL_AT[_name] = (NCOL, _n // P)
    NCOL += _n // P


class Events:

    def __init__(self, sem, per, unit=1):
        self.sem, self.per, self.unit = sem, per, unit

    def wait(self, eng, b, k, alone=None):
        v = b * (self.per * self.unit) + (k + 1) * self.unit
        if isinstance(v, int):
            if v > 0:
                eng.wait_ge(self.sem, v)
            return
        eng.wait_ge(self.sem, v)
        if alone is not None:
            eng.sem_inc(alone, 1)

    def up(self, instruction):
        instruction.then_inc(self.sem, self.unit)


class Names:
    pass


class Phase:

    def __init__(self, nc, ctx, name):
        self.nc, self.ctx, self.name, self.sems = nc, ctx, name, []
        self.passed = self.events("passed").sem
        ctx.callback(self.end)

    def end(self):
        self.nc.clear_and_free_semaphores(self.sems)
        self.nc.all_engine_barrier()

    def sb(self, name, shape, dt=F32):
        return self.ctx.enter_context(self.nc.sbuf_tensor(f"{self.name}_{name}", shape, dt))

    def banks(self, name, n):
        return [self.ctx.enter_context(self.nc.psum_tensor(f"{self.name}_{name}{i}", [P, 512], F32)) for i in range(n)]

    def events(self, name, per=1, unit=1):
        self.sems.append(self.nc.alloc_semaphore(f"{self.name}_{name}"))
        return Events(self.sems[-1], per, unit)


def run(eng, pro, body):
    pro()
    body(0, False)
    with eng.Fori(1, B - 1) as b:
        body(b, False)
    body(B - 1, True)


def static(b, value):
    return isinstance(b, int) and b == value


def f32(ap):
    return ap.bitcast(F32)


def flat(ap):
    return ap.rearrange("p a n -> p (a n)")



def product(nc, out, wh, wl, xh, xl, first, last):
    nc.tensor.matmul(out, wh, xh, start=first, stop=False)
    nc.tensor.matmul(out, wl, xh, start=False, stop=False)
    return nc.tensor.matmul(out, wh, xl, start=False, stop=last)


def add_hi(nc, hi, bank, bias):
    if bias is None:
        return nc.scalar.activation(hi, bank, ACT.Copy)
    return nc.scalar.activation(hi, bank, ACT.Identity, bias=bias)


def add_lo(nc, lo, hi, bank, bias):
    if bias is None:
        return nc.vector.tensor_tensor(lo, bank, f32(hi), ALU.subtract)
    return nc.vector.scalar_tensor_tensor(lo, bank, bias, f32(hi), ALU.add, ALU.subtract)


def diagonal(ap):
    return bass.AP(ap.tensor, ap.offset, [list(ap.ap[0]), [P + HD, 4], [1, HD]])


def weight_staging(ph, slots, parts=1):
    wt = Names()
    wt.slots = slots
    wt.ns = len(slots)
    wt.chunks = []
    wt.full = [ph.events(f"w_full{i}", 1, 16 * parts) for i in range(len(slots))]
    wt.hi = ph.events("w_hi")
    wt.lo = ph.events("w_lo")
    return wt


def add_matrix(wt, w, hi, lo, scale=1.0, rows=2):
    v = w.rearrange("(c p) n -> p c n", p=P)
    for c in range(0, v.shape[1], rows):
        wt.chunks.append(([v[:, c:c + rows, :]], flat(hi[:, c:c + rows, :]), flat(lo[:, c:c + rows, :]), scale))


def load_weights(sp, wt, first, end):
    for i in range(first, end):
        wt.lo.wait(sp, i - wt.ns, 0)
        at = 0
        for source in wt.chunks[i][0]:
            n = int(np.prod(source.shape[1:]))
            slot = wt.slots[i % wt.ns][:, at:at + n]
            if len(source.shape) == 3:
                slot = slot.rearrange("p (a n) -> p a n", a=source.shape[1])
            sp.dma_start(slot, source).then_inc(wt.full[i % wt.ns].sem, 16)
            at += n


def weight_hi(nc, wt, i):
    _, hi, _, scale = wt.chunks[i]
    return nc.scalar.activation(hi, wt.slots[i % wt.ns][:, 0:hi.shape[1]], ACT.Copy, scale=scale)


def weight_lo(nc, wt, i):
    _, hi, lo, scale = wt.chunks[i]
    return nc.vector.scalar_tensor_tensor(lo, wt.slots[i % wt.ns][:, 0:hi.shape[1]], scale, f32(hi),
                                          ALU.mult, ALU.subtract)


def token_buffers(ph, w, b, pars=1, temps=2):
    x = Names()
    x.w = w
    x.b = b
    x.temps = temps
    x.xs = ph.sb("xs", [P, TT, D])
    x.bias = ph.sb("bias", [P, D])
    x.htmp = ph.sb("htmp", [P, temps, S])
    x.hTh = ph.sb("hTh", [P, pars, KT, S], F32R)
    x.hTl = ph.sb("hTl", [P, pars, KT, S], F32R)
    x.stats = ph.sb("stats", [P, TT, 6])
    x.mv = ph.sb("mv", [P, TT, 2])
    x.ve = ph.sb("ve", [P, TT])
    x.rs = ph.sb("rs", [P, TT])
    x.power = ph.sb("power", [P, TT])
    x.full = [ph.events(f"xs_full{t}", 2, 16) for t in range(TT)]
    x.stored = [ph.events(f"stored{t}", 1, 16) for t in range(TT)]
    x.bias_in = ph.events("bias_in", 1, 16)
    x.e_power = ph.events("power_set")
    x.e_st = ph.events("ln_st", TT)
    x.e_mv = ph.events("ln_mv", TT)
    x.e_ve = ph.events("ln_ve")
    x.e_rs = ph.events("ln_rs")
    x.e_xn = ph.events("ln_xn", TT)
    x.e_tr = ph.events("ln_tr", KT)
    x.e_hf = ph.events("ln_hf", KT)
    x.e_hh = ph.events("ln_hh", KT)
    x.e_hl = ph.events("ln_hl", KT)
    x.e_xb = ph.events("xb", TT)
    x.e_res = ph.events("res", TT)
    return x


def token_tiles(x):
    return x.rearrange("(b t p) d -> b t p d", b=B, p=P)



def ln_stats(nc, x, t):
    return nc.vector.bn_stats(x.stats[:, t, :], x.xs[:, t, :])


def ln_mean(nc, x, t):
    return nc.vector.bn_aggr(x.mv[:, t, :], x.stats[:, t, :])


def ln_power(nc, x):
    return nc.gpsimd.memset(x.power[:, :], -0.5)


def ln_eps(nc, x):
    return nc.gpsimd.tensor_scalar(x.ve[:, :], x.mv[:, :, 1], EPS, 1.0, ALU.add, ALU.mult)


def ln_rsqrt(nc, x):
    return nc.gpsimd.tensor_tensor(x.rs[:, :], x.ve[:, :], x.power[:, :], ALU.pow)


def ln_normalise(nc, x, t):
    return nc.vector.tensor_scalar(x.xs[:, t, :], x.xs[:, t, :], x.mv[:, t, 0:1], x.rs[:, t:t + 1],
                                   ALU.subtract, ALU.mult)


def ln_transpose(nc, x, bank, c, ident):
    for t in range(TT):
        last = nc.tensor.transpose(bank[:, t * P:(t + 1) * P], x.xs[:, t, c * P:(c + 1) * P], ident)
    return last


def ln_whole(nc, x, bank, c):
    return nc.scalar.activation(x.htmp[:, c % x.temps, :], bank[:, :], ACT.Identity, bias=x.b[:, c:c + 1],
                                scale=x.w[:, c:c + 1])


def ln_hi(nc, x, c, par=0):
    return nc.vector.tensor_copy(x.hTh[:, par, c, :], x.htmp[:, c % x.temps, :])


def ln_lo(nc, x, c, par=0):
    return nc.gpsimd.tensor_tensor(x.hTl[:, par, c, :], x.htmp[:, c % x.temps, :], f32(x.hTh[:, par, c, :]),
                                   ALU.subtract)


def add_bias(nc, x, t):
    return nc.gpsimd.tensor_tensor(x.xs[:, t, :], x.xs[:, t, :], x.bias[:, :], ALU.add)


def add_out(nc, x, bank, t):
    return nc.vector.tensor_tensor(x.xs[:, t, :], bank[:, :], x.xs[:, t, :], ALU.add)


def feed_forward(nc, name, cst, x_in, x_out, ln_w, ln_b, w1, b1, w2, b2_row):
    with ExitStack() as ctx:
        ph = Phase(nc, ctx, name)
        Wh, Wl = ph.sb("Wh", [P, JT, 2 * S], F32R), ph.sb("Wl", [P, JT, 2 * S], F32R)
        gf = ph.sb("gf", [P, 2, S])
        gh, gl = ph.sb("gh", [P, 2, S], F32R), ph.sb("gl", [P, 2, S], F32R)
        x = token_buffers(ph, ln_w, ln_b, pars=2)
        x_old, x_new = token_tiles(x_in), token_tiles(x_out)
        wt = weight_staging(ph, [ph.sb(f"stage{i}", [P, 2 * S]) for i in range(2)], parts=2)
        w1v = w1.rearrange("(c p) n -> p c n", p=P)
        w2v = w2.rearrange("(j p) n -> p j n", p=P)
        for j in range(JT):
            wt.chunks.append(([w1v[:, :, j * P:(j + 1) * P], w2v[:, j, :]], Wh[:, j, :], Wl[:, j, :], 1.0))
        T_bank, f1_bank, acc = ph.banks("T", 2), ph.banks("f1", 2), ph.banks("acc", 4)
        e_f1 = ph.events("f1", JT)
        e_g = ph.events("g", JT)
        e_gh = ph.events("gh", JT)
        e_gl = ph.events("gl", JT)
        e_f2 = ph.events("f2", JT - 1)
        e_acc = ph.events("acc", TT)
        FIRST = 4

        def pairs(eng, pro, body):
            pro()
            for par in range(2):
                body(par, par, False)
            with eng.Fori(1, B // 2 - 1) as i:
                for par in range(2):
                    body(i * 2 + par, par, False)
            for par in range(2):
                body(B - 2 + par, par, par == 1)

        block = ctx.enter_context(nc.Block())

        @block.sync
        def _(sp):
            def pro():
                for t in range(TT):
                    x.full[t].up(sp.dma_start(x.xs[:, t, :], x_old[0, t]))
                load_weights(sp, wt, 0, FIRST)
                x.bias_in.up(sp.dma_start(x.bias[:, :], b2_row.partition_broadcast(P)))

            def body(b, par, last):
                if not last:
                    if static(b, 0):
                        x.e_tr.wait(sp, 0, KT - 1)
                    for t in range(TT):
                        x.stored[t].wait(sp, b - 1, 0, ph.passed)
                        x.full[t].up(sp.dma_start(x.xs[:, t, :], x_old[b + 1, t]))
                if static(b, 0):
                    load_weights(sp, wt, FIRST, JT)
                x.e_tr.wait(sp, b if last else b + 1, KT - 1, ph.passed)
                for t in range(TT):
                    x.full[t].up(sp.dma_start(x.xs[:, t, :], x_old[b, t]))
                for t in range(TT):
                    x.e_res.wait(sp, b, t, ph.passed)
                    x.stored[t].up(sp.dma_start(x_new[b, t], x.xs[:, t, :]))
            pairs(sp, pro, body)
            for t in range(TT):
                x.stored[t].wait(sp, B - 1, 0)

        @block.tensor
        def _(pe):
            def T(n, c):
                x.e_xn.wait(pe, n, TT - 1)
                x.e_hf.wait(pe, n, c - 2)
                x.e_tr.up(ln_transpose(nc, x, T_bank[c % 2], c, cst.ident[:, :]))

            def F1(b, par, j):
                if static(b, 0):
                    wt.lo.wait(pe, j, 0)
                if j == 0:
                    x.e_hl.wait(pe, b, KT - 1)
                e_g.wait(pe, b, j - 2)
                for c in range(KT):
                    w = slice(c * P, (c + 1) * P)
                    last = product(nc, f1_bank[j % 2][:, :], Wh[:, j, w], Wl[:, j, w],
                                   x.hTh[:, par, c, :], x.hTl[:, par, c, :], c == 0, c == KT - 1)
                e_f1.up(last)

            def F2(b, j):
                e_gl.wait(pe, b, j)
                for t in range(TT):
                    if j == 0:
                        x.e_res.wait(pe, b, t - TT)
                    ts = slice(t * P, (t + 1) * P)
                    last = product(nc, acc[t][:, :], gh[:, j % 2, ts], gl[:, j % 2, ts], Wh[:, j, S:2 * S],
                                   Wl[:, j, S:2 * S], j == 0, j == JT - 1)
                    if j == JT - 1:
                        e_acc.up(last)
                if j < JT - 1:
                    e_f2.up(last)

            def pro():
                cst.wait_ident(pe)
                for c in range(KT):
                    T(0, c)
                F1(0, 0, 0)

            def body(b, par, last):
                for j in range(1, JT):
                    F1(b, par, j)
                    F2(b, j - 1)
                    if 8 <= j < 12 and not last:
                        T(b + 1, j - 8)
                if not last:
                    F1(b + 1, 1 - par, 0)
                F2(b, JT - 1)
            pairs(pe, pro, body)

        @block.scalar
        def _(act):
            def gelu(b, j):
                e_f1.wait(act, b, j)
                e_gl.wait(act, b, j - 2)
                e_g.up(nc.scalar.activation(gf[:, j % 2, :], f1_bank[j % 2][:, :], ACT.Gelu, bias=b1[:, j:j + 1]))
                e_g.wait(act, b, j)
                if j == 0:
                    e_f2.wait(act, b, -1)
                elif j == 1:
                    e_acc.wait(act, b, -1)
                else:
                    e_f2.wait(act, b, j - 2)
                e_gh.up(nc.scalar.activation(gh[:, j % 2, :], gf[:, j % 2, :], ACT.Copy))

            def weights_hi(i):
                wt.full[i % wt.ns].wait(act, i // wt.ns, 0)
                wt.hi.up(weight_hi(nc, wt, i))

            def whole(n, c):
                x.e_tr.wait(act, n, c)
                x.e_hl.wait(act, n, c - x.temps)
                x.e_hf.up(ln_whole(nc, x, T_bank[c % 2], c))

            def pro():
                cst.wait_cols(act)
                weights_hi(0)
                for c in range(KT):
                    whole(0, c)
                weights_hi(1)
                gelu(0, 0)

            def body(b, par, last):
                for j in range(1, JT):
                    if static(b, 0) and j + 1 < JT:
                        weights_hi(j + 1)
                    gelu(b, j)
                    if 8 <= j < 12 and not last:
                        whole(b + 1, j - 8)
                if not last:
                    gelu(b + 1, 0)
            pairs(act, pro, body)

        @block.vector
        def _(dve):
            def lo(b, j):
                e_gh.wait(dve, b, j)
                e_gl.up(nc.vector.tensor_tensor(gl[:, j % 2, :], gf[:, j % 2, :], f32(gh[:, j % 2, :]), ALU.subtract))

            def weights_lo(i):
                wt.hi.wait(dve, i, 0)
                wt.lo.up(weight_lo(nc, wt, i))

            def stat(n, t):
                x.full[t].wait(dve, n, 0 if static(n, 0) else -1)
                x.e_st.up(ln_stats(nc, x, t))

            def aggregate(n):
                for t in range(TT):
                    x.e_st.wait(dve, n, t, ph.passed)
                    x.e_mv.up(ln_mean(nc, x, t))

            def normalise(n):
                x.e_rs.wait(dve, n, 0)
                for t in range(TT):
                    x.e_xn.up(ln_normalise(nc, x, t))

            def hi(n, c, par):
                x.e_hf.wait(dve, n, c)
                x.e_hh.up(ln_hi(nc, x, c, par))

            def pro():
                cst.wait_cols(dve)
                for t in range(TT):
                    stat(0, t)
                aggregate(0)
                normalise(0)
                weights_lo(0)
                for c in range(KT):
                    hi(0, c, 0)
                weights_lo(1)
                lo(0, 0)

            def body(b, par, last):
                for j in range(1, JT):
                    if static(b, 0) and j + 1 < JT:
                        weights_lo(j + 1)
                    lo(b, j)
                    if not last:
                        if 1 <= j < 5:
                            stat(b + 1, j - 1)
                        if j == 5:
                            aggregate(b + 1)
                        if j == 6:
                            normalise(b + 1)
                        if 8 <= j < 12:
                            hi(b + 1, j - 8, 1 - par)
                if not last:
                    lo(b + 1, 0)
                for t in range(TT):
                    x.e_xb.wait(dve, b, t)
                    e_acc.wait(dve, b, t)
                    x.e_res.up(add_out(nc, x, acc[t], t))
            pairs(dve, pro, body)

        @block.gpsimd
        def _(pool):
            def layer_norm(n, par):
                x.e_mv.wait(pool, n, TT - 1, ph.passed)
                x.e_ve.up(ln_eps(nc, x))
                x.e_power.wait(pool, 0, 0)
                x.e_ve.wait(pool, n, 0)
                x.e_rs.up(ln_rsqrt(nc, x))
                for c in range(KT):
                    x.e_hh.wait(pool, n, c)
                    x.e_hl.up(ln_lo(nc, x, c, par))

            def pro():
                x.e_power.up(ln_power(nc, x))
                layer_norm(0, 0)

            def body(b, par, last):
                if not last:
                    layer_norm(b + 1, 1 - par)
                if static(b, 0):
                    x.bias_in.wait(pool, 0, 0)
                for t in range(TT):
                    x.full[t].wait(pool, b, 1 if last else 2)
                    x.e_xb.up(add_bias(nc, x, t))
            pairs(pool, pro, body)


def self_attention(nc, name, cst, x_in, x_out, ln_w, ln_b, wq, bq, wk, bk, wv, bv, wo, bo_row):
    with ExitStack() as ctx:
        ph = Phase(nc, ctx, name)
        W = {n: (ph.sb(f"{n}h", [P, KT, D], F32R), ph.sb(f"{n}l", [P, KT, D], F32R)) for n in ("wq", "wk", "wv", "wo")}
        stack = {n: ph.sb(f"stack_{n}", [P, 2, 4, S], F32R) for n in "qk"}
        parts = {n: ph.sb(f"parts_{n}", [P, 2, S], F32R) for n in "qk"}
        Vh, Vl = (ph.sb(n, [P, TT, D], F32R) for n in ("Vh", "Vl"))
        Vbh, Vbl = (ph.sb(n, [P, TT, 4, P], F32R) for n in ("Vbh", "Vbl"))
        Pr = ph.sb("Pr", [P, 2, TT, S])
        PTh, PTl = (ph.sb(n, [P, 2, S], F32R) for n in ("PTh", "PTl"))
        nmax, rsum, rinv = (ph.sb(n, [P, 2, TT]) for n in ("nmax", "rsum", "rinv"))
        bqs = ph.sb("bqs", [P, KT])
        oTh, oTl = ph.sb("oTh", [P, G, S], F32R), ph.sb("oTl", [P, G, S], F32R)
        x = token_buffers(ph, ln_w, ln_b, temps=1)
        x_old, x_new = token_tiles(x_in), token_tiles(x_out)
        wt = weight_staging(ph, [flat(Pr[:, i // 2, 2 * (i % 2):2 * (i % 2) + 2, :]) for i in range(4)])
        for n, w, scale in (("wq", wq, SCALE), ("wk", wk, 1.0), ("wv", wv, 1.0), ("wo", wo, 1.0)):
            add_matrix(wt, w, *W[n], scale)
        QK_CHUNKS, V_CHUNKS, CHUNKS = 4, 6, 8
        pj, s_bank, t_bank, o_bank = ph.banks("pj", 2), ph.banks("s", 3), ph.banks("t", 2), ph.banks("o", 1)[0]

        e_zero = ph.events("v_zero", 2)
        e_bqs = ph.events("bqs_set")
        e_v = ph.events("v", TT)
        e_vh, e_vl = ph.events("vh", TT), ph.events("vl", TT)
        e_vb = ph.events("vb", 2 * H)
        e_qk = ph.events("qk", 2 * G)
        e_qkh, e_qkl = ph.events("qkh", 2 * G), ph.events("qkl", 2 * G)
        e_stack = ph.events("stack", 2 * G, 16 * 8)
        e_s = ph.events("s", H * TT)
        e_mx = ph.events("mx", H * TT)
        e_ex = ph.events("ex", H * TT)
        e_ri = ph.events("ri", H * TT)
        e_pn = ph.events("pn", H * TT)
        e_tp = ph.events("tp", H * TT)
        e_ph, e_pl = ph.events("ph", H * TT), ph.events("pl", H * TT)
        e_pv = ph.events("pv", H * TT)
        e_oh, e_ol = ph.events("oh", G), ph.events("ol", G)
        e_out = ph.events("out", TT)

        block = ctx.enter_context(nc.Block())

        @block.sync
        def _(sp):
            def stacks(b, g):
                for i, n in enumerate("qk"):
                    e_qkl.wait(sp, b, 2 * g + i, ph.passed)
                    e_s.wait(sp, b, 4 * (g - 1) * TT - 1, ph.passed)
                    for j in range(4):
                        src = f32(parts[n][32 * j:32 * j + 32, :, :])
                        for half in range(2):
                            rows = src if n == "k" else src[:, half:half + 1, :].broadcast_to([HD, 2, S])
                            sp.dma_start(f32(stack[n][64 * half:64 * half + 64, g % 2, j, :]), rows)\
                              .then_inc(e_stack.sem, 16)

            def pro():
                for t in range(TT):
                    x.full[t].up(sp.dma_start(x.xs[:, t, :], x_old[0, t]))
                load_weights(sp, wt, 0, CHUNKS)
                x.bias_in.up(sp.dma_start(x.bias[:, :], bo_row.partition_broadcast(P)))
                stacks(0, 0)

            def body(b, last):
                if not last:
                    if static(b, 0):
                        x.e_tr.wait(sp, 0, KT - 1)
                    for t in range(TT):
                        x.stored[t].wait(sp, b - 1, 0, ph.passed)
                        x.full[t].up(sp.dma_start(x.xs[:, t, :], x_old[b + 1, t]))
                for g in range(1, G):
                    stacks(b, g)
                x.e_tr.wait(sp, b if last else b + 1, KT - 1, ph.passed)
                for t in range(TT):
                    x.full[t].up(sp.dma_start(x.xs[:, t, :], x_old[b, t]))
                if not last:
                    stacks(b + 1, 0)
                for t in range(TT):
                    x.e_res.wait(sp, b, t, ph.passed)
                    x.stored[t].up(sp.dma_start(x_new[b, t], x.xs[:, t, :]))
            run(sp, pro, body)
            for t in range(TT):
                x.stored[t].wait(sp, B - 1, 0)

        @block.tensor
        def _(pe):
            def T(n, c):
                x.e_xn.wait(pe, n, TT - 1)
                if c < 2:
                    e_qkl.wait(pe, n, c - 2)
                else:
                    x.e_hf.wait(pe, n, c - 2)
                x.e_tr.up(ln_transpose(nc, x, pj[c % 2], c, cst.ident[:, :]))

            def QK(b, g):
                for i, n in enumerate("qk"):
                    if g == 0:
                        x.e_hl.wait(pe, b, KT - 1)
                    elif g == 1:
                        e_vl.wait(pe, b, 2 + i)
                    else:
                        e_qkl.wait(pe, b, 2 * (g - 1) + i)
                    wh, wl = W["w" + n]
                    gs = slice(g * P, (g + 1) * P)
                    for c in range(KT):
                        last = product(nc, pj[i][:, :], wh[:, c, gs], wl[:, c, gs], x.hTh[:, 0, c, :],
                                       x.hTl[:, 0, c, :], c == 0, c == KT - 1)
                    e_qk.up(last)

            def V(b, t):
                if static(b, 0):
                    wt.lo.wait(pe, V_CHUNKS - 1, 0)
                if t < 2:
                    e_qkl.wait(pe, b, t)
                    x.e_res.wait(pe, b, t - 2)
                else:
                    e_vl.wait(pe, b, t - 2)
                ts = slice(t * P, (t + 1) * P)
                wh, wl = W["wv"]
                for c in range(KT):
                    last = product(nc, pj[t % 2][:, :], x.hTh[:, 0, c, ts], x.hTl[:, 0, c, ts], wh[:, c, :],
                                   wl[:, c, :], c == 0, c == KT - 1)
                e_v.up(last)

            def scores(b, h, qts):
                g, j = h // 4, h % 4
                for qt in qts:
                    if qt == 0 and j == 0:
                        e_stack.wait(pe, b, 2 * g + 1)
                    e_ex.wait(pe, b, h * TT + qt - S_BEFORE[qt])
                    e_s.up(nc.tensor.matmul(s_bank[S_BANK[qt]][:, :], stack["q"][:, g % 2, j, qt * P:(qt + 1) * P],
                                            stack["k"][:, g % 2, j, :], start=True, stop=True))

            def P_transposed(b, i):
                h, kt = i // TT, i % TT
                if kt == 0:
                    e_pn.wait(pe, b, i + TT - 1)
                e_pl.wait(pe, b, i - 2)
                for qt in range(TT):
                    last = nc.tensor.transpose(t_bank[kt % 2][:, qt * P:(qt + 1) * P],
                                               Pr[:, h % 2, qt, kt * P:(kt + 1) * P], cst.ident[:, :])
                e_tp.up(last)

            def PV(b, i):
                h, kt = i // TT, i % TT
                g, j = h // 4, h % 4
                if kt == 0:
                    e_vb.wait(pe, b, 2 * h + 1)
                    if j == 0:
                        e_ol.wait(pe, b, g - 1)
                e_pl.wait(pe, b, i)
                e_pv.up(product(nc, o_bank[:, :], Vbh[:, kt, j, :], Vbl[:, kt, j, :], PTh[:, kt % 2, :],
                                PTl[:, kt % 2, :], j == 0 and kt == 0, j == 3 and kt == TT - 1))

            def O(b, last, t):
                if static(b, 0):
                    wt.lo.wait(pe, CHUNKS - 1, 0)
                if t == 0:
                    e_ol.wait(pe, b, G - 1)
                if t >= 2:
                    x.e_res.wait(pe, b, t - 2)
                elif last:
                    e_qkl.wait(pe, b, 6 + t)
                else:
                    e_qkl.wait(pe, b + 1, t)
                ts = slice(t * P, (t + 1) * P)
                wh, wl = W["wo"]
                for g in range(G):
                    m = product(nc, pj[t % 2][:, :], oTh[:, g, ts], oTl[:, g, ts], wh[:, g, :], wl[:, g, :],
                                g == 0, g == G - 1)
                e_out.up(m)

            def pro():
                cst.wait_ident(pe)
                for c in range(KT):
                    T(0, c)
                wt.lo.wait(pe, QK_CHUNKS - 1, 0)
                QK(0, 0)

            def body(b, last):
                scores(b, 0, [0, 1])
                V(b, 0)
                scores(b, 0, [2, 3])
                for t in range(1, TT):
                    V(b, t)
                for i in range(H * TT):
                    h, kt = i // TT, i % TT
                    if h < H - 1:
                        scores(b, h + 1, S_STEP[kt])
                    if h >= H - KT and kt == 0 and not last:
                        T(b + 1, h - (H - KT))
                    P_transposed(b, i)
                    if h % 4 == 0 and kt == 2 and h < H - 4:
                        QK(b, h // 4 + 1)
                    if i >= 2:
                        PV(b, i - 2)
                PV(b, H * TT - 2)
                PV(b, H * TT - 1)
                if not last:
                    QK(b + 1, 0)
                for t in range(TT):
                    O(b, last, t)
            run(pe, pro, body)

        @block.scalar
        def _(act):
            def qk_hi(b, g):
                for i, n in enumerate("qk"):
                    e_qk.wait(act, b, 2 * g + i)
                    e_stack.wait(act, b, 2 * (g - 1) + i)
                    e_qkh.up(add_hi(nc, parts[n][:, 0, :], pj[i][:, :], (bqs if i == 0 else bk)[:, g:g + 1]))

            def v_hi(b, t):
                e_v.wait(act, b, t)
                e_vb.wait(act, b, -1)
                e_vh.up(add_hi(nc, Vh[:, t, :], pj[t % 2][:, :], None))

            def exps(b, h, qts):
                for qt in qts:
                    e_mx.wait(act, b, h * TT + qt)
                    e_tp.wait(act, b, (h - 2) * TT + TT - 1)
                    e_ex.up(nc.scalar.activation(Pr[:, h % 2, qt, :], s_bank[S_BANK[qt]][:, :], ACT.Exp,
                                                 bias=nmax[:, h % 2, qt:qt + 1],
                                                 accum_out=rsum[:, h % 2, qt:qt + 1]))

            def p_hi(b, i):
                e_tp.wait(act, b, i)
                e_pv.wait(act, b, i - 2)
                e_ph.up(add_hi(nc, PTh[:, i % 2, :], t_bank[i % 2][:, :], None))

            def o_hi(b, g):
                e_pv.wait(act, b, (4 * g + 4) * TT - 1)
                e_out.wait(act, b, -1)
                e_oh.up(add_hi(nc, oTh[:, g, :], o_bank[:, :], bv[:, g:g + 1]))

            def whole(n, c):
                x.e_tr.wait(act, n, c)
                x.e_hl.wait(act, n, c - x.temps)
                x.e_hf.up(ln_whole(nc, x, pj[c % 2], c))

            def weights_hi(first, end):
                for i in range(first, end):
                    wt.full[i % wt.ns].wait(act, i // wt.ns, 0)
                    wt.hi.up(weight_hi(nc, wt, i))

            def pro():
                cst.wait_cols(act)
                weights_hi(0, QK_CHUNKS)
                for c in range(KT):
                    whole(0, c)
                e_bqs.wait(act, 0, 0)
                qk_hi(0, 0)
                weights_hi(QK_CHUNKS, CHUNKS)

            def body(b, last):
                exps(b, 0, [0, 1])
                v_hi(b, 0)
                exps(b, 0, [2, 3])
                for t in range(1, TT):
                    v_hi(b, t)
                for i in range(H * TT):
                    h, kt = i // TT, i % TT
                    if h >= H - KT and kt == 0 and not last:
                        whole(b + 1, h - (H - KT))
                    if h % 4 == 0 and kt == 2:
                        if h:
                            o_hi(b, h // 4 - 1)
                        if h < H - 4:
                            qk_hi(b, h // 4 + 1)
                    p_hi(b, i)
                    if h < H - 1:
                        exps(b, h + 1, S_STEP[kt])
                o_hi(b, G - 1)
                if not last:
                    qk_hi(b + 1, 0)
            run(act, pro, body)

        @block.vector
        def _(dve):
            def qk_lo(b, g):
                for i, n in enumerate("qk"):
                    e_qkh.wait(dve, b, 2 * g + i)
                    e_qkl.up(add_lo(nc, parts[n][:, 1, :], parts[n][:, 0, :], pj[i][:, :],
                                    (bqs if i == 0 else bk)[:, g:g + 1]))

            def v_lo(b, t):
                e_vh.wait(dve, b, t)
                e_vl.up(add_lo(nc, Vl[:, t, :], Vh[:, t, :], pj[t % 2][:, :], None))

            def maxima(b, h, qts):
                for qt in qts:
                    e_s.wait(dve, b, h * TT + qt)
                    e_mx.up(nc.vector.reduce_max(nmax[:, h % 2, qt:qt + 1], s_bank[S_BANK[qt]][:, :], AX.X, negate=True))

            def inverses(b, h, qts):
                for qt in qts:
                    e_ex.wait(dve, b, h * TT + qt)
                    e_ri.up(nc.vector.reciprocal(rinv[:, h % 2, qt:qt + 1], rsum[:, h % 2, qt:qt + 1]))

            def p_lo(b, i):
                e_ph.wait(dve, b, i)
                e_pl.up(add_lo(nc, PTl[:, i % 2, :], PTh[:, i % 2, :], t_bank[i % 2][:, :], None))

            def o_lo(b, g):
                e_oh.wait(dve, b, g)
                e_ol.up(add_lo(nc, oTl[:, g, :], oTh[:, g, :], o_bank[:, :], bv[:, g:g + 1]))

            def stat(n, t):
                x.full[t].wait(dve, n, 0 if static(n, 0) else -1)
                x.e_st.up(ln_stats(nc, x, t))

            def aggregate(n):
                for t in range(TT):
                    x.e_st.wait(dve, n, t, ph.passed)
                    x.e_mv.up(ln_mean(nc, x, t))

            def normalise(n, t):
                x.e_rs.wait(dve, n, 0)
                x.e_xn.up(ln_normalise(nc, x, t))

            def hi(n, c):
                x.e_hf.wait(dve, n, c)
                x.e_hh.up(ln_hi(nc, x, c))

            def weights_lo(first, end):
                for i in range(first, end):
                    wt.hi.wait(dve, i, 0)
                    wt.lo.up(weight_lo(nc, wt, i))

            def pro():
                cst.wait_cols(dve)
                e_bqs.up(nc.vector.tensor_scalar(bqs[:, :], bq, SCALE, None, ALU.mult))
                for t in range(TT):
                    stat(0, t)
                aggregate(0)
                for t in range(TT):
                    normalise(0, t)
                weights_lo(0, QK_CHUNKS)
                for c in range(KT):
                    hi(0, c)
                e_bqs.wait(dve, 0, 0)
                qk_lo(0, 0)
                weights_lo(QK_CHUNKS, CHUNKS)

            def body(b, last):
                maxima(b, 0, [0, 1])
                inverses(b, 0, [0, 1])
                v_lo(b, 0)
                maxima(b, 0, [2, 3])
                inverses(b, 0, [2, 3])
                for t in range(1, TT):
                    v_lo(b, t)
                for i in range(H * TT):
                    h, kt = i // TT, i % TT
                    if h % 4 == 0 and kt == 2:
                        if h:
                            o_lo(b, h // 4 - 1)
                        if h < H - 4:
                            qk_lo(b, h // 4 + 1)
                    if h < H - 1:
                        maxima(b, h + 1, S_STEP[kt])
                    p_lo(b, i)
                    if h < H - 1 and kt:
                        inverses(b, h + 1, S_STEP[kt - 1])
                    if not last and kt == 3:
                        if 1 <= h < 5:
                            stat(b + 1, h - 1)
                        if h == 5:
                            aggregate(b + 1)
                        if 6 <= h < 10:
                            normalise(b + 1, h - 6)
                    if not last and kt == 1 and h >= H - KT:
                        hi(b + 1, h - (H - KT))
                o_lo(b, G - 1)
                if not last:
                    qk_lo(b + 1, 0)
                for t in range(TT):
                    x.e_xb.wait(dve, b, t)
                    e_out.wait(dve, b, t)
                    x.e_res.up(add_out(nc, x, pj[t % 2], t))
            run(dve, pro, body)

        @block.gpsimd
        def _(pool):
            def normal(b, h):
                for qt in range(TT):
                    e_ri.wait(pool, b, h * TT + qt, ph.passed)
                    p = Pr[:, h % 2, qt, :]
                    e_pn.up(nc.gpsimd.tensor_scalar(p, p, rinv[:, h % 2, qt:qt + 1], 0.0, ALU.mult, ALU.add))

            def place_v(b, h):
                j = h % 4
                e_pv.wait(pool, b, (h - 4) * TT + TT - 1, ph.passed)
                if h == 0:
                    e_vl.wait(pool, b, TT - 1, ph.passed)
                for dst, src in ((Vbh, Vh), (Vbl, Vl)):
                    e_vb.up(nc.gpsimd.tensor_copy(dst[:, :, j, HD * j:HD * (j + 1)],
                                                  f32(src[:, :, HD * h:HD * (h + 1)])))

            def pro():
                x.e_power.up(ln_power(nc, x))
                x.e_mv.wait(pool, 0, TT - 1)
                x.e_ve.up(ln_eps(nc, x))
                x.e_power.wait(pool, 0, 0)
                x.e_ve.wait(pool, 0, 0)
                x.e_rs.up(ln_rsqrt(nc, x))
                for z in (Vbh, Vbl):
                    e_zero.up(nc.gpsimd.memset(f32(z[:, :, :, :]), 0.0))
                for c in range(KT):
                    x.e_hh.wait(pool, 0, c)
                    x.e_hl.up(ln_lo(nc, x, c))
                x.bias_in.wait(pool, 0, 0)
                e_zero.wait(pool, 0, 1)

            def body(b, last):
                normal(b, 0)
                for h in range(4):
                    place_v(b, h)
                for h in range(H):
                    if h < H - 1:
                        normal(b, h + 1)
                    if 1 <= h and h + 3 < H:
                        place_v(b, h + 3)
                    if h == 5 and not last:
                        x.e_mv.wait(pool, b + 1, TT - 1, ph.passed)
                        x.e_ve.up(ln_eps(nc, x))
                        x.e_ve.wait(pool, b + 1, 0)
                        x.e_rs.up(ln_rsqrt(nc, x))
                    if h >= H - KT and not last:
                        x.e_hh.wait(pool, b + 1, h - (H - KT))
                        x.e_hl.up(ln_lo(nc, x, h - (H - KT)))
                for t in range(TT):
                    x.full[t].wait(pool, b, 1 if last else 2)
                    x.e_xb.up(add_bias(nc, x, t))
            run(pool, pro, body)


def context_kv(nc, name, cst, ctx_in, ln, wk, bk, wv, K, V, later):
    with ExitStack() as ctx:
        ph = Phase(nc, ctx, name)
        N = B * L
        x = ph.sb("x", [L, B, CTX])
        cTh, cTl = ph.sb("cTh", [P, CT, N], F32R), ph.sb("cTl", [P, CT, N], F32R)
        tmp = ph.sb("tmp", [P, 2, GL])
        W = [(ph.sb(f"w{n}h", [P, CT, D], F32R), ph.sb(f"w{n}l", [P, CT, D], F32R)) for n in "kv"]
        wt = weight_staging(ph, [ph.sb(f"stage{i}", [P, CT * D]) for i in range(2)])
        for (wh, wl), w in zip(W, (wk, wv)):
            add_matrix(wt, w, wh, wl, rows=CT)
        stats, mv, ve, rs, power = (ph.sb(n, [L, B, k]) for n, k in
                                    (("stats", 6), ("mv", 2), ("ve", 1), ("rs", 1), ("power", 1)))
        banks = ph.banks("bank", 8)
        e_x = ph.events("x", 1, 16)
        e_st, e_mv, e_ve, e_rs, e_pw = (ph.events(n) for n in ("st", "mv", "ve", "rs", "pw"))
        e_xn = ph.events("xn")
        e_t = ph.events("t")
        e_hf = ph.events("hf")
        e_hh = ph.events("hh")
        e_hl = ph.events("hl")
        e_k, e_kc = ph.events("k"), ph.events("kc")
        e_v, e_vc = ph.events("v"), ph.events("vc")
        tiles = [(half, c) for half in range(2) for c in range(CT)]
        keys = [(g, half) for g in range(G) for half in range(2)]
        NT, NK = len(tiles), len(keys)
        block = ctx.enter_context(nc.Block())

        @block.sync
        def _(sp):
            e_x.up(sp.dma_start(x[:, :, :], ctx_in.rearrange("b l d -> l b d")))
            load_weights(sp, wt, 0, 2)
            load_weights(sp, later, 0, len(later.chunks))

        @block.vector
        def _(dve):
            cst.wait_cols(dve)
            e_x.wait(dve, 0, 0)
            if ln:
                for b in range(B):
                    e_st.up(nc.vector.bn_stats(stats[:, b, :], x[:, b, :]))
                for b in range(B):
                    e_st.wait(dve, b, 0)
                    e_mv.up(nc.vector.bn_aggr(mv[:, b, :], stats[:, b, :]))
                e_rs.wait(dve, 0, 0)
                for b in range(B):
                    e_xn.up(nc.vector.tensor_scalar(x[:, b, :], x[:, b, :], mv[:, b, 0:1], rs[:, b, :],
                                                    ALU.subtract, ALU.mult))
            wt.hi.wait(dve, 0, 0)
            wt.lo.up(weight_lo(nc, wt, 0))
            for u, (half, c) in enumerate(tiles):
                lo, hi = cTl[:, c, half * GL:(half + 1) * GL], cTh[:, c, half * GL:(half + 1) * GL]
                if ln:
                    e_t.wait(dve, u, 0)
                    e_hl.wait(dve, u - 2, 0)
                    e_hf.up(nc.vector.tensor_scalar(tmp[:, u % 2, :], banks[u][:, 0:GL], ln[0][:, c:c + 1],
                                                    ln[1][:, c:c + 1], ALU.mult, ALU.add))
                    e_hh.wait(dve, u, 0)
                    e_hl.up(nc.vector.tensor_tensor(lo, tmp[:, u % 2, :], f32(hi), ALU.subtract))
                else:
                    e_hh.wait(dve, u, 0)
                    e_hl.up(nc.vector.tensor_tensor(lo, banks[u][:, 0:GL], f32(hi), ALU.subtract))
            wt.hi.wait(dve, 1, 0)
            wt.lo.up(weight_lo(nc, wt, 1))
            for u, (g, half) in enumerate(keys):
                e_k.wait(dve, u, 0)
                dst, src = K[:, g, half * GL:(half + 1) * GL], banks[(NT + u) % 8][:, 0:GL]
                if bk is None:
                    e_kc.up(nc.vector.tensor_copy(dst, src))
                else:
                    e_kc.up(nc.vector.tensor_scalar(dst, src, bk[:, g:g + 1], None, ALU.add))
                if u % 2:
                    later.hi.wait(dve, u // 2, 0)
                    later.lo.up(weight_lo(nc, later, u // 2))

        @block.gpsimd
        def _(pool):
            if ln:
                e_pw.up(nc.gpsimd.memset(power[:, :, :], -0.5))
                e_mv.wait(pool, B - 1, 0)
                e_ve.up(nc.gpsimd.tensor_scalar(ve[:, :, 0], mv[:, :, 1], EPS, 1.0, ALU.add, ALU.mult))
                e_ve.wait(pool, 0, 0)
                e_pw.wait(pool, 0, 0)
                e_rs.up(nc.gpsimd.tensor_tensor(rs[:, :, 0], ve[:, :, 0], power[:, :, 0], ALU.pow))

        @block.scalar
        def _(act):
            cst.wait_cols(act)
            wt.full[0].wait(act, 0, 0)
            wt.hi.up(weight_hi(nc, wt, 0))
            for u, (half, c) in enumerate(tiles):
                hi = cTh[:, c, half * GL:(half + 1) * GL]
                if ln:
                    e_hf.wait(act, u, 0)
                    e_hh.up(nc.scalar.activation(hi, tmp[:, u % 2, :], ACT.Copy))
                else:
                    e_t.wait(act, u, 0)
                    e_hh.up(nc.scalar.activation(hi, banks[u][:, 0:GL], ACT.Copy))
            wt.full[1].wait(act, 0, 0)
            wt.hi.up(weight_hi(nc, wt, 1))
            for i in range(len(later.chunks)):
                later.full[i % later.ns].wait(act, i // later.ns, 0)
                later.hi.up(weight_hi(nc, later, i))
            for b in range(B):
                e_v.wait(act, b, 0)
                e_vc.up(nc.scalar.activation(V[:, b, :], banks[(NT + NK + b) % 8][0:L, :], ACT.Copy))

        @block.tensor
        def _(pe):
            cst.wait_ident(pe)
            e_x.wait(pe, 0, 0)
            if ln:
                e_xn.wait(pe, B - 1, 0)
            for u, (half, c) in enumerate(tiles):
                for i in range(4):
                    last = nc.tensor.transpose(banks[u][:, i * L:(i + 1) * L], x[:, half * 4 + i, c * P:(c + 1) * P],
                                               cst.ident[0:L, 0:L])
                e_t.up(last)
            e_hl.wait(pe, NT - 1, 0)
            wt.lo.wait(pe, 1, 0)
            for u, (g, half) in enumerate(keys):
                gs, hs = slice(g * P, (g + 1) * P), slice(half * GL, (half + 1) * GL)
                for c in range(CT):
                    last = product(nc, banks[(NT + u) % 8][:, 0:GL], W[0][0][:, c, gs], W[0][1][:, c, gs],
                                   cTh[:, c, hs], cTl[:, c, hs], c == 0, c == CT - 1)
                e_k.up(last)
            for b in range(B):
                e_kc.wait(pe, b, 0)
                ls = slice(b * L, (b + 1) * L)
                for c in range(CT):
                    last = product(nc, banks[(NT + NK + b) % 8][0:L, :], cTh[:, c, ls], cTl[:, c, ls],
                                   W[1][0][:, c, :], W[1][1][:, c, :], c == 0, c == CT - 1)
                e_v.up(last)


def cross_attention(nc, name, cst, x_in, x_out, ctx_in, ln_w, ln_b, ctx_ln, wq, bq, wk, bk, wv, bv, wo, bo_row):
    with ExitStack() as ctx:
        ph = Phase(nc, ctx, name)
        K, Vall = ph.sb("K", [P, G, B * L]), ph.sb("Vall", [L, B, D])
        W = {n: (ph.sb(f"{n}h", [P, KT, D], F32R), ph.sb(f"{n}l", [P, KT, D], F32R)) for n in ("wq", "wo")}
        wt = weight_staging(ph, [ph.sb(f"stage{i}", [P, 2 * D]) for i in range(2)])
        add_matrix(wt, wq, *W["wq"], SCALE)
        add_matrix(wt, wo, *W["wo"])
        context_kv(nc, name + "_kv", cst, ctx_in, ctx_ln, wk, bk, wv, K, Vall, wt)

        Kbh, Kbl = (ph.sb(n, [P, G, 4, L], F32R) for n in ("Kbh", "Kbl"))
        Vbh, Vbl = (ph.sb(n, [P, G, 4, P], F32R) for n in ("Vbh", "Vbl"))
        qTh, qTl = ph.sb("qTh", [P, G, S], F32R), ph.sb("qTl", [P, G, S], F32R)
        Pr = ph.sb("Pr", [P, G, TT, GL])
        PTh, PTl = (ph.sb(n, [L, 2, S], F32R) for n in ("PTh", "PTl"))
        nmax, rsum, rinv = (ph.sb(n, [P, G, TT, 4]) for n in ("nmax", "rsum", "rinv"))
        bqs = ph.sb("bqs", [P, KT])
        oTh, oTl = ph.sb("oTh", [P, G, S], F32R), ph.sb("oTl", [P, G, S], F32R)
        x = token_buffers(ph, ln_w, ln_b)
        x_old, x_new = token_tiles(x_in), token_tiles(x_out)
        pj, s_bank, t_bank, o_bank = ph.banks("pj", 2), ph.banks("s", 3), ph.banks("t", 2), ph.banks("o", 1)[0]

        e_zero = ph.events("zero", 4)
        e_bqs = ph.events("bqs_set")
        e_kb = ph.events("kb", 8)
        e_vb = ph.events("vb", 8)
        e_q = ph.events("q", G)
        e_qh, e_ql = ph.events("qh", G), ph.events("ql", G)
        e_s = ph.events("s", G * TT)
        e_mx = ph.events("mx", G * TT)
        e_sub = ph.events("sub", G * TT)
        e_ex = ph.events("ex", G * TT)
        e_sum = ph.events("sum", G * TT)
        e_ri = ph.events("ri", G * TT)
        e_pn = ph.events("pn", G * TT)
        e_tp = ph.events("tp", H)
        e_ph, e_pl = ph.events("ph", H), ph.events("pl", H)
        e_pv = ph.events("pv", H)
        e_oh, e_ol = ph.events("oh", G), ph.events("ol", G)
        e_out = ph.events("out", TT)

        EARLY = 8
        TAIL = [("Q", 0), ("Q", 1), ("S", 0), ("Q", 2), ("S", 1), ("Q", 3), ("S", 2), ("O", 0), ("S", 3), ("S", 4),
                ("O", 1), ("S", 5), ("O", 2), ("S", 6), ("O", 3), ("S", 7)]
        FIRST_TAIL = [step for step in TAIL if step[0] != "O"]
        LAST_TAIL = [step for step in TAIL if step[0] == "O"]

        block = ctx.enter_context(nc.Block())

        @block.sync
        def _(sp):
            def pro():
                for t in range(TT):
                    x.full[t].up(sp.dma_start(x.xs[:, t, :], x_old[0, t]))
                x.bias_in.up(sp.dma_start(x.bias[:, :], bo_row.partition_broadcast(P)))

            def body(b, last):
                if not last:
                    if static(b, 0):
                        x.e_tr.wait(sp, 0, KT - 1)
                    for t in range(TT):
                        x.stored[t].wait(sp, b - 1, 0, ph.passed)
                        x.full[t].up(sp.dma_start(x.xs[:, t, :], x_old[b + 1, t]))
                x.e_tr.wait(sp, b if last else b + 1, KT - 1, ph.passed)
                for t in range(TT):
                    x.full[t].up(sp.dma_start(x.xs[:, t, :], x_old[b, t]))
                for t in range(TT):
                    x.e_res.wait(sp, b, t, ph.passed)
                    x.stored[t].up(sp.dma_start(x_new[b, t], x.xs[:, t, :]))
            run(sp, pro, body)
            for t in range(TT):
                x.stored[t].wait(sp, B - 1, 0)

        @block.tensor
        def _(pe):
            def T(n, c):
                x.e_xn.wait(pe, n, TT - 1)
                if c < 2:
                    e_ql.wait(pe, n - 1, 2 + c)
                    x.e_res.wait(pe, n - 1, c - 2)
                else:
                    x.e_hf.wait(pe, n, c - 2)
                x.e_tr.up(ln_transpose(nc, x, pj[c % 2], c, cst.ident[:, :]))

            def Q(n, g):
                if g < 2:
                    x.e_hl.wait(pe, n, KT - 1)
                else:
                    e_ql.wait(pe, n, g - 2)
                wh, wl = W["wq"]
                gs = slice(g * P, (g + 1) * P)
                for c in range(KT):
                    last = product(nc, pj[g % 2][:, :], wh[:, c, gs], wl[:, c, gs], x.hTh[:, 0, c, :],
                                   x.hTl[:, 0, c, :], c == 0, c == KT - 1)
                e_q.up(last)

            def scores(b, s):
                g, qt = s // TT, s % TT
                e_ql.wait(pe, b, g)
                if s == 0:
                    e_kb.wait(pe, b, 7)
                e_sub.wait(pe, b, s - S_BEFORE[qt])
                qs = slice(qt * P, (qt + 1) * P)
                kh, kl = (k[:, g, :, :].rearrange("p j l -> p (j l)") for k in (Kbh, Kbl))
                e_s.up(product(nc, s_bank[S_BANK[qt]][:, 0:GL], qTh[:, g, qs], qTl[:, g, qs], kh, kl, True, True))

            def P_transposed(b, h):
                g, j = h // 4, h % 4
                if j == 0:
                    e_pn.wait(pe, b, g * TT + TT - 1)
                e_pl.wait(pe, b, h - 2)
                for qt in range(TT):
                    last = nc.tensor.transpose(t_bank[j % 2][0:L, qt * P:(qt + 1) * P],
                                               Pr[:, g, qt, j * L:(j + 1) * L], cst.ident[:, :])
                e_tp.up(last)

            def PV(b, h):
                g, j = h // 4, h % 4
                if j == 0:
                    e_ol.wait(pe, b, g - 1)
                    e_vb.wait(pe, b, 2 * g + 1)
                e_pl.wait(pe, b, h)
                e_pv.up(product(nc, o_bank[:, :], Vbh[0:L, g, j, :], Vbl[0:L, g, j, :], PTh[:, j % 2, :],
                                PTl[:, j % 2, :], j == 0, j == 3))

            def O(b, last, t):
                if t == 0:
                    e_ol.wait(pe, b, G - 1)
                if t < 2 and not last:
                    e_ql.wait(pe, b + 1, 2 + t)
                else:
                    x.e_res.wait(pe, b, t - 2)
                ts = slice(t * P, (t + 1) * P)
                wh, wl = W["wo"]
                for g in range(G):
                    m = product(nc, pj[t % 2][:, :], oTh[:, g, ts], oTl[:, g, ts], wh[:, g, :], wl[:, g, :],
                                g == 0, g == G - 1)
                e_out.up(m)

            def pro():
                for c in range(KT):
                    T(0, c)
                for step, k in FIRST_TAIL:
                    Q(0, k) if step == "Q" else scores(0, k)

            def body(b, last):
                for h in range(H):
                    if h + EARLY < G * TT:
                        scores(b, h + EARLY)
                    if h // 4 == 2 and not last:
                        T(b + 1, h % 4)
                    P_transposed(b, h)
                    if h:
                        PV(b, h - 1)
                PV(b, H - 1)
                for step, k in LAST_TAIL if last else TAIL:
                    if step == "Q":
                        Q(b + 1, k)
                    elif step == "S":
                        scores(b + 1, k)
                    else:
                        O(b, last, k)
            run(pe, pro, body)

        @block.scalar
        def _(act):
            def q_hi(n, g):
                e_q.wait(act, n, g)
                e_qh.up(add_hi(nc, qTh[:, g, :], pj[g % 2][:, :], None if bq is None else bqs[:, g:g + 1]))

            def exp(b, s):
                e_sub.wait(act, b, s)
                p = Pr[:, s // TT, s % TT, :]
                e_ex.up(nc.scalar.activation(p, p, ACT.Exp))

            def p_hi(b, h):
                e_tp.wait(act, b, h)
                e_pv.wait(act, b, h - 2)
                e_ph.up(add_hi(nc, PTh[:, h % 2, :], t_bank[h % 2][0:L, :], None))

            def o_hi(b, g):
                e_pv.wait(act, b, 4 * g + 3)
                e_out.wait(act, b, -1)
                e_oh.up(add_hi(nc, oTh[:, g, :], o_bank[:, :], None if bv is None else bv[:, g:g + 1]))

            def whole(n, c):
                x.e_tr.wait(act, n, c)
                x.e_hl.wait(act, n, c - x.temps)
                x.e_hf.up(ln_whole(nc, x, pj[c % 2], c))

            def pro():
                for c in range(KT):
                    whole(0, c)
                if bq is not None:
                    e_bqs.wait(act, 0, 0)
                for step, k in FIRST_TAIL:
                    q_hi(0, k) if step == "Q" else exp(0, k)

            def body(b, last):
                for h in range(H):
                    if h // 4 == 2 and not last:
                        whole(b + 1, h % 4)
                    p_hi(b, h)
                    if h % 4 == 0 and h:
                        o_hi(b, h // 4 - 1)
                    if h + EARLY < G * TT:
                        exp(b, h + EARLY)
                o_hi(b, G - 1)
                if not last:
                    for step, k in FIRST_TAIL:
                        q_hi(b + 1, k) if step == "Q" else exp(b + 1, k)
            run(act, pro, body)

        @block.vector
        def _(dve):
            def q_lo(n, g):
                e_qh.wait(dve, n, g)
                e_ql.up(add_lo(nc, qTl[:, g, :], qTh[:, g, :], pj[g % 2][:, :], None if bq is None else bqs[:, g:g + 1]))

            def centre(b, s):
                g, qt = s // TT, s % TT
                bank = s_bank[S_BANK[qt]][:, 0:GL].rearrange("p (j l) -> p j l", j=4)
                m = nmax[:, g, qt, :]
                e_s.wait(dve, b, s)
                e_mx.up(nc.vector.reduce_max(m, bank, AX.X, negate=True))
                e_mx.wait(dve, b, s)
                e_tp.wait(dve, b - 1, 4 * g + 3)
                e_sub.up(nc.vector.tensor_tensor(Pr[:, g, qt, :].rearrange("p (j l) -> p j l", j=4), bank,
                                                 m.unsqueeze(2).broadcast_to([P, 4, L]), ALU.add))

            def inverse(b, s):
                g, qt = s // TT, s % TT
                e_ex.wait(dve, b, s)
                e_sum.up(nc.vector.reduce_sum(rsum[:, g, qt, :], Pr[:, g, qt, :].rearrange("p (j l) -> p j l", j=4),
                                              AX.X))
                e_sum.wait(dve, b, s)
                e_ri.up(nc.vector.reciprocal(rinv[:, g, qt, :], rsum[:, g, qt, :]))

            def softmax(b, s):
                centre(b, s)
                if s % EARLY:
                    inverse(b, s - 1)

            def p_lo(b, h):
                e_ph.wait(dve, b, h)
                e_pl.up(add_lo(nc, PTl[:, h % 2, :], PTh[:, h % 2, :], t_bank[h % 2][0:L, :], None))

            def o_lo(b, g):
                e_oh.wait(dve, b, g)
                e_ol.up(add_lo(nc, oTl[:, g, :], oTh[:, g, :], o_bank[:, :], None if bv is None else bv[:, g:g + 1]))

            def stat(n, t):
                x.full[t].wait(dve, n, 0 if static(n, 0) else -1)
                x.e_st.up(ln_stats(nc, x, t))

            def aggregate(n):
                for t in range(TT):
                    x.e_st.wait(dve, n, t, ph.passed)
                    x.e_mv.up(ln_mean(nc, x, t))

            def normalise(n, t):
                x.e_rs.wait(dve, n, 0)
                x.e_xn.up(ln_normalise(nc, x, t))

            def hi(n, c):
                x.e_hf.wait(dve, n, c)
                x.e_hh.up(ln_hi(nc, x, c))

            def pro():
                if bq is not None:
                    e_bqs.up(nc.vector.tensor_scalar(bqs[:, :], bq, SCALE, None, ALU.mult))
                    e_bqs.wait(dve, 0, 0)
                for t in range(TT):
                    stat(0, t)
                aggregate(0)
                for t in range(TT):
                    normalise(0, t)
                for c in range(KT):
                    hi(0, c)
                for step, k in FIRST_TAIL:
                    q_lo(0, k) if step == "Q" else softmax(0, k)
                inverse(0, EARLY - 1)

            def body(b, last):
                for h in range(H):
                    if h + EARLY < G * TT:
                        softmax(b, h + EARLY)
                    if h + EARLY == G * TT:
                        inverse(b, G * TT - 1)
                    p_lo(b, h)
                    if h % 4 == 0 and h:
                        o_lo(b, h // 4 - 1)
                    if not last:
                        if h < 4:
                            stat(b + 1, h)
                        if h == 4:
                            aggregate(b + 1)
                        if h in (5, 6):
                            for t in range(2 * (h - 5), 2 * (h - 5) + 2):
                                normalise(b + 1, t)
                        if h // 4 == 2:
                            hi(b + 1, h % 4)
                o_lo(b, G - 1)
                for step, k in LAST_TAIL if last else TAIL:
                    if step == "Q":
                        q_lo(b + 1, k)
                    elif step == "S":
                        softmax(b + 1, k)
                    else:
                        x.e_xb.wait(dve, b, k)
                        e_out.wait(dve, b, k)
                        x.e_res.up(add_out(nc, x, pj[k % 2], k))
                if not last:
                    inverse(b + 1, EARLY - 1)
            run(dve, pro, body)

        @block.gpsimd
        def _(pool):
            def place_k(n, j):
                rows = slice(HD * j, HD * (j + 1))
                src = K[rows, :, bass.ds(n * L, L)]
                e_s.wait(pool, n, -1, ph.passed)
                e_kb.up(nc.gpsimd.tensor_copy(Kbh[rows, :, j, :], src))
                e_kb.wait(pool, n, 2 * j, ph.passed)
                e_kb.up(nc.gpsimd.tensor_tensor(Kbl[rows, :, j, :], src, f32(Kbh[rows, :, j, :]), ALU.subtract))
                e_kb.wait(pool, n, 2 * j + 1, ph.passed)

            def place_v(n, g):
                src = Vall[:, n, P * g:P * (g + 1)].rearrange("p (j d) -> p j d", j=4)
                e_pv.wait(pool, n - 1, 4 * g + 3, ph.passed)
                e_vb.up(nc.gpsimd.tensor_copy(diagonal(Vbh[0:L, g, :, :]), src))
                e_vb.wait(pool, n, 2 * g, ph.passed)
                e_vb.up(nc.gpsimd.tensor_tensor(diagonal(Vbl[0:L, g, :, :]), src, f32(diagonal(Vbh[0:L, g, :, :])),
                                                ALU.subtract))
                e_vb.wait(pool, n, 2 * g + 1, ph.passed)

            def normal(b, s):
                e_ri.wait(pool, b, s, ph.passed)
                p = Pr[:, s // TT, s % TT, :].rearrange("p (j l) -> p j l", j=4)
                e_pn.up(nc.gpsimd.tensor_tensor(p, p, rinv[:, s // TT, s % TT, :].unsqueeze(2).broadcast_to([P, 4, L]),
                                                ALU.mult))

            def rsqrt(n):
                x.e_mv.wait(pool, n, TT - 1, ph.passed)
                x.e_ve.up(ln_eps(nc, x))
                x.e_ve.wait(pool, n, 0)
                x.e_rs.up(ln_rsqrt(nc, x))

            def lo(n, c):
                x.e_hh.wait(pool, n, c)
                x.e_hl.up(ln_lo(nc, x, c))

            def pro():
                x.e_power.up(ln_power(nc, x))
                for z in (Kbh, Kbl, Vbh, Vbl):
                    e_zero.up(nc.gpsimd.memset(f32(z[:, :, :, :]), 0.0))
                x.e_power.wait(pool, 0, 0)
                rsqrt(0)
                e_zero.wait(pool, 0, 3)
                x.e_rs.wait(pool, 0, 0)
                for j in range(4):
                    place_k(0, j)
                for g in range(G):
                    place_v(0, g)
                for c in range(KT):
                    lo(0, c)
                for s in range(EARLY):
                    normal(0, s)
                x.bias_in.wait(pool, 0, 0)

            def body(b, last):
                for h in range(H):
                    if h + EARLY < G * TT:
                        normal(b, h + EARLY)
                    if not last:
                        if h == 4:
                            rsqrt(b + 1)
                        if h == 5:
                            e_pn.wait(pool, b, h + EARLY)
                            place_v(b + 1, 0)
                        if h // 4 == 2:
                            if h % 4:
                                x.e_hl.wait(pool, b + 1, h % 4 - 1)
                            else:
                                e_pn.wait(pool, b, G * TT - 1)
                            place_k(b + 1, h % 4)
                            lo(b + 1, h % 4)
                        if h == 12:
                            x.e_hl.wait(pool, b + 1, KT - 1)
                            place_v(b + 1, 1)
                        if h == 13:
                            place_v(b + 1, 2)
                if not last:
                    place_v(b + 1, 3)
                for t in range(TT):
                    x.full[t].wait(pool, b, 1 if last else 2)
                    x.e_xb.up(add_bias(nc, x, t))
                if not last:
                    for s in range(EARLY):
                        normal(b + 1, s)
            run(pool, pro, body)


class Constants:

    def __init__(self, nc, ctx, cols):
        self.nc = nc
        self.ident = ctx.enter_context(nc.sbuf_tensor("ident", [P, P], F32))
        self.cols = ctx.enter_context(nc.sbuf_tensor("cols", [P, NCOL], F32))
        self.s_ident, self.s_cols = (ctx.enter_context(nc.semaphore(n)) for n in ("s_ident", "s_cols"))
        with nc.Block() as block:
            @block.gpsimd
            def _(pool):
                nc.gpsimd.memset(self.ident[:, :], 0.0).then_inc(self.s_ident, 1)
                pool.wait_ge(self.s_ident, 1)
                nc.gpsimd.affine_select(out=self.ident[:, :], in_=self.ident[:, :], compare_op=ALU.not_equal, fill=1.0,
                                        base=0, pattern=[[-1, P]], channel_multiplier=1).then_inc(self.s_ident, 1)

            @block.sync
            def _(sp):
                sp.dma_start(self.cols[:, :], cols).then_inc(self.s_cols, 16)

    def wait_ident(self, eng):
        eng.wait_ge(self.s_ident, 2)

    def wait_cols(self, eng):
        eng.wait_ge(self.s_cols, 16)

    def col(self, name):
        at, n = COL_AT[name]
        return self.cols[:, at:at + n]


def program(nc, a, out):
    with ExitStack() as ctx:
        cst = Constants(nc, ctx, a["cols"])
        c = cst.col
        x = [a["x"]] + [nc.dram_tensor(f"x_{i}", (B * S, D), F32).ap() for i in range(1, 5)] + [out]
        cross_attention(nc, "L0ca", cst, x[0], x[1], a["ctx"], c("L0_ln1_w"), c("L0_ln1_b"),
                        (c("L0_ln2_w"), c("L0_ln2_b")), a["L0_wq"], None, a["L0_wkv"][:, 0:D], None,
                        a["L0_wkv"][:, D:2 * D], None, a["L0_wo"], a["L0_bo"])
        feed_forward(nc, "L0ff", cst, x[1], x[2], c("L0_ln3_w"), c("L0_ln3_b"), a["L0_w1"], c("L0_b1"),
                     a["L0_w2"], a["L0_b2"])
        self_attention(nc, "L1sa", cst, x[2], x[3], c("L1_ln1_g"), c("L1_ln1_b"), a["L1_sa_wq"], c("L1_sa_bq"),
                       a["L1_sa_wk"], c("L1_sa_bk"), a["L1_sa_wv"], c("L1_sa_bv"), a["L1_sa_wo"], a["L1_sa_bo"])
        cross_attention(nc, "L1ca", cst, x[3], x[4], a["ctx"], c("L1_ln2_g"), c("L1_ln2_b"), None, a["L1_ca_wq"],
                        c("L1_ca_bq"), a["L1_ca_wk"], c("L1_ca_bk"), a["L1_ca_wv"], c("L1_ca_bv"), a["L1_ca_wo"],
                        a["L1_ca_bo"])
        feed_forward(nc, "L1ff", cst, x[4], x[5], c("L1_ln3_g"), c("L1_ln3_b"), a["L1_w1"], c("L1_mlp_b1"),
                     a["L1_w2"], a["L1_b2"])


def kernel(**inputs):
    import concourse.bacc as bacc
    from concourse.bass_utils import run_bass_kernel_spmd

    v = {k.replace("_xattn", ""): np.asarray(w) for k, w in inputs.items()}
    arrays = {
        "x": v["x"].reshape(B * S, D), "ctx": v["ctx_768"],
        "cols": np.concatenate([v[n].reshape(-1, P).T for n, _ in COLS], axis=1),
        "L0_wq": v["L0_Wq"], "L0_wkv": v["L0_Wkv"], "L0_wo": v["L0_Wproj"], "L0_w1": v["L0_W1"], "L0_w2": v["L0_W2"],
        "L0_bo": v["L0_bproj"], "L0_b2": v["L0_b2"], "L1_sa_bo": v["L1_sa_bo"], "L1_ca_bo": v["L1_ca_bo"],
        "L1_b2": v["L1_mlp_b2"],
        "L1_w1": v["L1_mlp_w1"].T, "L1_w2": v["L1_mlp_w2"].T,
    }
    for n in ("sa_wq", "sa_wk", "sa_wv", "sa_wo", "ca_wq", "ca_wk", "ca_wv", "ca_wo"):
        arrays[f"L1_{n}"] = v[f"L1_{n}"].T
    arrays = {k: np.ascontiguousarray(w) for k, w in arrays.items()}

    nc = bacc.Bacc("TRN2", target_bir_lowering=False, num_devices=1)
    aps = {k: nc.dram_tensor(f"in_{k}", w.shape, mybir.dt.from_np(w.dtype), kind="ExternalInput").ap()
           for k, w in arrays.items()}
    out = nc.dram_tensor("out", (B * S, D), F32, kind="ExternalOutput").ap()
    program(nc, aps, out)
    r = run_bass_kernel_spmd(nc, [{f"in_{k}": w for k, w in arrays.items()}], core_ids=[0])
    return r.results[0]["out"].reshape(B, S, D)
```

```python
from contextlib import ExitStack

import numpy as np

import concourse.bass as bass
from concourse import mybir

F32 = mybir.dt.float32
F32R = mybir.dt.float32r
ACT = mybir.ActivationFunctionType
ALU = mybir.AluOpType
AX = mybir.AxisListType

P = 128
B, S, D = 8, 512, 512
L, CTX = 77, 384
H, HD = 16, 32
HID = 4 * D
KT = D // P
CT = CTX // P
TT = S // P
G = H // 4
JT = HID // P
GL = 4 * L
SCALE = HD ** -0.5
EPS = 1e-5

S_BANK = [0, 1, 2, 0]
S_BEFORE = {0: 1, 1: TT, 2: TT, 3: 3}

COLS = [("L0_ln1_w", D), ("L0_ln1_b", D), ("L0_ln2_w", CTX), ("L0_ln2_b", CTX), ("L0_ln3_w", D), ("L0_ln3_b", D),
        ("L0_b1", HID), ("L1_ln1_g", D), ("L1_ln1_b", D), ("L1_ln2_g", D), ("L1_ln2_b", D), ("L1_ln3_g", D),
        ("L1_ln3_b", D), ("L1_sa_bq", D), ("L1_sa_bk", D), ("L1_sa_bv", D), ("L1_ca_bq", D), ("L1_ca_bk", D),
        ("L1_ca_bv", D), ("L1_mlp_b1", HID)]
COL_AT, NCOL = {}, 0
for _name, _n in COLS:
    COL_AT[_name] = (NCOL, _n // P)
    NCOL += _n // P


class Events:

    def __init__(self, sem, per, unit=1):
        self.sem, self.per, self.unit = sem, per, unit

    def wait(self, eng, b, k, alone=None):
        v = b * (self.per * self.unit) + (k + 1) * self.unit
        if isinstance(v, int):
            if v > 0:
                eng.wait_ge(self.sem, v)
            return
        eng.wait_ge(self.sem, v)
        if alone is not None:
            eng.sem_inc(alone, 1)

    def up(self, instruction):
        instruction.then_inc(self.sem, self.unit)


class Names:
    pass


class Phase:

    def __init__(self, nc, ctx, name):
        self.nc, self.ctx, self.name, self.sems = nc, ctx, name, []
        self.passed = self.events("passed").sem
        ctx.callback(self.end)

    def end(self):
        self.nc.clear_and_free_semaphores(self.sems)
        self.nc.all_engine_barrier()

    def sb(self, name, shape, dt=F32):
        return self.ctx.enter_context(self.nc.sbuf_tensor(f"{self.name}_{name}", shape, dt))

    def banks(self, name, n):
        return [self.ctx.enter_context(self.nc.psum_tensor(f"{self.name}_{name}{i}", [P, 512], F32)) for i in range(n)]

    def events(self, name, per=1, unit=1):
        self.sems.append(self.nc.alloc_semaphore(f"{self.name}_{name}"))
        return Events(self.sems[-1], per, unit)


def run(eng, pro, body):
    pro()
    body(0, False)
    with eng.Fori(1, B - 1) as b:
        body(b, False)
    body(B - 1, True)


def static(b, value):
    return isinstance(b, int) and b == value


def f32(ap):
    return ap.bitcast(F32)


def flat(ap):
    return ap.rearrange("p a n -> p (a n)")



def product(nc, out, wh, wl, xh, xl, first, last):
    nc.tensor.matmul(out, wh, xh, start=first, stop=False)
    nc.tensor.matmul(out, wl, xh, start=False, stop=False)
    return nc.tensor.matmul(out, wh, xl, start=False, stop=last)


def add_hi(nc, hi, bank, bias):
    if bias is None:
        return nc.scalar.activation(hi, bank, ACT.Copy)
    return nc.scalar.activation(hi, bank, ACT.Identity, bias=bias)


def add_lo(nc, lo, hi, bank, bias):
    if bias is None:
        return nc.vector.tensor_tensor(lo, bank, f32(hi), ALU.subtract)
    return nc.vector.scalar_tensor_tensor(lo, bank, bias, f32(hi), ALU.add, ALU.subtract)


def diagonal(ap):
    return bass.AP(ap.tensor, ap.offset, [list(ap.ap[0]), [P + HD, 4], [1, HD]])


def weight_staging(ph, slots, parts=1):
    wt = Names()
    wt.slots = slots
    wt.ns = len(slots)
    wt.chunks = []
    wt.full = [ph.events(f"w_full{i}", 1, 16 * parts) for i in range(len(slots))]
    wt.hi = ph.events("w_hi")
    wt.lo = ph.events("w_lo")
    return wt


def add_matrix(wt, w, hi, lo, scale=1.0, rows=2):
    v = w.rearrange("(c p) n -> p c n", p=P)
    for c in range(0, v.shape[1], rows):
        wt.chunks.append(([v[:, c:c + rows, :]], flat(hi[:, c:c + rows, :]), flat(lo[:, c:c + rows, :]), scale))


def load_weights(sp, wt, first, end):
    for i in range(first, end):
        wt.lo.wait(sp, i - wt.ns, 0)
        at = 0
        for source in wt.chunks[i][0]:
            n = int(np.prod(source.shape[1:]))
            slot = wt.slots[i % wt.ns][:, at:at + n]
            if len(source.shape) == 3:
                slot = slot.rearrange("p (a n) -> p a n", a=source.shape[1])
            sp.dma_start(slot, source).then_inc(wt.full[i % wt.ns].sem, 16)
            at += n


def weight_hi(nc, wt, i):
    _, hi, _, scale = wt.chunks[i]
    return nc.scalar.activation(hi, wt.slots[i % wt.ns][:, 0:hi.shape[1]], ACT.Copy, scale=scale)


def weight_lo(nc, wt, i):
    _, hi, lo, scale = wt.chunks[i]
    return nc.vector.scalar_tensor_tensor(lo, wt.slots[i % wt.ns][:, 0:hi.shape[1]], scale, f32(hi),
                                          ALU.mult, ALU.subtract)


def token_buffers(ph, w, b, pars=1, temps=2):
    x = Names()
    x.w = w
    x.b = b
    x.temps = temps
    x.xs = ph.sb("xs", [P, TT, D])
    x.bias = ph.sb("bias", [P, D])
    x.htmp = ph.sb("htmp", [P, temps, S])
    x.hTh = ph.sb("hTh", [P, pars, KT, S], F32R)
    x.hTl = ph.sb("hTl", [P, pars, KT, S], F32R)
    x.stats = ph.sb("stats", [P, TT, 6])
    x.mv = ph.sb("mv", [P, TT, 2])
    x.ve = ph.sb("ve", [P, TT])
    x.rs = ph.sb("rs", [P, TT])
    x.power = ph.sb("power", [P, TT])
    x.full = [ph.events(f"xs_full{t}", 2, 16) for t in range(TT)]
    x.stored = [ph.events(f"stored{t}", 1, 16) for t in range(TT)]
    x.bias_in = ph.events("bias_in", 1, 16)
    x.e_power = ph.events("power_set")
    x.e_st = ph.events("ln_st", TT)
    x.e_mv = ph.events("ln_mv", TT)
    x.e_ve = ph.events("ln_ve")
    x.e_rs = ph.events("ln_rs")
    x.e_xn = ph.events("ln_xn", TT)
    x.e_tr = ph.events("ln_tr", KT)
    x.e_hf = ph.events("ln_hf", KT)
    x.e_hh = ph.events("ln_hh", KT)
    x.e_hl = ph.events("ln_hl", KT)
    x.e_xb = ph.events("xb", TT)
    x.e_res = ph.events("res", TT)
    return x


def token_tiles(x):
    return x.rearrange("(b t p) d -> b t p d", b=B, p=P)



def ln_stats(nc, x, t):
    return nc.vector.bn_stats(x.stats[:, t, :], x.xs[:, t, :])


def ln_mean(nc, x, t):
    return nc.vector.bn_aggr(x.mv[:, t, :], x.stats[:, t, :])


def ln_power(nc, x):
    return nc.gpsimd.memset(x.power[:, :], -0.5)


def ln_eps(nc, x):
    return nc.gpsimd.tensor_scalar(x.ve[:, :], x.mv[:, :, 1], EPS, 1.0, ALU.add, ALU.mult)


def ln_rsqrt(nc, x):
    return nc.gpsimd.tensor_tensor(x.rs[:, :], x.ve[:, :], x.power[:, :], ALU.pow)


def ln_normalise(nc, x, t):
    return nc.vector.tensor_scalar(x.xs[:, t, :], x.xs[:, t, :], x.mv[:, t, 0:1], x.rs[:, t:t + 1],
                                   ALU.subtract, ALU.mult)


def ln_transpose(nc, x, bank, c, ident):
    for t in range(TT):
        last = nc.tensor.transpose(bank[:, t * P:(t + 1) * P], x.xs[:, t, c * P:(c + 1) * P], ident)
    return last


def ln_whole(nc, x, bank, c):
    return nc.scalar.activation(x.htmp[:, c % x.temps, :], bank[:, :], ACT.Identity, bias=x.b[:, c:c + 1],
                                scale=x.w[:, c:c + 1])


def ln_hi(nc, x, c, par=0):
    return nc.vector.tensor_copy(x.hTh[:, par, c, :], x.htmp[:, c % x.temps, :])


def ln_lo(nc, x, c, par=0):
    return nc.gpsimd.tensor_tensor(x.hTl[:, par, c, :], x.htmp[:, c % x.temps, :], f32(x.hTh[:, par, c, :]),
                                   ALU.subtract)


def add_bias(nc, x, t):
    return nc.gpsimd.tensor_tensor(x.xs[:, t, :], x.xs[:, t, :], x.bias[:, :], ALU.add)


def add_out(nc, x, bank, t):
    return nc.vector.tensor_tensor(x.xs[:, t, :], bank[:, :], x.xs[:, t, :], ALU.add)


def feed_forward(nc, name, cst, x_in, x_out, ln_w, ln_b, w1, b1, w2, b2_row):
    with ExitStack() as ctx:
        ph = Phase(nc, ctx, name)
        Wh, Wl = ph.sb("Wh", [P, JT, 2 * S], F32R), ph.sb("Wl", [P, JT, 2 * S], F32R)
        gf = ph.sb("gf", [P, 2, S])
        gh, gl = ph.sb("gh", [P, 2, S], F32R), ph.sb("gl", [P, 2, S], F32R)
        x = token_buffers(ph, ln_w, ln_b, pars=2)
        x_old, x_new = token_tiles(x_in), token_tiles(x_out)
        wt = weight_staging(ph, [ph.sb(f"stage{i}", [P, 2 * S]) for i in range(2)], parts=2)
        w1v = w1.rearrange("(c p) n -> p c n", p=P)
        w2v = w2.rearrange("(j p) n -> p j n", p=P)
        for j in range(JT):
            wt.chunks.append(([w1v[:, :, j * P:(j + 1) * P], w2v[:, j, :]], Wh[:, j, :], Wl[:, j, :], 1.0))
        T_bank, f1_bank, acc = ph.banks("T", 2), ph.banks("f1", 2), ph.banks("acc", 4)
        e_f1 = ph.events("f1", JT)
        e_g = ph.events("g", JT)
        e_gh = ph.events("gh", JT)
        e_gl = ph.events("gl", JT)
        e_f2 = ph.events("f2", JT - 1)
        e_acc = ph.events("acc", TT)
        FIRST = 4

        def pairs(eng, pro, body):
            pro()
            for par in range(2):
                body(par, par, False)
            with eng.Fori(1, B // 2 - 1) as i:
                for par in range(2):
                    body(i * 2 + par, par, False)
            for par in range(2):
                body(B - 2 + par, par, par == 1)

        block = ctx.enter_context(nc.Block())

        @block.sync
        def _(sp):
            def pro():
                for t in range(TT):
                    x.full[t].up(sp.dma_start(x.xs[:, t, :], x_old[0, t]))
                load_weights(sp, wt, 0, FIRST)
                x.bias_in.up(sp.dma_start(x.bias[:, :], b2_row.partition_broadcast(P)))

            def body(b, par, last):
                if not last:
                    if static(b, 0):
                        x.e_tr.wait(sp, 0, KT - 1)
                    for t in range(TT):
                        x.stored[t].wait(sp, b - 1, 0, ph.passed)
                        x.full[t].up(sp.dma_start(x.xs[:, t, :], x_old[b + 1, t]))
                if static(b, 0):
                    load_weights(sp, wt, FIRST, JT)
                x.e_tr.wait(sp, b if last else b + 1, KT - 1, ph.passed)
                for t in range(TT):
                    x.full[t].up(sp.dma_start(x.xs[:, t, :], x_old[b, t]))
                for t in range(TT):
                    x.e_res.wait(sp, b, t, ph.passed)
                    x.stored[t].up(sp.dma_start(x_new[b, t], x.xs[:, t, :]))
            pairs(sp, pro, body)
            for t in range(TT):
                x.stored[t].wait(sp, B - 1, 0)

        @block.tensor
        def _(pe):
            def T(n, c):
                x.e_xn.wait(pe, n, TT - 1)
                x.e_hf.wait(pe, n, c - 2)
                x.e_tr.up(ln_transpose(nc, x, T_bank[c % 2], c, cst.ident[:, :]))

            def F1(b, par, j):
                if static(b, 0):
                    wt.lo.wait(pe, j, 0)
                if j == 0:
                    x.e_hl.wait(pe, b, KT - 1)
                e_g.wait(pe, b, j - 2)
                for c in range(KT):
                    w = slice(c * P, (c + 1) * P)
                    last = product(nc, f1_bank[j % 2][:, :], Wh[:, j, w], Wl[:, j, w],
                                   x.hTh[:, par, c, :], x.hTl[:, par, c, :], c == 0, c == KT - 1)
                e_f1.up(last)

            def F2(b, j):
                e_gl.wait(pe, b, j)
                for t in range(TT):
                    if j == 0:
                        x.e_res.wait(pe, b, t - TT)
                    ts = slice(t * P, (t + 1) * P)
                    last = product(nc, acc[t][:, :], gh[:, j % 2, ts], gl[:, j % 2, ts], Wh[:, j, S:2 * S],
                                   Wl[:, j, S:2 * S], j == 0, j == JT - 1)
                    if j == JT - 1:
                        e_acc.up(last)
                if j < JT - 1:
                    e_f2.up(last)

            def pro():
                cst.wait_ident(pe)
                for c in range(KT):
                    T(0, c)
                F1(0, 0, 0)

            def body(b, par, last):
                for j in range(1, JT):
                    F1(b, par, j)
                    F2(b, j - 1)
                    if 8 <= j < 12 and not last:
                        T(b + 1, j - 8)
                if not last:
                    F1(b + 1, 1 - par, 0)
                F2(b, JT - 1)
            pairs(pe, pro, body)

        @block.scalar
        def _(act):
            def gelu(b, j):
                e_f1.wait(act, b, j)
                e_gl.wait(act, b, j - 2)
                e_g.up(nc.scalar.activation(gf[:, j % 2, :], f1_bank[j % 2][:, :], ACT.Gelu, bias=b1[:, j:j + 1]))
                e_g.wait(act, b, j)
                if j == 0:
                    e_f2.wait(act, b, -1)
                elif j == 1:
                    e_acc.wait(act, b, -1)
                else:
                    e_f2.wait(act, b, j - 2)
                e_gh.up(nc.scalar.activation(gh[:, j % 2, :], gf[:, j % 2, :], ACT.Copy))

            def weights_hi(i):
                wt.full[i % wt.ns].wait(act, i // wt.ns, 0)
                wt.hi.up(weight_hi(nc, wt, i))

            def whole(n, c):
                x.e_tr.wait(act, n, c)
                x.e_hl.wait(act, n, c - x.temps)
                x.e_hf.up(ln_whole(nc, x, T_bank[c % 2], c))

            def pro():
                cst.wait_cols(act)
                weights_hi(0)
                for c in range(KT):
                    whole(0, c)
                weights_hi(1)
                gelu(0, 0)

            def body(b, par, last):
                for j in range(1, JT):
                    if static(b, 0) and j + 1 < JT:
                        weights_hi(j + 1)
                    gelu(b, j)
                    if 8 <= j < 12 and not last:
                        whole(b + 1, j - 8)
                if not last:
                    gelu(b + 1, 0)
            pairs(act, pro, body)

        @block.vector
        def _(dve):
            def lo(b, j):
                e_gh.wait(dve, b, j)
                e_gl.up(nc.vector.tensor_tensor(gl[:, j % 2, :], gf[:, j % 2, :], f32(gh[:, j % 2, :]), ALU.subtract))

            def weights_lo(i):
                wt.hi.wait(dve, i, 0)
                wt.lo.up(weight_lo(nc, wt, i))

            def stat(n, t):
                x.full[t].wait(dve, n, 0 if static(n, 0) else -1)
                x.e_st.up(ln_stats(nc, x, t))

            def aggregate(n):
                for t in range(TT):
                    x.e_st.wait(dve, n, t, ph.passed)
                    x.e_mv.up(ln_mean(nc, x, t))

            def normalise(n):
                x.e_rs.wait(dve, n, 0)
                for t in range(TT):
                    x.e_xn.up(ln_normalise(nc, x, t))

            def hi(n, c, par):
                x.e_hf.wait(dve, n, c)
                x.e_hh.up(ln_hi(nc, x, c, par))

            def pro():
                cst.wait_cols(dve)
                for t in range(TT):
                    stat(0, t)
                aggregate(0)
                normalise(0)
                weights_lo(0)
                for c in range(KT):
                    hi(0, c, 0)
                weights_lo(1)
                lo(0, 0)

            def body(b, par, last):
                for j in range(1, JT):
                    if static(b, 0) and j + 1 < JT:
                        weights_lo(j + 1)
                    lo(b, j)
                    if not last:
                        if 1 <= j < 5:
                            stat(b + 1, j - 1)
                        if j == 5:
                            aggregate(b + 1)
                        if j == 6:
                            normalise(b + 1)
                        if 8 <= j < 12:
                            hi(b + 1, j - 8, 1 - par)
                if not last:
                    lo(b + 1, 0)
                for t in range(TT):
                    x.e_xb.wait(dve, b, t)
                    e_acc.wait(dve, b, t)
                    x.e_res.up(add_out(nc, x, acc[t], t))
            pairs(dve, pro, body)

        @block.gpsimd
        def _(pool):
            def layer_norm(n, par):
                x.e_mv.wait(pool, n, TT - 1, ph.passed)
                x.e_ve.up(ln_eps(nc, x))
                x.e_power.wait(pool, 0, 0)
                x.e_ve.wait(pool, n, 0)
                x.e_rs.up(ln_rsqrt(nc, x))
                for c in range(KT):
                    x.e_hh.wait(pool, n, c)
                    x.e_hl.up(ln_lo(nc, x, c, par))

            def pro():
                x.e_power.up(ln_power(nc, x))
                layer_norm(0, 0)

            def body(b, par, last):
                if not last:
                    layer_norm(b + 1, 1 - par)
                if static(b, 0):
                    x.bias_in.wait(pool, 0, 0)
                for t in range(TT):
                    x.full[t].wait(pool, b, 1 if last else 2)
                    x.e_xb.up(add_bias(nc, x, t))
            pairs(pool, pro, body)


def self_attention(nc, name, cst, x_in, x_out, ln_w, ln_b, wq, bq, wk, bk, wv, bv, wo, bo_row):
    with ExitStack() as ctx:
        ph = Phase(nc, ctx, name)
        W = {n: (ph.sb(f"{n}h", [P, KT, D], F32R), ph.sb(f"{n}l", [P, KT, D], F32R)) for n in ("wq", "wk", "wv", "wo")}
        stack = {n: ph.sb(f"stack_{n}", [P, 2, 4, S], F32R) for n in "qk"}
        parts = {n: ph.sb(f"parts_{n}", [P, 2, S], F32R) for n in "qk"}
        Vh, Vl = (ph.sb(n, [P, TT, D], F32R) for n in ("Vh", "Vl"))
        Vbh, Vbl = (ph.sb(n, [P, TT, 4, P], F32R) for n in ("Vbh", "Vbl"))
        Pr = ph.sb("Pr", [P, 2, TT, S])
        PTh, PTl = (ph.sb(n, [P, 2, S], F32R) for n in ("PTh", "PTl"))
        nmax, rsum, rinv = (ph.sb(n, [P, 2, TT]) for n in ("nmax", "rsum", "rinv"))
        bqs = ph.sb("bqs", [P, KT])
        oTh, oTl = ph.sb("oTh", [P, G, S], F32R), ph.sb("oTl", [P, G, S], F32R)
        x = token_buffers(ph, ln_w, ln_b, temps=1)
        x_old, x_new = token_tiles(x_in), token_tiles(x_out)
        wt = weight_staging(ph, [flat(Pr[:, i // 2, 2 * (i % 2):2 * (i % 2) + 2, :]) for i in range(4)])
        for n, w, scale in (("wq", wq, SCALE), ("wk", wk, 1.0), ("wv", wv, 1.0), ("wo", wo, 1.0)):
            add_matrix(wt, w, *W[n], scale)
        QK_CHUNKS, V_CHUNKS, CHUNKS = 4, 6, 8
        TILES = H * TT
        pj, s_bank, t_bank, o_bank = ph.banks("pj", 2), ph.banks("s", 3), ph.banks("t", 2), ph.banks("o", 1)[0]

        e_zero = ph.events("v_zero", 2)
        e_bqs = ph.events("bqs_set")
        e_v = ph.events("v", TT)
        e_vh, e_vl = ph.events("vh", TT), ph.events("vl", TT)
        e_vb = ph.events("vb", 2 * H)
        e_qk = ph.events("qk", 2 * G)
        e_qkh, e_qkl = ph.events("qkh", 2 * G), ph.events("qkl", 2 * G)
        e_stack = ph.events("stack", 2 * G, 16 * 8)
        e_s = ph.events("s", TILES)
        e_mx = ph.events("mx", TILES)
        e_ex = ph.events("ex", TILES)
        e_ri = ph.events("ri", TILES)
        e_pn = ph.events("pn", TILES)
        e_tp = ph.events("tp", TILES)
        e_ph, e_pl = ph.events("ph", TILES), ph.events("pl", TILES)
        e_pv = ph.events("pv", TILES)
        e_oh, e_ol = ph.events("oh", G), ph.events("ol", G)
        e_out = ph.events("out", TT)

        LEAD, LAG = 6, 2
        JOBS = {2: ("qk", 0, 1, 0), 4: ("qk", 0, 1, 1),
                7: ("O", -1, 0), 9: ("O", -1, 1), 12: ("O", -1, 2), 14: ("O", -1, 3),
                18: ("qk", 0, 2, 0), 21: ("qk", 0, 2, 1), 29: ("qk", 0, 3, 0), 34: ("qk", 0, 3, 1),
                36: ("T", 1, 0), 38: ("T", 1, 1), 40: ("T", 1, 2), 42: ("T", 1, 3),
                44: ("qk", 1, 0, 0), 46: ("qk", 1, 0, 1),
                51: ("V", 1, 0), 53: ("V", 1, 1), 56: ("V", 1, 2), 58: ("V", 1, 3)}

        def jobs(b, last, v, actions):
            kind, ahead, *which = JOBS.get(v, (None, 0))
            if kind and not (ahead == 1 and last) and not (ahead == -1 and static(b, 0)):
                actions[kind](b + ahead, *which)

        def tile(b, s):
            return (b, s) if s < TILES else (b + 1, s - TILES)

        def s_bank_of(s):
            return s_bank[s % 3]

        def s_before(s):
            return s - 3 if s >= 3 else {0: -1, 1: -3, 2: -2}[s]

        block = ctx.enter_context(nc.Block())

        @block.sync
        def _(sp):
            def stacks(b, g):
                for i, n in enumerate("qk"):
                    e_qkl.wait(sp, b, 2 * g + i, ph.passed)
                    e_s.wait(sp, b, 4 * (g - 1) * TT - 1, ph.passed)
                    for j in range(4):
                        src = f32(parts[n][32 * j:32 * j + 32, :, :])
                        for half in range(2):
                            rows = src if n == "k" else src[:, half:half + 1, :].broadcast_to([HD, 2, S])
                            sp.dma_start(f32(stack[n][64 * half:64 * half + 64, g % 2, j, :]), rows)\
                              .then_inc(e_stack.sem, 16)

            def store(b):
                for t in range(TT):
                    x.e_res.wait(sp, b, t, ph.passed)
                    x.stored[t].up(sp.dma_start(x_new[b, t], x.xs[:, t, :]))

            def pro():
                for t in range(TT):
                    x.full[t].up(sp.dma_start(x.xs[:, t, :], x_old[0, t]))
                load_weights(sp, wt, 0, CHUNKS)
                x.bias_in.up(sp.dma_start(x.bias[:, :], bo_row.partition_broadcast(P)))
                stacks(0, 0)

            def body(b, last):
                stacks(b, 1)
                if static(b, 0):
                    x.e_tr.wait(sp, 0, KT - 1)
                else:
                    store(b - 1)
                if not last:
                    for t in range(TT):
                        x.stored[t].wait(sp, b - 1, 0, ph.passed)
                        x.full[t].up(sp.dma_start(x.xs[:, t, :], x_old[b + 1, t]))
                stacks(b, 2)
                stacks(b, 3)
                if last:
                    for t in range(TT):
                        x.stored[t].wait(sp, b - 1, 0)
                        x.full[t].up(sp.dma_start(x.xs[:, t, :], x_old[b, t]))
                    store(b)
                else:
                    x.e_tr.wait(sp, b + 1, KT - 1, ph.passed)
                    for t in range(TT):
                        x.full[t].up(sp.dma_start(x.xs[:, t, :], x_old[b, t]))
                    stacks(b + 1, 0)
            run(sp, pro, body)
            for t in range(TT):
                x.stored[t].wait(sp, B - 1, 0)

        @block.tensor
        def _(pe):
            def T(n, c):
                x.e_xn.wait(pe, n, TT - 1)
                if c < 2:
                    e_qkl.wait(pe, n, c - 2)
                else:
                    x.e_hf.wait(pe, n, c - 2)
                x.e_tr.up(ln_transpose(nc, x, pj[c % 2], c, cst.ident[:, :]))

            def qk(b, g, i):
                if g == 0:
                    x.e_hl.wait(pe, b, KT - 1)
                elif g == 1:
                    e_vl.wait(pe, b, 2 + i)
                elif g == 2 and not static(b, 0):
                    x.e_res.wait(pe, b - 1, 2 + i)
                else:
                    e_qkl.wait(pe, b, 2 * (g - 1) + i)
                wh, wl = W["w" + "qk"[i]]
                gs = slice(g * P, (g + 1) * P)
                for c in range(KT):
                    last = product(nc, pj[i][:, :], wh[:, c, gs], wl[:, c, gs], x.hTh[:, 0, c, :],
                                   x.hTl[:, 0, c, :], c == 0, c == KT - 1)
                e_qk.up(last)

            def V(b, t):
                if static(b, 0):
                    wt.lo.wait(pe, V_CHUNKS - 1, 0)
                if t < 2:
                    e_qkl.wait(pe, b, t)
                else:
                    e_vl.wait(pe, b, t - 2)
                ts = slice(t * P, (t + 1) * P)
                wh, wl = W["wv"]
                for c in range(KT):
                    last = product(nc, pj[t % 2][:, :], x.hTh[:, 0, c, ts], x.hTl[:, 0, c, ts], wh[:, c, :],
                                   wl[:, c, :], c == 0, c == KT - 1)
                e_v.up(last)

            def scores(b, s):
                h, qt = s // TT, s % TT
                g, j = h // 4, h % 4
                if qt == 0 and j == 0:
                    e_stack.wait(pe, b, 2 * g + 1)
                e_ex.wait(pe, b, s_before(s))
                e_s.up(nc.tensor.matmul(s_bank_of(s)[:, :], stack["q"][:, g % 2, j, qt * P:(qt + 1) * P],
                                        stack["k"][:, g % 2, j, :], start=True, stop=True))

            def P_transposed(b, v):
                h, pair, kp = v // 4, v // 2 % 2, v % 2
                if kp == 0:
                    e_pn.wait(pe, b, v + 1)
                e_pl.wait(pe, b, v - 2)
                for k in range(2):
                    for q in range(2):
                        kt, qt = 2 * kp + k, 2 * pair + q
                        last = nc.tensor.transpose(t_bank[v % 2][:, (2 * k + q) * P:(2 * k + q + 1) * P],
                                                   Pr[:, h % 2, qt, kt * P:(kt + 1) * P], cst.ident[:, :])
                e_tp.up(last)

            def PV(b, v):
                h, pair, kp = v // 4, v // 2 % 2, v % 2
                g, j = h // 4, h % 4
                if v % 4 == 0:
                    e_vb.wait(pe, b, 2 * h + 1)
                if v % 16 == 0:
                    e_ol.wait(pe, b, g - 1)
                e_pl.wait(pe, b, v)
                for k in range(2):
                    kt, cols = 2 * kp + k, slice(2 * k * P, 2 * (k + 1) * P)
                    last = product(nc, o_bank[:, 2 * pair * P:2 * (pair + 1) * P], Vbh[:, kt, j, :], Vbl[:, kt, j, :],
                                   PTh[:, v % 2, cols], PTl[:, v % 2, cols], v % 16 == 0 and k == 0,
                                   v % 16 == 15 and k == 1)
                e_pv.up(last)

            def O(b, t, last=False):
                if t == 0:
                    e_ol.wait(pe, b, G - 1)
                if t >= 2:
                    x.e_res.wait(pe, b, t - 2)
                elif last:
                    e_qkl.wait(pe, b, 6 + t)
                else:
                    e_qkl.wait(pe, b + 1, 2 + t)
                ts = slice(t * P, (t + 1) * P)
                wh, wl = W["wo"]
                for g in range(G):
                    m = product(nc, pj[t % 2][:, :], oTh[:, g, ts], oTl[:, g, ts], wh[:, g, :], wl[:, g, :],
                                g == 0, g == G - 1)
                e_out.up(m)

            def pro():
                cst.wait_ident(pe)
                for c in range(KT):
                    T(0, c)
                wt.lo.wait(pe, QK_CHUNKS - 1, 0)
                for i in range(2):
                    qk(0, 0, i)
                for t in range(TT):
                    V(0, t)
                for s in range(LEAD):
                    scores(0, s)
                wt.lo.wait(pe, CHUNKS - 1, 0)

            def body(b, last):
                for v in range(TILES):
                    jobs(b, last, v, {"qk": qk, "O": O, "T": T, "V": V})
                    if not (last and v + LEAD >= TILES):
                        scores(*tile(b, v + LEAD))
                    P_transposed(b, v)
                    if v >= LAG:
                        PV(b, v - LAG)
                    elif not static(b, 0):
                        PV(b - 1, v - LAG + TILES)
                if last:
                    for v in range(TILES - LAG, TILES):
                        PV(b, v)
                    for t in range(TT):
                        O(b, t, last=True)
            run(pe, pro, body)

        @block.scalar
        def _(act):
            def qk_hi(b, g, i):
                e_qk.wait(act, b, 2 * g + i)
                e_stack.wait(act, b, 2 * (g - 1) + i)
                e_qkh.up(add_hi(nc, parts["qk"[i]][:, 0, :], pj[i][:, :], (bqs if i == 0 else bk)[:, g:g + 1]))

            def v_hi(b, t):
                e_v.wait(act, b, t)
                e_vb.wait(act, b, -1)
                e_vh.up(add_hi(nc, Vh[:, t, :], pj[t % 2][:, :], None))

            def exp(b, s):
                h, qt = s // TT, s % TT
                e_mx.wait(act, b, s)
                e_tp.wait(act, b, (s - 8) // 2 * 2 + 1)
                e_ex.up(nc.scalar.activation(Pr[:, h % 2, qt, :], s_bank_of(s)[:, :], ACT.Exp,
                                             bias=nmax[:, h % 2, qt:qt + 1], accum_out=rsum[:, h % 2, qt:qt + 1]))

            def p_hi(b, v):
                e_tp.wait(act, b, v)
                e_pv.wait(act, b, v - 2)
                e_ph.up(add_hi(nc, PTh[:, v % 2, :], t_bank[v % 2][:, :], None))

            def o_hi(b, g):
                e_pv.wait(act, b, (4 * g + 4) * TT - 1)
                e_out.wait(act, b, -1)
                e_oh.up(add_hi(nc, oTh[:, g, :], o_bank[:, :], bv[:, g:g + 1]))

            def whole(n, c):
                x.e_tr.wait(act, n, c)
                x.e_hl.wait(act, n, c - x.temps)
                x.e_hf.up(ln_whole(nc, x, pj[c % 2], c))

            def weights_hi(first, end):
                for i in range(first, end):
                    wt.full[i % wt.ns].wait(act, i // wt.ns, 0)
                    wt.hi.up(weight_hi(nc, wt, i))

            def pro():
                cst.wait_cols(act)
                weights_hi(0, QK_CHUNKS)
                for c in range(KT):
                    whole(0, c)
                e_bqs.wait(act, 0, 0)
                for i in range(2):
                    qk_hi(0, 0, i)
                weights_hi(QK_CHUNKS, CHUNKS)
                for t in range(TT):
                    v_hi(0, t)
                for s in range(LEAD):
                    exp(0, s)

            def body(b, last):
                for v in range(TILES):
                    if v == LAG and not static(b, 0):
                        o_hi(b - 1, G - 1)
                    elif v % 16 == LAG and v > LAG:
                        o_hi(b, v // 16 - 1)
                    jobs(b, last, v, {"qk": qk_hi, "O": lambda n, t: None, "T": whole, "V": v_hi})
                    p_hi(b, v)
                    if not (last and v + LEAD >= TILES):
                        exp(*tile(b, v + LEAD))
                if last:
                    o_hi(b, G - 1)
            run(act, pro, body)

        @block.vector
        def _(dve):
            def qk_lo(b, g, i):
                e_qkh.wait(dve, b, 2 * g + i)
                n = "qk"[i]
                e_qkl.up(add_lo(nc, parts[n][:, 1, :], parts[n][:, 0, :], pj[i][:, :],
                                (bqs if i == 0 else bk)[:, g:g + 1]))

            def v_lo(b, t):
                e_vh.wait(dve, b, t)
                e_vl.up(add_lo(nc, Vl[:, t, :], Vh[:, t, :], pj[t % 2][:, :], None))

            def maximum(b, s):
                h, qt = s // TT, s % TT
                e_s.wait(dve, b, s)
                e_mx.up(nc.vector.reduce_max(nmax[:, h % 2, qt:qt + 1], s_bank_of(s)[:, :], AX.X, negate=True))

            def inverse(b, s):
                h, qt = s // TT, s % TT
                e_ex.wait(dve, b, s)
                e_ri.up(nc.vector.reciprocal(rinv[:, h % 2, qt:qt + 1], rsum[:, h % 2, qt:qt + 1]))

            def p_lo(b, v):
                e_ph.wait(dve, b, v)
                e_pl.up(add_lo(nc, PTl[:, v % 2, :], PTh[:, v % 2, :], t_bank[v % 2][:, :], None))

            def o_lo(b, g):
                e_oh.wait(dve, b, g)
                e_ol.up(add_lo(nc, oTl[:, g, :], oTh[:, g, :], o_bank[:, :], bv[:, g:g + 1]))

            def stat(n, t):
                x.full[t].wait(dve, n, 0 if static(n, 0) else -1)
                x.e_st.up(ln_stats(nc, x, t))

            def aggregate(n):
                for t in range(TT):
                    x.e_st.wait(dve, n, t, ph.passed)
                    x.e_mv.up(ln_mean(nc, x, t))

            def normalise(n, t):
                x.e_rs.wait(dve, n, 0)
                x.e_xn.up(ln_normalise(nc, x, t))

            def hi(n, c):
                x.e_hf.wait(dve, n, c)
                x.e_hh.up(ln_hi(nc, x, c))

            def weights_lo(first, end):
                for i in range(first, end):
                    wt.hi.wait(dve, i, 0)
                    wt.lo.up(weight_lo(nc, wt, i))

            def add_output(b, t):
                x.e_xb.wait(dve, b, t)
                e_out.wait(dve, b, t)
                x.e_res.up(add_out(nc, x, pj[t % 2], t))

            def pro():
                cst.wait_cols(dve)
                e_bqs.up(nc.vector.tensor_scalar(bqs[:, :], bq, SCALE, None, ALU.mult))
                for t in range(TT):
                    stat(0, t)
                aggregate(0)
                for t in range(TT):
                    normalise(0, t)
                weights_lo(0, QK_CHUNKS)
                for c in range(KT):
                    hi(0, c)
                e_bqs.wait(dve, 0, 0)
                for i in range(2):
                    qk_lo(0, 0, i)
                weights_lo(QK_CHUNKS, CHUNKS)
                for t in range(TT):
                    v_lo(0, t)
                for s in range(LEAD):
                    maximum(0, s)
                    if s:
                        inverse(0, s - 1)

            def body(b, last):
                for v in range(TILES):
                    if v == LAG and not static(b, 0):
                        o_lo(b - 1, G - 1)
                    elif v % 16 == LAG and v > LAG:
                        o_lo(b, v // 16 - 1)
                    jobs(b, last, v, {"qk": qk_lo, "O": add_output, "T": hi, "V": v_lo})
                    if not (last and v + LEAD >= TILES):
                        maximum(*tile(b, v + LEAD))
                    p_lo(b, v)
                    if not (last and v + LEAD - 1 >= TILES):
                        inverse(*tile(b, v + LEAD - 1))
                    if not last:
                        if 22 <= v < 26:
                            stat(b + 1, v - 22)
                        if v == 26:
                            aggregate(b + 1)
                        if 28 <= v < 32:
                            normalise(b + 1, v - 28)
                if last:
                    o_lo(b, G - 1)
                    for t in range(TT):
                        add_output(b, t)
            run(dve, pro, body)

        @block.gpsimd
        def _(pool):
            def normal(b, s):
                h, qt = s // TT, s % TT
                e_ri.wait(pool, b, s, ph.passed)
                p = Pr[:, h % 2, qt, :]
                e_pn.up(nc.gpsimd.tensor_scalar(p, p, rinv[:, h % 2, qt:qt + 1], 0.0, ALU.mult, ALU.add))

            def place_v(b, h):
                j = h % 4
                e_pv.wait(pool, b, (h - 4) * TT + TT - 1, ph.passed)
                if h == 0:
                    e_vl.wait(pool, b, TT - 1, ph.passed)
                for dst, src in ((Vbh, Vh), (Vbl, Vl)):
                    e_vb.up(nc.gpsimd.tensor_copy(dst[:, :, j, HD * j:HD * (j + 1)],
                                                  f32(src[:, :, HD * h:HD * (h + 1)])))

            def pro():
                x.e_power.up(ln_power(nc, x))
                x.e_mv.wait(pool, 0, TT - 1)
                x.e_ve.up(ln_eps(nc, x))
                x.e_power.wait(pool, 0, 0)
                x.e_ve.wait(pool, 0, 0)
                x.e_rs.up(ln_rsqrt(nc, x))
                for z in (Vbh, Vbl):
                    e_zero.up(nc.gpsimd.memset(f32(z[:, :, :, :]), 0.0))
                for c in range(KT):
                    x.e_hh.wait(pool, 0, c)
                    x.e_hl.up(ln_lo(nc, x, c))
                x.bias_in.wait(pool, 0, 0)
                e_zero.wait(pool, 0, 1)
                for h in range(3):
                    place_v(0, h)
                for s in range(LEAD - 1):
                    normal(0, s)

            def body(b, last):
                for v in range(TILES):
                    if v % 4 == 2 and v // 4 + 3 < H:
                        place_v(b, v // 4 + 3)
                    if not (last and v + LEAD - 1 >= TILES):
                        normal(*tile(b, v + LEAD - 1))
                    if not last:
                        if v == 26:
                            x.e_mv.wait(pool, b + 1, TT - 1, ph.passed)
                            x.e_ve.up(ln_eps(nc, x))
                            x.e_ve.wait(pool, b + 1, 0)
                            x.e_rs.up(ln_rsqrt(nc, x))
                        if JOBS.get(v, "-")[0] == "T":
                            x.e_hh.wait(pool, b + 1, JOBS[v][2])
                            x.e_hl.up(ln_lo(nc, x, JOBS[v][2]))
                        if v >= TILES - 3:
                            place_v(b + 1, v - (TILES - 3))
                    if v in (48, 50, 52, 54):
                        x.full[(v - 48) // 2].wait(pool, b, 1 if last else 2)
                        x.e_xb.up(add_bias(nc, x, (v - 48) // 2))
            run(pool, pro, body)


def context_kv(nc, name, cst, ctx_in, ln, wk, bk, wv, K, V, later):
    with ExitStack() as ctx:
        ph = Phase(nc, ctx, name)
        N = B * L
        x = ph.sb("x", [L, B, CTX])
        cTh, cTl = ph.sb("cTh", [P, CT, N], F32R), ph.sb("cTl", [P, CT, N], F32R)
        tmp = ph.sb("tmp", [P, 2, GL])
        W = [(ph.sb(f"w{n}h", [P, CT, D], F32R), ph.sb(f"w{n}l", [P, CT, D], F32R)) for n in "kv"]
        wt = weight_staging(ph, [ph.sb(f"stage{i}", [P, CT * D]) for i in range(2)])
        for (wh, wl), w in zip(W, (wk, wv)):
            add_matrix(wt, w, wh, wl, rows=CT)
        stats, mv, ve, rs, power = (ph.sb(n, [L, B, k]) for n, k in
                                    (("stats", 6), ("mv", 2), ("ve", 1), ("rs", 1), ("power", 1)))
        banks = ph.banks("bank", 8)
        e_x = ph.events("x", 1, 16)
        e_st, e_mv, e_ve, e_rs, e_pw = (ph.events(n) for n in ("st", "mv", "ve", "rs", "pw"))
        e_xn = ph.events("xn")
        e_t = ph.events("t")
        e_hf = ph.events("hf")
        e_hh = ph.events("hh")
        e_hl = ph.events("hl")
        e_k, e_kc = ph.events("k"), ph.events("kc")
        e_v, e_vc = ph.events("v"), ph.events("vc")
        tiles = [(half, c) for half in range(2) for c in range(CT)]
        keys = [(g, half) for g in range(G) for half in range(2)]
        NT, NK = len(tiles), len(keys)
        block = ctx.enter_context(nc.Block())

        @block.sync
        def _(sp):
            e_x.up(sp.dma_start(x[:, :, :], ctx_in.rearrange("b l d -> l b d")))
            load_weights(sp, wt, 0, 2)
            load_weights(sp, later, 0, len(later.chunks))

        @block.vector
        def _(dve):
            cst.wait_cols(dve)
            e_x.wait(dve, 0, 0)
            if ln:
                for b in range(B):
                    e_st.up(nc.vector.bn_stats(stats[:, b, :], x[:, b, :]))
                for b in range(B):
                    e_st.wait(dve, b, 0)
                    e_mv.up(nc.vector.bn_aggr(mv[:, b, :], stats[:, b, :]))
                e_rs.wait(dve, 0, 0)
                for b in range(B):
                    e_xn.up(nc.vector.tensor_scalar(x[:, b, :], x[:, b, :], mv[:, b, 0:1], rs[:, b, :],
                                                    ALU.subtract, ALU.mult))
            wt.hi.wait(dve, 0, 0)
            wt.lo.up(weight_lo(nc, wt, 0))
            for u, (half, c) in enumerate(tiles):
                lo, hi = cTl[:, c, half * GL:(half + 1) * GL], cTh[:, c, half * GL:(half + 1) * GL]
                if ln:
                    e_t.wait(dve, u, 0)
                    e_hl.wait(dve, u - 2, 0)
                    e_hf.up(nc.vector.tensor_scalar(tmp[:, u % 2, :], banks[u][:, 0:GL], ln[0][:, c:c + 1],
                                                    ln[1][:, c:c + 1], ALU.mult, ALU.add))
                    e_hh.wait(dve, u, 0)
                    e_hl.up(nc.vector.tensor_tensor(lo, tmp[:, u % 2, :], f32(hi), ALU.subtract))
                else:
                    e_hh.wait(dve, u, 0)
                    e_hl.up(nc.vector.tensor_tensor(lo, banks[u][:, 0:GL], f32(hi), ALU.subtract))
            wt.hi.wait(dve, 1, 0)
            wt.lo.up(weight_lo(nc, wt, 1))
            for u, (g, half) in enumerate(keys):
                e_k.wait(dve, u, 0)
                dst, src = K[:, g, half * GL:(half + 1) * GL], banks[(NT + u) % 8][:, 0:GL]
                if bk is None:
                    e_kc.up(nc.vector.tensor_copy(dst, src))
                else:
                    e_kc.up(nc.vector.tensor_scalar(dst, src, bk[:, g:g + 1], None, ALU.add))
                if u % 2:
                    later.hi.wait(dve, u // 2, 0)
                    later.lo.up(weight_lo(nc, later, u // 2))

        @block.gpsimd
        def _(pool):
            if ln:
                e_pw.up(nc.gpsimd.memset(power[:, :, :], -0.5))
                e_mv.wait(pool, B - 1, 0)
                e_ve.up(nc.gpsimd.tensor_scalar(ve[:, :, 0], mv[:, :, 1], EPS, 1.0, ALU.add, ALU.mult))
                e_ve.wait(pool, 0, 0)
                e_pw.wait(pool, 0, 0)
                e_rs.up(nc.gpsimd.tensor_tensor(rs[:, :, 0], ve[:, :, 0], power[:, :, 0], ALU.pow))

        @block.scalar
        def _(act):
            cst.wait_cols(act)
            wt.full[0].wait(act, 0, 0)
            wt.hi.up(weight_hi(nc, wt, 0))
            for u, (half, c) in enumerate(tiles):
                hi = cTh[:, c, half * GL:(half + 1) * GL]
                if ln:
                    e_hf.wait(act, u, 0)
                    e_hh.up(nc.scalar.activation(hi, tmp[:, u % 2, :], ACT.Copy))
                else:
                    e_t.wait(act, u, 0)
                    e_hh.up(nc.scalar.activation(hi, banks[u][:, 0:GL], ACT.Copy))
            wt.full[1].wait(act, 0, 0)
            wt.hi.up(weight_hi(nc, wt, 1))
            for i in range(len(later.chunks)):
                later.full[i % later.ns].wait(act, i // later.ns, 0)
                later.hi.up(weight_hi(nc, later, i))
            for b in range(B):
                e_v.wait(act, b, 0)
                e_vc.up(nc.scalar.activation(V[:, b, :], banks[(NT + NK + b) % 8][0:L, :], ACT.Copy))

        @block.tensor
        def _(pe):
            cst.wait_ident(pe)
            e_x.wait(pe, 0, 0)
            if ln:
                e_xn.wait(pe, B - 1, 0)
            for u, (half, c) in enumerate(tiles):
                for i in range(4):
                    last = nc.tensor.transpose(banks[u][:, i * L:(i + 1) * L], x[:, half * 4 + i, c * P:(c + 1) * P],
                                               cst.ident[0:L, 0:L])
                e_t.up(last)
            e_hl.wait(pe, NT - 1, 0)
            wt.lo.wait(pe, 1, 0)
            for u, (g, half) in enumerate(keys):
                gs, hs = slice(g * P, (g + 1) * P), slice(half * GL, (half + 1) * GL)
                for c in range(CT):
                    last = product(nc, banks[(NT + u) % 8][:, 0:GL], W[0][0][:, c, gs], W[0][1][:, c, gs],
                                   cTh[:, c, hs], cTl[:, c, hs], c == 0, c == CT - 1)
                e_k.up(last)
            for b in range(B):
                e_kc.wait(pe, b, 0)
                ls = slice(b * L, (b + 1) * L)
                for c in range(CT):
                    last = product(nc, banks[(NT + NK + b) % 8][0:L, :], cTh[:, c, ls], cTl[:, c, ls],
                                   W[1][0][:, c, :], W[1][1][:, c, :], c == 0, c == CT - 1)
                e_v.up(last)


def cross_attention(nc, name, cst, x_in, x_out, ctx_in, ln_w, ln_b, ctx_ln, wq, bq, wk, bk, wv, bv, wo, bo_row):
    with ExitStack() as ctx:
        ph = Phase(nc, ctx, name)
        K, Vall = ph.sb("K", [P, G, B * L]), ph.sb("Vall", [L, B, D])
        W = {n: (ph.sb(f"{n}h", [P, KT, D], F32R), ph.sb(f"{n}l", [P, KT, D], F32R)) for n in ("wq", "wo")}
        wt = weight_staging(ph, [ph.sb(f"stage{i}", [P, 2 * D]) for i in range(2)])
        add_matrix(wt, wq, *W["wq"], SCALE)
        add_matrix(wt, wo, *W["wo"])
        context_kv(nc, name + "_kv", cst, ctx_in, ctx_ln, wk, bk, wv, K, Vall, wt)

        Kbh, Kbl = (ph.sb(n, [P, G, 4, L], F32R) for n in ("Kbh", "Kbl"))
        Vbh, Vbl = (ph.sb(n, [P, G, 4, P], F32R) for n in ("Vbh", "Vbl"))
        qTh, qTl = ph.sb("qTh", [P, G, S], F32R), ph.sb("qTl", [P, G, S], F32R)
        Pr = ph.sb("Pr", [P, G, TT, GL])
        PTh, PTl = (ph.sb(n, [L, 2, S], F32R) for n in ("PTh", "PTl"))
        nmax, rsum, rinv = (ph.sb(n, [P, G, TT, 4]) for n in ("nmax", "rsum", "rinv"))
        bqs = ph.sb("bqs", [P, KT])
        oTh, oTl = ph.sb("oTh", [P, G, S], F32R), ph.sb("oTl", [P, G, S], F32R)
        x = token_buffers(ph, ln_w, ln_b)
        x_old, x_new = token_tiles(x_in), token_tiles(x_out)
        pj, s_bank, t_bank, o_bank = ph.banks("pj", 2), ph.banks("s", 3), ph.banks("t", 2), ph.banks("o", 1)[0]

        e_zero = ph.events("zero", 4)
        e_bqs = ph.events("bqs_set")
        e_kb = ph.events("kb", 8)
        e_vb = ph.events("vb", 8)
        e_q = ph.events("q", G)
        e_qh, e_ql = ph.events("qh", G), ph.events("ql", G)
        e_s = ph.events("s", G * TT)
        e_mx = ph.events("mx", G * TT)
        e_sub = ph.events("sub", G * TT)
        e_ex = ph.events("ex", G * TT)
        e_sum = ph.events("sum", G * TT)
        e_ri = ph.events("ri", G * TT)
        e_pn = ph.events("pn", G * TT)
        e_tp = ph.events("tp", H)
        e_ph, e_pl = ph.events("ph", H), ph.events("pl", H)
        e_pv = ph.events("pv", H)
        e_oh, e_ol = ph.events("oh", G), ph.events("ol", G)
        e_out = ph.events("out", TT)

        EARLY = 8
        TAIL = [("Q", 0), ("Q", 1), ("S", 0), ("Q", 2), ("S", 1), ("Q", 3), ("S", 2), ("O", 0), ("S", 3), ("S", 4),
                ("O", 1), ("S", 5), ("O", 2), ("S", 6), ("O", 3), ("S", 7)]
        FIRST_TAIL = [step for step in TAIL if step[0] != "O"]
        LAST_TAIL = [step for step in TAIL if step[0] == "O"]

        block = ctx.enter_context(nc.Block())

        @block.sync
        def _(sp):
            def pro():
                for t in range(TT):
                    x.full[t].up(sp.dma_start(x.xs[:, t, :], x_old[0, t]))
                x.bias_in.up(sp.dma_start(x.bias[:, :], bo_row.partition_broadcast(P)))

            def body(b, last):
                if not last:
                    if static(b, 0):
                        x.e_tr.wait(sp, 0, KT - 1)
                    for t in range(TT):
                        x.stored[t].wait(sp, b - 1, 0, ph.passed)
                        x.full[t].up(sp.dma_start(x.xs[:, t, :], x_old[b + 1, t]))
                x.e_tr.wait(sp, b if last else b + 1, KT - 1, ph.passed)
                for t in range(TT):
                    x.full[t].up(sp.dma_start(x.xs[:, t, :], x_old[b, t]))
                for t in range(TT):
                    x.e_res.wait(sp, b, t, ph.passed)
                    x.stored[t].up(sp.dma_start(x_new[b, t], x.xs[:, t, :]))
            run(sp, pro, body)
            for t in range(TT):
                x.stored[t].wait(sp, B - 1, 0)

        @block.tensor
        def _(pe):
            def T(n, c):
                x.e_xn.wait(pe, n, TT - 1)
                if c < 2:
                    e_ql.wait(pe, n - 1, 2 + c)
                    x.e_res.wait(pe, n - 1, c - 2)
                else:
                    x.e_hf.wait(pe, n, c - 2)
                x.e_tr.up(ln_transpose(nc, x, pj[c % 2], c, cst.ident[:, :]))

            def Q(n, g):
                if g < 2:
                    x.e_hl.wait(pe, n, KT - 1)
                else:
                    e_ql.wait(pe, n, g - 2)
                wh, wl = W["wq"]
                gs = slice(g * P, (g + 1) * P)
                for c in range(KT):
                    last = product(nc, pj[g % 2][:, :], wh[:, c, gs], wl[:, c, gs], x.hTh[:, 0, c, :],
                                   x.hTl[:, 0, c, :], c == 0, c == KT - 1)
                e_q.up(last)

            def scores(b, s):
                g, qt = s // TT, s % TT
                e_ql.wait(pe, b, g)
                if s == 0:
                    e_kb.wait(pe, b, 7)
                e_sub.wait(pe, b, s - S_BEFORE[qt])
                qs = slice(qt * P, (qt + 1) * P)
                kh, kl = (k[:, g, :, :].rearrange("p j l -> p (j l)") for k in (Kbh, Kbl))
                e_s.up(product(nc, s_bank[S_BANK[qt]][:, 0:GL], qTh[:, g, qs], qTl[:, g, qs], kh, kl, True, True))

            def P_transposed(b, h):
                g, j = h // 4, h % 4
                if j == 0:
                    e_pn.wait(pe, b, g * TT + TT - 1)
                e_pl.wait(pe, b, h - 2)
                for qt in range(TT):
                    last = nc.tensor.transpose(t_bank[j % 2][0:L, qt * P:(qt + 1) * P],
                                               Pr[:, g, qt, j * L:(j + 1) * L], cst.ident[:, :])
                e_tp.up(last)

            def PV(b, h):
                g, j = h // 4, h % 4
                if j == 0:
                    e_ol.wait(pe, b, g - 1)
                    e_vb.wait(pe, b, 2 * g + 1)
                e_pl.wait(pe, b, h)
                e_pv.up(product(nc, o_bank[:, :], Vbh[0:L, g, j, :], Vbl[0:L, g, j, :], PTh[:, j % 2, :],
                                PTl[:, j % 2, :], j == 0, j == 3))

            def O(b, last, t):
                if t == 0:
                    e_ol.wait(pe, b, G - 1)
                if t < 2 and not last:
                    e_ql.wait(pe, b + 1, 2 + t)
                else:
                    x.e_res.wait(pe, b, t - 2)
                ts = slice(t * P, (t + 1) * P)
                wh, wl = W["wo"]
                for g in range(G):
                    m = product(nc, pj[t % 2][:, :], oTh[:, g, ts], oTl[:, g, ts], wh[:, g, :], wl[:, g, :],
                                g == 0, g == G - 1)
                e_out.up(m)

            def pro():
                for c in range(KT):
                    T(0, c)
                for step, k in FIRST_TAIL:
                    Q(0, k) if step == "Q" else scores(0, k)

            def body(b, last):
                for h in range(H):
                    if h + EARLY < G * TT:
                        scores(b, h + EARLY)
                    if h // 4 == 2 and not last:
                        T(b + 1, h % 4)
                    P_transposed(b, h)
                    if h:
                        PV(b, h - 1)
                PV(b, H - 1)
                for step, k in LAST_TAIL if last else TAIL:
                    if step == "Q":
                        Q(b + 1, k)
                    elif step == "S":
                        scores(b + 1, k)
                    else:
                        O(b, last, k)
            run(pe, pro, body)

        @block.scalar
        def _(act):
            def q_hi(n, g):
                e_q.wait(act, n, g)
                e_qh.up(add_hi(nc, qTh[:, g, :], pj[g % 2][:, :], None if bq is None else bqs[:, g:g + 1]))

            def exp(b, s):
                e_sub.wait(act, b, s)
                p = Pr[:, s // TT, s % TT, :]
                e_ex.up(nc.scalar.activation(p, p, ACT.Exp))

            def p_hi(b, h):
                e_tp.wait(act, b, h)
                e_pv.wait(act, b, h - 2)
                e_ph.up(add_hi(nc, PTh[:, h % 2, :], t_bank[h % 2][0:L, :], None))

            def o_hi(b, g):
                e_pv.wait(act, b, 4 * g + 3)
                e_out.wait(act, b, -1)
                e_oh.up(add_hi(nc, oTh[:, g, :], o_bank[:, :], None if bv is None else bv[:, g:g + 1]))

            def whole(n, c):
                x.e_tr.wait(act, n, c)
                x.e_hl.wait(act, n, c - x.temps)
                x.e_hf.up(ln_whole(nc, x, pj[c % 2], c))

            def pro():
                for c in range(KT):
                    whole(0, c)
                if bq is not None:
                    e_bqs.wait(act, 0, 0)
                for step, k in FIRST_TAIL:
                    q_hi(0, k) if step == "Q" else exp(0, k)

            def body(b, last):
                for h in range(H):
                    if h // 4 == 2 and not last:
                        whole(b + 1, h % 4)
                    p_hi(b, h)
                    if h % 4 == 0 and h:
                        o_hi(b, h // 4 - 1)
                    if h + EARLY < G * TT:
                        exp(b, h + EARLY)
                o_hi(b, G - 1)
                if not last:
                    for step, k in FIRST_TAIL:
                        q_hi(b + 1, k) if step == "Q" else exp(b + 1, k)
            run(act, pro, body)

        @block.vector
        def _(dve):
            def q_lo(n, g):
                e_qh.wait(dve, n, g)
                e_ql.up(add_lo(nc, qTl[:, g, :], qTh[:, g, :], pj[g % 2][:, :], None if bq is None else bqs[:, g:g + 1]))

            def centre(b, s):
                g, qt = s // TT, s % TT
                bank = s_bank[S_BANK[qt]][:, 0:GL].rearrange("p (j l) -> p j l", j=4)
                m = nmax[:, g, qt, :]
                e_s.wait(dve, b, s)
                e_mx.up(nc.vector.reduce_max(m, bank, AX.X, negate=True))
                e_mx.wait(dve, b, s)
                e_tp.wait(dve, b - 1, 4 * g + 3)
                e_sub.up(nc.vector.tensor_tensor(Pr[:, g, qt, :].rearrange("p (j l) -> p j l", j=4), bank,
                                                 m.unsqueeze(2).broadcast_to([P, 4, L]), ALU.add))

            def inverse(b, s):
                g, qt = s // TT, s % TT
                e_ex.wait(dve, b, s)
                e_sum.up(nc.vector.reduce_sum(rsum[:, g, qt, :], Pr[:, g, qt, :].rearrange("p (j l) -> p j l", j=4),
                                              AX.X))
                e_sum.wait(dve, b, s)
                e_ri.up(nc.vector.reciprocal(rinv[:, g, qt, :], rsum[:, g, qt, :]))

            def softmax(b, s):
                centre(b, s)
                if s % EARLY:
                    inverse(b, s - 1)

            def p_lo(b, h):
                e_ph.wait(dve, b, h)
                e_pl.up(add_lo(nc, PTl[:, h % 2, :], PTh[:, h % 2, :], t_bank[h % 2][0:L, :], None))

            def o_lo(b, g):
                e_oh.wait(dve, b, g)
                e_ol.up(add_lo(nc, oTl[:, g, :], oTh[:, g, :], o_bank[:, :], None if bv is None else bv[:, g:g + 1]))

            def stat(n, t):
                x.full[t].wait(dve, n, 0 if static(n, 0) else -1)
                x.e_st.up(ln_stats(nc, x, t))

            def aggregate(n):
                for t in range(TT):
                    x.e_st.wait(dve, n, t, ph.passed)
                    x.e_mv.up(ln_mean(nc, x, t))

            def normalise(n, t):
                x.e_rs.wait(dve, n, 0)
                x.e_xn.up(ln_normalise(nc, x, t))

            def hi(n, c):
                x.e_hf.wait(dve, n, c)
                x.e_hh.up(ln_hi(nc, x, c))

            def pro():
                if bq is not None:
                    e_bqs.up(nc.vector.tensor_scalar(bqs[:, :], bq, SCALE, None, ALU.mult))
                    e_bqs.wait(dve, 0, 0)
                for t in range(TT):
                    stat(0, t)
                aggregate(0)
                for t in range(TT):
                    normalise(0, t)
                for c in range(KT):
                    hi(0, c)
                for step, k in FIRST_TAIL:
                    q_lo(0, k) if step == "Q" else softmax(0, k)
                inverse(0, EARLY - 1)

            def body(b, last):
                for h in range(H):
                    if h + EARLY < G * TT:
                        softmax(b, h + EARLY)
                    if h + EARLY == G * TT:
                        inverse(b, G * TT - 1)
                    p_lo(b, h)
                    if h % 4 == 0 and h:
                        o_lo(b, h // 4 - 1)
                    if not last:
                        if h < 4:
                            stat(b + 1, h)
                        if h == 4:
                            aggregate(b + 1)
                        if h in (5, 6):
                            for t in range(2 * (h - 5), 2 * (h - 5) + 2):
                                normalise(b + 1, t)
                        if h // 4 == 2:
                            hi(b + 1, h % 4)
                o_lo(b, G - 1)
                for step, k in LAST_TAIL if last else TAIL:
                    if step == "Q":
                        q_lo(b + 1, k)
                    elif step == "S":
                        softmax(b + 1, k)
                    else:
                        x.e_xb.wait(dve, b, k)
                        e_out.wait(dve, b, k)
                        x.e_res.up(add_out(nc, x, pj[k % 2], k))
                if not last:
                    inverse(b + 1, EARLY - 1)
            run(dve, pro, body)

        @block.gpsimd
        def _(pool):
            def place_k(n, j):
                rows = slice(HD * j, HD * (j + 1))
                src = K[rows, :, bass.ds(n * L, L)]
                e_s.wait(pool, n, -1, ph.passed)
                e_kb.up(nc.gpsimd.tensor_copy(Kbh[rows, :, j, :], src))
                e_kb.wait(pool, n, 2 * j, ph.passed)
                e_kb.up(nc.gpsimd.tensor_tensor(Kbl[rows, :, j, :], src, f32(Kbh[rows, :, j, :]), ALU.subtract))
                e_kb.wait(pool, n, 2 * j + 1, ph.passed)

            def place_v(n, g):
                src = Vall[:, n, P * g:P * (g + 1)].rearrange("p (j d) -> p j d", j=4)
                e_pv.wait(pool, n - 1, 4 * g + 3, ph.passed)
                e_vb.up(nc.gpsimd.tensor_copy(diagonal(Vbh[0:L, g, :, :]), src))
                e_vb.wait(pool, n, 2 * g, ph.passed)
                e_vb.up(nc.gpsimd.tensor_tensor(diagonal(Vbl[0:L, g, :, :]), src, f32(diagonal(Vbh[0:L, g, :, :])),
                                                ALU.subtract))
                e_vb.wait(pool, n, 2 * g + 1, ph.passed)

            def normal(b, s):
                e_ri.wait(pool, b, s, ph.passed)
                p = Pr[:, s // TT, s % TT, :].rearrange("p (j l) -> p j l", j=4)
                e_pn.up(nc.gpsimd.tensor_tensor(p, p, rinv[:, s // TT, s % TT, :].unsqueeze(2).broadcast_to([P, 4, L]),
                                                ALU.mult))

            def rsqrt(n):
                x.e_mv.wait(pool, n, TT - 1, ph.passed)
                x.e_ve.up(ln_eps(nc, x))
                x.e_ve.wait(pool, n, 0)
                x.e_rs.up(ln_rsqrt(nc, x))

            def lo(n, c):
                x.e_hh.wait(pool, n, c)
                x.e_hl.up(ln_lo(nc, x, c))

            def pro():
                x.e_power.up(ln_power(nc, x))
                for z in (Kbh, Kbl, Vbh, Vbl):
                    e_zero.up(nc.gpsimd.memset(f32(z[:, :, :, :]), 0.0))
                x.e_power.wait(pool, 0, 0)
                rsqrt(0)
                e_zero.wait(pool, 0, 3)
                x.e_rs.wait(pool, 0, 0)
                for j in range(4):
                    place_k(0, j)
                for g in range(G):
                    place_v(0, g)
                for c in range(KT):
                    lo(0, c)
                for s in range(EARLY):
                    normal(0, s)
                x.bias_in.wait(pool, 0, 0)

            def body(b, last):
                for h in range(H):
                    if h + EARLY < G * TT:
                        normal(b, h + EARLY)
                    if not last:
                        if h == 4:
                            rsqrt(b + 1)
                        if h == 5:
                            e_pn.wait(pool, b, h + EARLY)
                            place_v(b + 1, 0)
                        if h // 4 == 2:
                            if h % 4:
                                x.e_hl.wait(pool, b + 1, h % 4 - 1)
                            else:
                                e_pn.wait(pool, b, G * TT - 1)
                            place_k(b + 1, h % 4)
                            lo(b + 1, h % 4)
                        if h == 12:
                            x.e_hl.wait(pool, b + 1, KT - 1)
                            place_v(b + 1, 1)
                        if h == 13:
                            place_v(b + 1, 2)
                if not last:
                    place_v(b + 1, 3)
                for t in range(TT):
                    x.full[t].wait(pool, b, 1 if last else 2)
                    x.e_xb.up(add_bias(nc, x, t))
                if not last:
                    for s in range(EARLY):
                        normal(b + 1, s)
            run(pool, pro, body)


class Constants:

    def __init__(self, nc, ctx, cols):
        self.nc = nc
        self.ident = ctx.enter_context(nc.sbuf_tensor("ident", [P, P], F32))
        self.cols = ctx.enter_context(nc.sbuf_tensor("cols", [P, NCOL], F32))
        self.s_ident, self.s_cols = (ctx.enter_context(nc.semaphore(n)) for n in ("s_ident", "s_cols"))
        with nc.Block() as block:
            @block.gpsimd
            def _(pool):
                nc.gpsimd.memset(self.ident[:, :], 0.0).then_inc(self.s_ident, 1)
                pool.wait_ge(self.s_ident, 1)
                nc.gpsimd.affine_select(out=self.ident[:, :], in_=self.ident[:, :], compare_op=ALU.not_equal, fill=1.0,
                                        base=0, pattern=[[-1, P]], channel_multiplier=1).then_inc(self.s_ident, 1)

            @block.sync
            def _(sp):
                sp.dma_start(self.cols[:, :], cols).then_inc(self.s_cols, 16)

    def wait_ident(self, eng):
        eng.wait_ge(self.s_ident, 2)

    def wait_cols(self, eng):
        eng.wait_ge(self.s_cols, 16)

    def col(self, name):
        at, n = COL_AT[name]
        return self.cols[:, at:at + n]


def program(nc, a, out):
    with ExitStack() as ctx:
        cst = Constants(nc, ctx, a["cols"])
        c = cst.col
        x = [a["x"]] + [nc.dram_tensor(f"x_{i}", (B * S, D), F32).ap() for i in range(1, 5)] + [out]
        cross_attention(nc, "L0ca", cst, x[0], x[1], a["ctx"], c("L0_ln1_w"), c("L0_ln1_b"),
                        (c("L0_ln2_w"), c("L0_ln2_b")), a["L0_wq"], None, a["L0_wkv"][:, 0:D], None,
                        a["L0_wkv"][:, D:2 * D], None, a["L0_wo"], a["L0_bo"])
        feed_forward(nc, "L0ff", cst, x[1], x[2], c("L0_ln3_w"), c("L0_ln3_b"), a["L0_w1"], c("L0_b1"),
                     a["L0_w2"], a["L0_b2"])
        self_attention(nc, "L1sa", cst, x[2], x[3], c("L1_ln1_g"), c("L1_ln1_b"), a["L1_sa_wq"], c("L1_sa_bq"),
                       a["L1_sa_wk"], c("L1_sa_bk"), a["L1_sa_wv"], c("L1_sa_bv"), a["L1_sa_wo"], a["L1_sa_bo"])
        cross_attention(nc, "L1ca", cst, x[3], x[4], a["ctx"], c("L1_ln2_g"), c("L1_ln2_b"), None, a["L1_ca_wq"],
                        c("L1_ca_bq"), a["L1_ca_wk"], c("L1_ca_bk"), a["L1_ca_wv"], c("L1_ca_bv"), a["L1_ca_wo"],
                        a["L1_ca_bo"])
        feed_forward(nc, "L1ff", cst, x[4], x[5], c("L1_ln3_g"), c("L1_ln3_b"), a["L1_w1"], c("L1_mlp_b1"),
                     a["L1_w2"], a["L1_b2"])


def kernel(**inputs):
    import concourse.bacc as bacc
    from concourse.bass_utils import run_bass_kernel_spmd

    v = {k.replace("_xattn", ""): np.asarray(w) for k, w in inputs.items()}
    arrays = {
        "x": v["x"].reshape(B * S, D), "ctx": v["ctx_768"],
        "cols": np.concatenate([v[n].reshape(-1, P).T for n, _ in COLS], axis=1),
        "L0_wq": v["L0_Wq"], "L0_wkv": v["L0_Wkv"], "L0_wo": v["L0_Wproj"], "L0_w1": v["L0_W1"], "L0_w2": v["L0_W2"],
        "L0_bo": v["L0_bproj"], "L0_b2": v["L0_b2"], "L1_sa_bo": v["L1_sa_bo"], "L1_ca_bo": v["L1_ca_bo"],
        "L1_b2": v["L1_mlp_b2"],
        "L1_w1": v["L1_mlp_w1"].T, "L1_w2": v["L1_mlp_w2"].T,
    }
    for n in ("sa_wq", "sa_wk", "sa_wv", "sa_wo", "ca_wq", "ca_wk", "ca_wv", "ca_wo"):
        arrays[f"L1_{n}"] = v[f"L1_{n}"].T
    arrays = {k: np.ascontiguousarray(w) for k, w in arrays.items()}

    nc = bacc.Bacc("TRN2", target_bir_lowering=False, num_devices=1)
    aps = {k: nc.dram_tensor(f"in_{k}", w.shape, mybir.dt.from_np(w.dtype), kind="ExternalInput").ap()
           for k, w in arrays.items()}
    out = nc.dram_tensor("out", (B * S, D), F32, kind="ExternalOutput").ap()
    program(nc, aps, out)
    r = run_bass_kernel_spmd(nc, [{f"in_{k}": w for k, w in arrays.items()}], core_ids=[0])
    return r.results[0]["out"].reshape(B, S, D)
```

```python
from contextlib import ExitStack

import numpy as np

import concourse.bass as bass
from concourse import mybir

F32 = mybir.dt.float32
F32R = mybir.dt.float32r
ACT = mybir.ActivationFunctionType
ALU = mybir.AluOpType
AX = mybir.AxisListType

P = 128
B, S, D = 8, 512, 512
L, CTX = 77, 384
H, HD = 16, 32
HID = 4 * D
KT = D // P
CT = CTX // P
TT = S // P
G = H // 4
JT = HID // P
GL = 4 * L
SCALE = HD ** -0.5
EPS = 1e-5

COLS = [("L0_ln1_w", D), ("L0_ln1_b", D), ("L0_ln2_w", CTX), ("L0_ln2_b", CTX), ("L0_ln3_w", D), ("L0_ln3_b", D),
        ("L0_b1", HID), ("L1_ln1_g", D), ("L1_ln1_b", D), ("L1_ln2_g", D), ("L1_ln2_b", D), ("L1_ln3_g", D),
        ("L1_ln3_b", D), ("L1_sa_bq", D), ("L1_sa_bk", D), ("L1_sa_bv", D), ("L1_ca_bq", D), ("L1_ca_bk", D),
        ("L1_ca_bv", D), ("L1_mlp_b1", HID)]
COL_AT, NCOL = {}, 0
for _name, _n in COLS:
    COL_AT[_name] = (NCOL, _n // P)
    NCOL += _n // P


class Events:

    def __init__(self, sem, per, unit=1):
        self.sem, self.per, self.unit = sem, per, unit

    def wait(self, eng, b, k, alone=None):
        v = b * (self.per * self.unit) + (k + 1) * self.unit
        if isinstance(v, int):
            if v > 0:
                eng.wait_ge(self.sem, v)
            return
        eng.wait_ge(self.sem, v)
        if alone is not None:
            eng.sem_inc(alone, 1)

    def up(self, instruction):
        instruction.then_inc(self.sem, self.unit)


class Names:
    pass


class Phase:

    def __init__(self, nc, ctx, name):
        self.nc, self.ctx, self.name, self.sems = nc, ctx, name, []
        self.passed = self.events("passed").sem
        ctx.callback(self.end)

    def end(self):
        self.nc.clear_and_free_semaphores(self.sems)
        self.nc.all_engine_barrier()

    def sb(self, name, shape, dt=F32):
        return self.ctx.enter_context(self.nc.sbuf_tensor(f"{self.name}_{name}", shape, dt))

    def banks(self, name, n):
        return [self.ctx.enter_context(self.nc.psum_tensor(f"{self.name}_{name}{i}", [P, 512], F32)) for i in range(n)]

    def events(self, name, per=1, unit=1):
        self.sems.append(self.nc.alloc_semaphore(f"{self.name}_{name}"))
        return Events(self.sems[-1], per, unit)


def run(eng, pro, body):
    pro()
    body(0, False)
    with eng.Fori(1, B - 1) as b:
        body(b, False)
    body(B - 1, True)


def pairs(eng, pro, body):
    pro()
    for par in range(2):
        body(par, par, False)
    with eng.Fori(1, B // 2 - 1) as i:
        for par in range(2):
            body(i * 2 + par, par, False)
    for par in range(2):
        body(B - 2 + par, par, par == 1)


def exists(b):
    return not isinstance(b, int) or 0 <= b < B


def static(b, value):
    return isinstance(b, int) and b == value


def f32(ap):
    return ap.bitcast(F32)


def flat(ap):
    return ap.rearrange("p a n -> p (a n)")



def product(nc, out, wh, wl, xh, xl, first, last):
    nc.tensor.matmul(out, wh, xh, start=first, stop=False)
    nc.tensor.matmul(out, wl, xh, start=False, stop=False)
    return nc.tensor.matmul(out, wh, xl, start=False, stop=last)


def add_hi(nc, hi, bank, bias):
    if bias is None:
        return nc.scalar.activation(hi, bank, ACT.Copy)
    return nc.scalar.activation(hi, bank, ACT.Identity, bias=bias)


def add_lo(nc, lo, hi, bank, bias):
    if bias is None:
        return nc.vector.tensor_tensor(lo, bank, f32(hi), ALU.subtract)
    return nc.vector.scalar_tensor_tensor(lo, bank, bias, f32(hi), ALU.add, ALU.subtract)


def diagonal(ap):
    return bass.AP(ap.tensor, ap.offset, [list(ap.ap[0]), [P + HD, 4], [1, HD]])


def weight_staging(ph, slots, parts=1):
    wt = Names()
    wt.slots = slots
    wt.ns = len(slots)
    wt.chunks = []
    wt.full = [ph.events(f"w_full{i}", 1, 16 * parts) for i in range(len(slots))]
    wt.hi = ph.events("w_hi")
    wt.lo = ph.events("w_lo")
    return wt


def add_matrix(wt, w, hi, lo, scale=1.0, rows=2):
    v = w.rearrange("(c p) n -> p c n", p=P)
    for c in range(0, v.shape[1], rows):
        wt.chunks.append(([v[:, c:c + rows, :]], flat(hi[:, c:c + rows, :]), flat(lo[:, c:c + rows, :]), scale))


def load_weights(sp, wt, first, end):
    for i in range(first, end):
        wt.lo.wait(sp, i - wt.ns, 0)
        at = 0
        for source in wt.chunks[i][0]:
            n = int(np.prod(source.shape[1:]))
            slot = wt.slots[i % wt.ns][:, at:at + n]
            if len(source.shape) == 3:
                slot = slot.rearrange("p (a n) -> p a n", a=source.shape[1])
            sp.dma_start(slot, source).then_inc(wt.full[i % wt.ns].sem, 16)
            at += n


def weight_hi(nc, wt, i):
    _, hi, _, scale = wt.chunks[i]
    return nc.scalar.activation(hi, wt.slots[i % wt.ns][:, 0:hi.shape[1]], ACT.Copy, scale=scale)


def weight_lo(nc, wt, i):
    _, hi, lo, scale = wt.chunks[i]
    return nc.vector.scalar_tensor_tensor(lo, wt.slots[i % wt.ns][:, 0:hi.shape[1]], scale, f32(hi),
                                          ALU.mult, ALU.subtract)


def token_buffers(ph, w, b, pars=1, temps=2, residual=None):
    x = Names()
    x.w = w
    x.b = b
    x.temps = temps
    x.xs = ph.sb("xs", [P, TT, D])
    x.bias = ph.sb("bias", [P, D])
    x.htmp = ph.sb("htmp", [P, temps, S])
    x.hTh = ph.sb("hTh", [P, pars, KT, S], F32R)
    x.hTl = ph.sb("hTl", [P, pars, KT, S], F32R)
    x.stats = ph.sb("stats", [P, TT, 6])
    x.mv = ph.sb("mv", [P, TT, 2])
    x.ve = ph.sb("ve", [P, TT])
    x.rs = ph.sb("rs", [P, TT])
    x.power = ph.sb("power", [P, TT])
    x.xr = x.xs if residual is None else residual
    loads = 2 if residual is None else 1
    x.full = [ph.events(f"xs_full{t}", loads, 16) for t in range(TT)]
    x.stored = [ph.events(f"stored{t}", 1, 16) for t in range(TT)]
    x.bias_in = ph.events("bias_in", 1, 16)
    x.e_power = ph.events("power_set")
    x.e_st = ph.events("ln_st", TT)
    x.e_mv = ph.events("ln_mv", TT)
    x.e_ve = ph.events("ln_ve")
    x.e_rs = ph.events("ln_rs")
    x.e_xn = ph.events("ln_xn", TT)
    x.e_tr = ph.events("ln_tr", KT)
    x.e_hf = ph.events("ln_hf", KT)
    x.e_hh = ph.events("ln_hh", KT)
    x.e_hl = ph.events("ln_hl", KT)
    x.e_xb = ph.events("xb", TT)
    x.e_res = ph.events("res", TT)
    return x


def token_tiles(x):
    return x.rearrange("(b t p) d -> b t p d", b=B, p=P)



def ln_stats(nc, x, t):
    return nc.vector.bn_stats(x.stats[:, t, :], x.xs[:, t, :])


def ln_mean(nc, x, t):
    return nc.vector.bn_aggr(x.mv[:, t, :], x.stats[:, t, :])


def ln_power(nc, x):
    return nc.gpsimd.memset(x.power[:, :], -0.5)


def ln_eps(nc, x):
    return nc.gpsimd.tensor_scalar(x.ve[:, :], x.mv[:, :, 1], EPS, 1.0, ALU.add, ALU.mult)


def ln_rsqrt(nc, x):
    return nc.gpsimd.tensor_tensor(x.rs[:, :], x.ve[:, :], x.power[:, :], ALU.pow)


def ln_normalise(nc, x, t):
    return nc.vector.tensor_scalar(x.xs[:, t, :], x.xs[:, t, :], x.mv[:, t, 0:1], x.rs[:, t:t + 1],
                                   ALU.subtract, ALU.mult)


def ln_transpose(nc, x, bank, c, ident):
    for t in range(TT):
        last = nc.tensor.transpose(bank[:, t * P:(t + 1) * P], x.xs[:, t, c * P:(c + 1) * P], ident)
    return last


def ln_whole(nc, x, bank, c):
    return nc.scalar.activation(x.htmp[:, c % x.temps, :], bank[:, :], ACT.Identity, bias=x.b[:, c:c + 1],
                                scale=x.w[:, c:c + 1])


def ln_hi(nc, x, c, par=0):
    return nc.vector.tensor_copy(x.hTh[:, par, c, :], x.htmp[:, c % x.temps, :])


def ln_lo(nc, x, c, par=0):
    return nc.gpsimd.tensor_tensor(x.hTl[:, par, c, :], x.htmp[:, c % x.temps, :], f32(x.hTh[:, par, c, :]),
                                   ALU.subtract)


def add_bias(nc, x, t):
    return nc.gpsimd.tensor_tensor(x.xr[:, t, :], x.xr[:, t, :], x.bias[:, :], ALU.add)


def add_out(nc, x, bank, t):
    return nc.vector.tensor_tensor(x.xr[:, t, :], bank[:, :], x.xr[:, t, :], ALU.add)


def feed_forward(nc, name, cst, x_in, x_out, ln_w, ln_b, w1, b1, w2, b2_row):
    with ExitStack() as ctx:
        ph = Phase(nc, ctx, name)
        Wh, Wl = ph.sb("Wh", [P, JT, 2 * S], F32R), ph.sb("Wl", [P, JT, 2 * S], F32R)
        gf = ph.sb("gf", [P, 2, S])
        gh, gl = ph.sb("gh", [P, 2, S], F32R), ph.sb("gl", [P, 2, S], F32R)
        x = token_buffers(ph, ln_w, ln_b, pars=2)
        x_old, x_new = token_tiles(x_in), token_tiles(x_out)
        wt = weight_staging(ph, [ph.sb(f"stage{i}", [P, 2 * S]) for i in range(2)], parts=2)
        w1v = w1.rearrange("(c p) n -> p c n", p=P)
        w2v = w2.rearrange("(j p) n -> p j n", p=P)
        for j in range(JT):
            wt.chunks.append(([w1v[:, :, j * P:(j + 1) * P], w2v[:, j, :]], Wh[:, j, :], Wl[:, j, :], 1.0))
        T_bank, f1_bank, acc = ph.banks("T", 2), ph.banks("f1", 2), ph.banks("acc", 4)
        e_f1 = ph.events("f1", JT)
        e_g = ph.events("g", JT)
        e_gh = ph.events("gh", JT)
        e_gl = ph.events("gl", JT)
        e_f2 = ph.events("f2", JT - 1)
        e_acc = ph.events("acc", TT)
        FIRST = 4

        block = ctx.enter_context(nc.Block())

        @block.sync
        def _(sp):
            def pro():
                for t in range(TT):
                    x.full[t].up(sp.dma_start(x.xs[:, t, :], x_old[0, t]))
                load_weights(sp, wt, 0, FIRST)
                x.bias_in.up(sp.dma_start(x.bias[:, :], b2_row.partition_broadcast(P)))

            def body(b, par, last):
                if not last:
                    if static(b, 0):
                        x.e_tr.wait(sp, 0, KT - 1)
                    for t in range(TT):
                        x.stored[t].wait(sp, b - 1, 0, ph.passed)
                        x.full[t].up(sp.dma_start(x.xs[:, t, :], x_old[b + 1, t]))
                if static(b, 0):
                    load_weights(sp, wt, FIRST, JT)
                x.e_tr.wait(sp, b if last else b + 1, KT - 1, ph.passed)
                for t in range(TT):
                    x.full[t].up(sp.dma_start(x.xs[:, t, :], x_old[b, t]))
                for t in range(TT):
                    x.e_res.wait(sp, b, t, ph.passed)
                    x.stored[t].up(sp.dma_start(x_new[b, t], x.xs[:, t, :]))
            pairs(sp, pro, body)
            for t in range(TT):
                x.stored[t].wait(sp, B - 1, 0)

        @block.tensor
        def _(pe):
            def T(n, c):
                x.e_xn.wait(pe, n, TT - 1)
                x.e_hf.wait(pe, n, c - 2)
                x.e_tr.up(ln_transpose(nc, x, T_bank[c % 2], c, cst.ident[:, :]))

            def F1(b, par, j):
                if static(b, 0):
                    wt.lo.wait(pe, j, 0)
                if j == 0:
                    x.e_hl.wait(pe, b, KT - 1)
                e_g.wait(pe, b, j - 2)
                for c in range(KT):
                    w = slice(c * P, (c + 1) * P)
                    last = product(nc, f1_bank[j % 2][:, :], Wh[:, j, w], Wl[:, j, w],
                                   x.hTh[:, par, c, :], x.hTl[:, par, c, :], c == 0, c == KT - 1)
                e_f1.up(last)

            def F2(b, j):
                e_gl.wait(pe, b, j)
                for t in range(TT):
                    if j == 0:
                        x.e_res.wait(pe, b, t - TT)
                    ts = slice(t * P, (t + 1) * P)
                    last = product(nc, acc[t][:, :], gh[:, j % 2, ts], gl[:, j % 2, ts], Wh[:, j, S:2 * S],
                                   Wl[:, j, S:2 * S], j == 0, j == JT - 1)
                    if j == JT - 1:
                        e_acc.up(last)
                if j < JT - 1:
                    e_f2.up(last)

            def pro():
                cst.wait_ident(pe)
                for c in range(KT):
                    T(0, c)
                F1(0, 0, 0)

            def body(b, par, last):
                for j in range(1, JT):
                    F1(b, par, j)
                    F2(b, j - 1)
                    if 8 <= j < 12 and not last:
                        T(b + 1, j - 8)
                if not last:
                    F1(b + 1, 1 - par, 0)
                F2(b, JT - 1)
            pairs(pe, pro, body)

        @block.scalar
        def _(act):
            def gelu(b, j):
                e_f1.wait(act, b, j)
                e_gl.wait(act, b, j - 2)
                e_g.up(nc.scalar.activation(gf[:, j % 2, :], f1_bank[j % 2][:, :], ACT.Gelu, bias=b1[:, j:j + 1]))
                e_g.wait(act, b, j)
                if j == 0:
                    e_f2.wait(act, b, -1)
                elif j == 1:
                    e_acc.wait(act, b, -1)
                else:
                    e_f2.wait(act, b, j - 2)
                e_gh.up(nc.scalar.activation(gh[:, j % 2, :], gf[:, j % 2, :], ACT.Copy))

            def weights_hi(i):
                wt.full[i % wt.ns].wait(act, i // wt.ns, 0)
                wt.hi.up(weight_hi(nc, wt, i))

            def whole(n, c):
                x.e_tr.wait(act, n, c)
                x.e_hl.wait(act, n, c - x.temps)
                x.e_hf.up(ln_whole(nc, x, T_bank[c % 2], c))

            def pro():
                cst.wait_cols(act)
                weights_hi(0)
                for c in range(KT):
                    whole(0, c)
                weights_hi(1)
                gelu(0, 0)

            def body(b, par, last):
                for j in range(1, JT):
                    if static(b, 0) and j + 1 < JT:
                        weights_hi(j + 1)
                    gelu(b, j)
                    if 8 <= j < 12 and not last:
                        whole(b + 1, j - 8)
                if not last:
                    gelu(b + 1, 0)
            pairs(act, pro, body)

        @block.vector
        def _(dve):
            def lo(b, j):
                e_gh.wait(dve, b, j)
                e_gl.up(nc.vector.tensor_tensor(gl[:, j % 2, :], gf[:, j % 2, :], f32(gh[:, j % 2, :]), ALU.subtract))

            def weights_lo(i):
                wt.hi.wait(dve, i, 0)
                wt.lo.up(weight_lo(nc, wt, i))

            def stat(n, t):
                x.full[t].wait(dve, n, 0 if static(n, 0) else -1)
                x.e_st.up(ln_stats(nc, x, t))

            def aggregate(n):
                for t in range(TT):
                    x.e_st.wait(dve, n, t, ph.passed)
                    x.e_mv.up(ln_mean(nc, x, t))

            def normalise(n):
                x.e_rs.wait(dve, n, 0)
                for t in range(TT):
                    x.e_xn.up(ln_normalise(nc, x, t))

            def hi(n, c, par):
                x.e_hf.wait(dve, n, c)
                x.e_hh.up(ln_hi(nc, x, c, par))

            def pro():
                cst.wait_cols(dve)
                for t in range(TT):
                    stat(0, t)
                aggregate(0)
                normalise(0)
                weights_lo(0)
                for c in range(KT):
                    hi(0, c, 0)
                weights_lo(1)
                lo(0, 0)

            def body(b, par, last):
                for j in range(1, JT):
                    if static(b, 0) and j + 1 < JT:
                        weights_lo(j + 1)
                    lo(b, j)
                    if not last:
                        if 1 <= j < 5:
                            stat(b + 1, j - 1)
                        if j == 5:
                            aggregate(b + 1)
                        if j == 6:
                            normalise(b + 1)
                        if 8 <= j < 12:
                            hi(b + 1, j - 8, 1 - par)
                if not last:
                    lo(b + 1, 0)
                for t in range(TT):
                    x.e_xb.wait(dve, b, t)
                    e_acc.wait(dve, b, t)
                    x.e_res.up(add_out(nc, x, acc[t], t))
            pairs(dve, pro, body)

        @block.gpsimd
        def _(pool):
            def layer_norm(n, par):
                x.e_mv.wait(pool, n, TT - 1, ph.passed)
                x.e_ve.up(ln_eps(nc, x))
                x.e_power.wait(pool, 0, 0)
                x.e_ve.wait(pool, n, 0)
                x.e_rs.up(ln_rsqrt(nc, x))
                for c in range(KT):
                    x.e_hh.wait(pool, n, c)
                    x.e_hl.up(ln_lo(nc, x, c, par))

            def pro():
                x.e_power.up(ln_power(nc, x))
                layer_norm(0, 0)

            def body(b, par, last):
                if not last:
                    layer_norm(b + 1, 1 - par)
                if static(b, 0):
                    x.bias_in.wait(pool, 0, 0)
                for t in range(TT):
                    x.full[t].wait(pool, b, 1 if last else 2)
                    x.e_xb.up(add_bias(nc, x, t))
            pairs(pool, pro, body)


def self_attention(nc, name, cst, x_in, x_out, ln_w, ln_b, wq, bq, wk, bk, wv, bv, wo, bo_row):
    with ExitStack() as ctx:
        ph = Phase(nc, ctx, name)
        W = {n: (ph.sb(f"{n}h", [P, KT, D], F32R), ph.sb(f"{n}l", [P, KT, D], F32R)) for n in ("wq", "wk", "wv", "wo")}
        stack = {n: ph.sb(f"stack_{n}", [P, 2, 4, S], F32R) for n in "qk"}
        parts = {n: ph.sb(f"parts_{n}", [P, 2, S], F32R) for n in "qk"}
        Vh, Vl = (ph.sb(n, [P, TT, D], F32R) for n in ("Vh", "Vl"))
        Vbh, Vbl = (ph.sb(n, [P, TT, 4, P], F32R) for n in ("Vbh", "Vbl"))
        Pr = ph.sb("Pr", [P, 2, TT, S])
        PTh, PTl = (ph.sb(n, [P, 2, S], F32R) for n in ("PTh", "PTl"))
        nmax, rsum, rinv = (ph.sb(n, [P, 2, TT]) for n in ("nmax", "rsum", "rinv"))
        bqs = ph.sb("bqs", [P, KT])
        oTh, oTl = ph.sb("oTh", [P, G, S], F32R), ph.sb("oTl", [P, G, S], F32R)
        x = token_buffers(ph, ln_w, ln_b)
        x_old, x_new = token_tiles(x_in), token_tiles(x_out)
        wt = weight_staging(ph, [flat(Pr[:, i // 2, 2 * (i % 2):2 * (i % 2) + 2, :]) for i in range(4)])
        for n, w, scale in (("wq", wq, SCALE), ("wk", wk, 1.0), ("wv", wv, 1.0), ("wo", wo, 1.0)):
            add_matrix(wt, w, *W[n], scale)
        QK_CHUNKS, V_CHUNKS, CHUNKS = 4, 6, 8
        TILES = H * TT
        pj, s_bank, t_bank, o_bank = ph.banks("pj", 2), ph.banks("s", 3), ph.banks("t", 2), ph.banks("o", 1)[0]

        e_zero = ph.events("v_zero", 2)
        e_bqs = ph.events("bqs_set")
        e_v = ph.events("v", TT)
        e_vh, e_vl = ph.events("vh", TT), ph.events("vl", TT)
        e_vb = ph.events("vb", 2 * H)
        e_qk = ph.events("qk", 2 * G)
        e_qkh, e_qkl = ph.events("qkh", 2 * G), ph.events("qkl", 2 * G)
        e_stack = {n: ph.events(f"stack_{n}", G, 16 * 8) for n in "qk"}
        e_s = ph.events("s", TILES)
        e_mx = ph.events("mx", TILES)
        e_ex = ph.events("ex", TILES)
        e_ri = ph.events("ri", TILES // 2)
        e_pn = ph.events("pn", TILES)
        e_tp = ph.events("tp", TILES)
        e_ph, e_pl = ph.events("ph", TILES), ph.events("pl", TILES)
        e_pv = ph.events("pv", TILES)
        e_oh, e_ol = ph.events("oh", G), ph.events("ol", G)
        e_out = ph.events("out", TT)

        LEAD, LAG, S_BANKS = 6, 2, 3

        def s_before(s):
            return s - S_BANKS if s >= S_BANKS else (-1, -3, -2)[s]

        JOBS = [(("qk", 0, 1, 0), [0, 1, 2, 2]), (("qk", 0, 1, 1), [2, 2, 3, 4]),
                (("O", -1, 0), [5, 6, 6, 7]), (("O", -1, 1), [7, 8, 8, 9]),
                (("O", -1, 2), [10, 10, 11, 12]), (("O", -1, 3), [12, 13, 13, 14]),
                (("qk", 0, 2, 0), [15, 15, 16, 17]), (("qk", 0, 2, 1), [18, 18, 18, 18]),
                (("qk", 0, 3, 0), [24, 25, 26, 27]), (("qk", 0, 3, 1), [34, 34, 34, 34]),
                (("T", 1, 0), [35]), (("T", 1, 1), [37]), (("T", 1, 2), [39]), (("T", 1, 3), [41]),
                (("qk", 1, 0, 0), [45, 46, 47, 47]), (("qk", 1, 0, 1), [48, 48, 49, 49]),
                (("V", 1, 0), [50, 50, 50, 50]), (("V", 1, 1), [51, 52, 53, 54]),
                (("V", 1, 2), [55, 56, 56, 57]), (("V", 1, 3), [58, 59, 59, 60])]

        def jobs(b, v, actions):
            for (kind, ahead, *which), steps in JOBS:
                if steps[-1] == v and kind in actions and exists(b + ahead):
                    actions[kind](b + ahead, *which)

        def tile(b, s):
            return (b, s) if s < TILES else (b + 1, s - TILES)

        block = ctx.enter_context(nc.Block())

        @block.sync
        def _(sp):
            def stacks(b, g):
                for i, n in enumerate("qk"):
                    e_qkl.wait(sp, b, 2 * g + i, ph.passed)
                    e_s.wait(sp, b, 4 * (g - 1) * TT - 1, ph.passed)
                    for j in range(4):
                        src = f32(parts[n][32 * j:32 * j + 32, :, :])
                        for half in range(2):
                            rows = src if n == "k" else src[:, half:half + 1, :].broadcast_to([HD, 2, S])
                            sp.dma_start(f32(stack[n][64 * half:64 * half + 64, g % 2, j, :]), rows)\
                              .then_inc(e_stack[n].sem, 16)

            def store(b):
                for t in range(TT):
                    x.e_res.wait(sp, b, t, ph.passed)
                    x.stored[t].up(sp.dma_start(x_new[b, t], x.xs[:, t, :]))

            def pro():
                for t in range(TT):
                    x.full[t].up(sp.dma_start(x.xs[:, t, :], x_old[0, t]))
                load_weights(sp, wt, 0, CHUNKS)
                x.bias_in.up(sp.dma_start(x.bias[:, :], bo_row.partition_broadcast(P)))
                stacks(0, 0)

            def body(b, last):
                stacks(b, 1)
                if static(b, 0):
                    x.e_tr.wait(sp, 0, KT - 1)
                else:
                    store(b - 1)
                if not last:
                    for t in range(TT):
                        x.stored[t].wait(sp, b - 1, 0, ph.passed)
                        x.full[t].up(sp.dma_start(x.xs[:, t, :], x_old[b + 1, t]))
                stacks(b, 2)
                stacks(b, 3)
                if last:
                    for t in range(TT):
                        x.stored[t].wait(sp, b - 1, 0)
                        x.full[t].up(sp.dma_start(x.xs[:, t, :], x_old[b, t]))
                    store(b)
                else:
                    x.e_tr.wait(sp, b + 1, KT - 1, ph.passed)
                    for t in range(TT):
                        x.full[t].up(sp.dma_start(x.xs[:, t, :], x_old[b, t]))
                    stacks(b + 1, 0)
            run(sp, pro, body)
            for t in range(TT):
                x.stored[t].wait(sp, B - 1, 0)

        @block.tensor
        def _(pe):
            def T(n, c, _=0):
                x.e_xn.wait(pe, n, TT - 1)
                if c < 2:
                    e_qkl.wait(pe, n, c - 2)
                else:
                    x.e_hf.wait(pe, n, c - 2)
                x.e_tr.up(ln_transpose(nc, x, pj[c % 2], c, cst.ident[:, :]))

            def qk(b, g, i, c):
                if c:
                    pass
                elif g == 0:
                    x.e_hl.wait(pe, b, KT - 1)
                elif g == 1:
                    e_vl.wait(pe, b, 2 + i)
                elif g == 2 and not static(b, 0):
                    x.e_res.wait(pe, b - 1, 2 + i)
                else:
                    e_qkl.wait(pe, b, 2 * (g - 1) + i)
                wh, wl = W["w" + "qk"[i]]
                gs = slice(g * P, (g + 1) * P)
                last = product(nc, pj[i][:, :], wh[:, c, gs], wl[:, c, gs], x.hTh[:, 0, c, :], x.hTl[:, 0, c, :],
                               c == 0, c == KT - 1)
                if c == KT - 1:
                    e_qk.up(last)

            def V(b, t, c):
                if c:
                    pass
                elif t < 2:
                    e_qkl.wait(pe, b, t)
                else:
                    e_vl.wait(pe, b, t - 2)
                ts = slice(t * P, (t + 1) * P)
                wh, wl = W["wv"]
                last = product(nc, pj[t % 2][:, :], x.hTh[:, 0, c, ts], x.hTl[:, 0, c, ts], wh[:, c, :], wl[:, c, :],
                               c == 0, c == KT - 1)
                if c == KT - 1:
                    e_v.up(last)

            def scores(b, s):
                h, qt = s // TT, s % TT
                g, j = h // 4, h % 4
                if qt == 0 and j == 0:
                    for n in "qk":
                        e_stack[n].wait(pe, b, g)
                e_ex.wait(pe, b, s_before(s))
                e_s.up(nc.tensor.matmul(s_bank[s % S_BANKS][:, :], stack["q"][:, g % 2, j, qt * P:(qt + 1) * P],
                                        stack["k"][:, g % 2, j, :], start=True, stop=True))

            def P_transposed(b, v):
                h, pair, kp = v // 4, v // 2 % 2, v % 2
                if kp == 0:
                    e_pn.wait(pe, b, v + 1)
                e_pl.wait(pe, b, v - 2)
                for k in range(2):
                    for q in range(2):
                        kt, qt = 2 * kp + k, 2 * pair + q
                        last = nc.tensor.transpose(t_bank[v % 2][:, (2 * k + q) * P:(2 * k + q + 1) * P],
                                                   Pr[:, h % 2, qt, kt * P:(kt + 1) * P], cst.ident[:, :])
                e_tp.up(last)

            def PV(b, v):
                h, pair, kp = v // 4, v // 2 % 2, v % 2
                g, j = h // 4, h % 4
                if v % 16 == 0:
                    e_ol.wait(pe, b, g - 1)
                for k in range(2):
                    kt, cols = 2 * kp + k, slice(2 * k * P, 2 * (k + 1) * P)
                    last = product(nc, o_bank[:, 2 * pair * P:2 * (pair + 1) * P], Vbh[:, kt, j, :], Vbl[:, kt, j, :],
                                   PTh[:, v % 2, cols], PTl[:, v % 2, cols], v % 16 == 0 and k == 0,
                                   v % 16 == 15 and k == 1)
                e_pv.up(last)

            def O(b, t, c):
                if t == 0 and c == 0:
                    e_ol.wait(pe, b, G - 1)
                if c:
                    pass
                elif t >= 2:
                    x.e_res.wait(pe, b, t - 2)
                elif static(b, B - 1):
                    e_qkl.wait(pe, b, 6 + t)
                else:
                    e_qkl.wait(pe, b + 1, 2 + t)
                ts = slice(t * P, (t + 1) * P)
                wh, wl = W["wo"]
                last = product(nc, pj[t % 2][:, :], oTh[:, c, ts], oTl[:, c, ts], wh[:, c, :], wl[:, c, :],
                               c == 0, c == KT - 1)
                if c == KT - 1:
                    e_out.up(last)

            def pro():
                cst.wait_ident(pe)
                for c in range(KT):
                    T(0, c)
                wt.lo.wait(pe, QK_CHUNKS - 1, 0)
                for i in range(2):
                    for c in range(KT):
                        qk(0, 0, i, c)
                wt.lo.wait(pe, V_CHUNKS - 1, 0)
                for t in range(TT):
                    for c in range(KT):
                        V(0, t, c)
                for s in range(LEAD):
                    scores(0, s)
                wt.lo.wait(pe, CHUNKS - 1, 0)

            def body(b, last):
                for v in range(TILES):
                    for (kind, ahead, *which), steps in JOBS:
                        for c in range(len(steps)):
                            if steps[c] == v and exists(b + ahead):
                                {"qk": qk, "O": O, "T": T, "V": V}[kind](b + ahead, *which, c)
                    ahead = not (last and v + LEAD >= TILES)
                    if ahead and v + LEAD != TILES:
                        scores(*tile(b, v + LEAD))
                    P_transposed(b, v)
                    if v >= LAG:
                        PV(b, v - LAG)
                    elif not static(b, 0):
                        PV(b - 1, v - LAG + TILES)
                    if ahead and v + LEAD == TILES:
                        scores(b + 1, 0)
                if last:
                    for v in range(TILES - LAG, TILES):
                        e_pl.wait(pe, b, v)
                        PV(b, v)
                    for t in range(TT):
                        for c in range(KT):
                            O(b, t, c)
            run(pe, pro, body)

        @block.scalar
        def _(act):
            def qk_hi(b, g, i):
                e_qk.wait(act, b, 2 * g + i)
                e_stack["qk"[i]].wait(act, b, g - 1)
                e_qkh.up(add_hi(nc, parts["qk"[i]][:, 0, :], pj[i][:, :], (bqs if i == 0 else bk)[:, g:g + 1]))

            def v_hi(b, t):
                e_v.wait(act, b, t)
                e_vb.wait(act, b, -1)
                e_vh.up(add_hi(nc, Vh[:, t, :], pj[t % 2][:, :], None))

            def exp(b, s):
                h, qt = s // TT, s % TT
                e_mx.wait(act, b, s)
                e_tp.wait(act, b, (s - 8) // 2 * 2 + 1)
                e_ex.up(nc.scalar.activation(Pr[:, h % 2, qt, :], s_bank[s % S_BANKS][:, :], ACT.Exp,
                                             bias=nmax[:, h % 2, qt:qt + 1], accum_out=rsum[:, h % 2, qt:qt + 1]))

            def p_hi(b, v):
                e_tp.wait(act, b, v)
                e_pv.wait(act, b, v - 2)
                e_ph.up(add_hi(nc, PTh[:, v % 2, :], t_bank[v % 2][:, :], None))

            def o_hi(b, g):
                e_pv.wait(act, b, (4 * g + 4) * TT - 1)
                e_out.wait(act, b, -1)
                e_oh.up(add_hi(nc, oTh[:, g, :], o_bank[:, :], bv[:, g:g + 1]))

            def whole(n, c):
                x.e_tr.wait(act, n, c)
                x.e_hl.wait(act, n, c - x.temps)
                x.e_hf.up(ln_whole(nc, x, pj[c % 2], c))

            def weights_hi(first, end):
                for i in range(first, end):
                    wt.full[i % wt.ns].wait(act, i // wt.ns, 0)
                    wt.hi.up(weight_hi(nc, wt, i))

            def pro():
                cst.wait_cols(act)
                weights_hi(0, QK_CHUNKS)
                for c in range(KT):
                    whole(0, c)
                e_bqs.wait(act, 0, 0)
                for i in range(2):
                    qk_hi(0, 0, i)
                weights_hi(QK_CHUNKS, CHUNKS)
                for t in range(TT):
                    v_hi(0, t)
                for s in range(LEAD):
                    exp(0, s)

            def body(b, last):
                for v in range(TILES):
                    if v == LAG and not static(b, 0):
                        o_hi(b - 1, G - 1)
                    elif v % 16 == LAG and v > LAG:
                        o_hi(b, v // 16 - 1)
                    jobs(b, v, {"qk": qk_hi, "T": whole, "V": v_hi})
                    p_hi(b, v)
                    if not (last and v + LEAD >= TILES):
                        exp(*tile(b, v + LEAD))
                if last:
                    o_hi(b, G - 1)
            run(act, pro, body)

        @block.vector
        def _(dve):
            def qk_lo(b, g, i):
                e_qkh.wait(dve, b, 2 * g + i)
                n = "qk"[i]
                e_qkl.up(add_lo(nc, parts[n][:, 1, :], parts[n][:, 0, :], pj[i][:, :],
                                (bqs if i == 0 else bk)[:, g:g + 1]))

            def v_lo(b, t):
                e_vh.wait(dve, b, t)
                e_vl.up(add_lo(nc, Vl[:, t, :], Vh[:, t, :], pj[t % 2][:, :], None))

            def maximum(b, s):
                h, qt = s // TT, s % TT
                e_s.wait(dve, b, s)
                e_mx.up(nc.vector.reduce_max(nmax[:, h % 2, qt:qt + 1], s_bank[s % S_BANKS][:, :], AX.X, negate=True))

            def inverse(b, s):
                h, qt = s // TT, s % TT
                if s % 2:
                    e_ex.wait(dve, b, s)
                    e_ri.up(nc.vector.reciprocal(rinv[:, h % 2, qt - 1:qt + 1], rsum[:, h % 2, qt - 1:qt + 1]))

            def p_lo(b, v):
                e_ph.wait(dve, b, v)
                e_pl.up(add_lo(nc, PTl[:, v % 2, :], PTh[:, v % 2, :], t_bank[v % 2][:, :], None))

            def o_lo(b, g):
                e_oh.wait(dve, b, g)
                e_ol.up(add_lo(nc, oTl[:, g, :], oTh[:, g, :], o_bank[:, :], bv[:, g:g + 1]))

            def stat(n, t):
                x.full[t].wait(dve, n, 0 if static(n, 0) else -1)
                x.e_st.up(ln_stats(nc, x, t))

            def aggregate(n):
                for t in range(TT):
                    x.e_st.wait(dve, n, t, ph.passed)
                    x.e_mv.up(ln_mean(nc, x, t))

            def normalise(n, t):
                x.e_rs.wait(dve, n, 0)
                x.e_xn.up(ln_normalise(nc, x, t))

            def hi(n, c):
                x.e_hf.wait(dve, n, c)
                x.e_hh.up(ln_hi(nc, x, c))

            def weights_lo(first, end):
                for i in range(first, end):
                    wt.hi.wait(dve, i, 0)
                    wt.lo.up(weight_lo(nc, wt, i))

            def add_output(b, t):
                x.e_xb.wait(dve, b, t)
                e_out.wait(dve, b, t)
                x.e_res.up(add_out(nc, x, pj[t % 2], t))

            def pro():
                cst.wait_cols(dve)
                e_bqs.up(nc.vector.tensor_scalar(bqs[:, :], bq, SCALE, None, ALU.mult))
                for t in range(TT):
                    stat(0, t)
                aggregate(0)
                for t in range(TT):
                    normalise(0, t)
                weights_lo(0, QK_CHUNKS)
                for c in range(KT):
                    hi(0, c)
                e_bqs.wait(dve, 0, 0)
                for i in range(2):
                    qk_lo(0, 0, i)
                weights_lo(QK_CHUNKS, CHUNKS)
                for t in range(TT):
                    v_lo(0, t)
                for s in range(LEAD):
                    maximum(0, s)
                    if s:
                        inverse(0, s - 1)

            def body(b, last):
                for v in range(TILES):
                    if v == LAG and not static(b, 0):
                        o_lo(b - 1, G - 1)
                    elif v % 16 == LAG and v > LAG:
                        o_lo(b, v // 16 - 1)
                    jobs(b, v, {"qk": qk_lo, "O": add_output, "T": hi, "V": v_lo})
                    ahead = not (last and v + LEAD >= TILES)
                    if ahead and v + LEAD != TILES:
                        maximum(*tile(b, v + LEAD))
                    p_lo(b, v)
                    if ahead and v + LEAD == TILES:
                        maximum(b + 1, 0)
                    if not (last and v + LEAD - 1 >= TILES):
                        inverse(*tile(b, v + LEAD - 1))
                    if not last:
                        if 21 <= v < 25:
                            stat(b + 1, v - 21)
                        if v == 26:
                            aggregate(b + 1)
                        if 29 <= v < 33:
                            normalise(b + 1, v - 29)
                if last:
                    o_lo(b, G - 1)
                    for t in range(TT):
                        add_output(b, t)
            run(dve, pro, body)

        @block.gpsimd
        def _(pool):
            def normal(b, s):
                h, qt = s // TT, s % TT
                if s % 2 == 0:
                    e_ri.wait(pool, b, s // 2, ph.passed)
                p = Pr[:, h % 2, qt, :]
                e_pn.up(nc.gpsimd.tensor_scalar(p, p, rinv[:, h % 2, qt:qt + 1], 0.0, ALU.mult, ALU.add))

            def lo(n, c):
                x.e_hh.wait(pool, n, c)
                x.e_hl.up(ln_lo(nc, x, c))

            def place_v(b, h):
                j = h % 4
                e_pv.wait(pool, b, (h - 4) * TT + TT - 1, ph.passed)
                if h == 0:
                    e_vl.wait(pool, b, TT - 1, ph.passed)
                for dst, src in ((Vbh, Vh), (Vbl, Vl)):
                    e_vb.up(nc.gpsimd.tensor_copy(dst[:, :, j, HD * j:HD * (j + 1)],
                                                  f32(src[:, :, HD * h:HD * (h + 1)])))

            def pro():
                x.e_power.up(ln_power(nc, x))
                x.e_mv.wait(pool, 0, TT - 1)
                x.e_ve.up(ln_eps(nc, x))
                x.e_power.wait(pool, 0, 0)
                x.e_ve.wait(pool, 0, 0)
                x.e_rs.up(ln_rsqrt(nc, x))
                for z in (Vbh, Vbl):
                    e_zero.up(nc.gpsimd.memset(f32(z[:, :, :, :]), 0.0))
                for c in range(KT):
                    x.e_hh.wait(pool, 0, c)
                    x.e_hl.up(ln_lo(nc, x, c))
                x.bias_in.wait(pool, 0, 0)
                e_zero.wait(pool, 0, 1)
                for h in range(3):
                    place_v(0, h)
                for s in range(LEAD - 2):
                    normal(0, s)

            def body(b, last):
                for v in range(TILES):
                    if v % 4 == 2 and v // 4 + 3 < H:
                        place_v(b, v // 4 + 3)
                    if not (last and v + LEAD - 2 >= TILES):
                        normal(*tile(b, v + LEAD - 2))
                    if not last:
                        if v == 26:
                            x.e_mv.wait(pool, b + 1, TT - 1, ph.passed)
                            x.e_ve.up(ln_eps(nc, x))
                            x.e_ve.wait(pool, b + 1, 0)
                            x.e_rs.up(ln_rsqrt(nc, x))
                        jobs(b, v - 1, {"T": lo})
                        if v >= TILES - 3:
                            place_v(b + 1, v - (TILES - 3))
                    if v in (48, 50, 52, 54):
                        x.full[(v - 48) // 2].wait(pool, b, 1 if last else 2)
                        x.e_xb.up(add_bias(nc, x, (v - 48) // 2))
            run(pool, pro, body)


def context_kv(nc, name, cst, ctx_in, ln, wk, bk, wv, Kh, Kl, V, later):
    with ExitStack() as ctx:
        ph = Phase(nc, ctx, name)
        N = B * L
        x = ph.sb("x", [L, B, CTX])
        cTh, cTl = ph.sb("cTh", [P, CT, N], F32R), ph.sb("cTl", [P, CT, N], F32R)
        tmp = ph.sb("tmp", [P, 2, GL])
        W = [(ph.sb(f"w{n}h", [P, CT, D], F32R), ph.sb(f"w{n}l", [P, CT, D], F32R)) for n in "kv"]
        wt = weight_staging(ph, [ph.sb(f"stage{i}", [P, CT * D]) for i in range(2)])
        for (wh, wl), w in zip(W, (wk, wv)):
            add_matrix(wt, w, wh, wl, rows=CT)
        stats, mv, ve, rs, power = (ph.sb(n, [L, B, k]) for n, k in
                                    (("stats", 6), ("mv", 2), ("ve", 1), ("rs", 1), ("power", 1)))
        banks = ph.banks("bank", 8)
        e_x = ph.events("x", 1, 16)
        e_st, e_mv, e_ve, e_rs, e_pw = (ph.events(n) for n in ("st", "mv", "ve", "rs", "pw"))
        e_xn = ph.events("xn")
        e_t = ph.events("t")
        e_hf = ph.events("hf")
        e_hh = ph.events("hh")
        e_hl = ph.events("hl")
        e_k = ph.events("k")
        e_kh, e_kc = ph.events("kh"), ph.events("kc")
        e_v, e_vc = ph.events("v"), ph.events("vc")
        tiles = [(half, c) for half in range(2) for c in range(CT)]
        keys = [(g, half) for g in range(G) for half in range(2)]
        NT, NK = len(tiles), len(keys)
        block = ctx.enter_context(nc.Block())

        @block.sync
        def _(sp):
            e_x.up(sp.dma_start(x[:, :, :], ctx_in.rearrange("b l d -> l b d")))
            load_weights(sp, wt, 0, 2)
            load_weights(sp, later, 0, len(later.chunks))

        @block.vector
        def _(dve):
            cst.wait_cols(dve)
            e_x.wait(dve, 0, 0)
            if ln:
                for b in range(B):
                    e_st.up(nc.vector.bn_stats(stats[:, b, :], x[:, b, :]))
                for b in range(B):
                    e_st.wait(dve, b, 0)
                    e_mv.up(nc.vector.bn_aggr(mv[:, b, :], stats[:, b, :]))
                e_rs.wait(dve, 0, 0)
                for b in range(B):
                    e_xn.up(nc.vector.tensor_scalar(x[:, b, :], x[:, b, :], mv[:, b, 0:1], rs[:, b, :],
                                                    ALU.subtract, ALU.mult))
            wt.hi.wait(dve, 0, 0)
            wt.lo.up(weight_lo(nc, wt, 0))
            for u, (half, c) in enumerate(tiles):
                lo, hi = cTl[:, c, half * GL:(half + 1) * GL], cTh[:, c, half * GL:(half + 1) * GL]
                if ln:
                    e_t.wait(dve, u, 0)
                    e_hl.wait(dve, u - 2, 0)
                    e_hf.up(nc.vector.tensor_scalar(tmp[:, u % 2, :], banks[u][:, 0:GL], ln[0][:, c:c + 1],
                                                    ln[1][:, c:c + 1], ALU.mult, ALU.add))
                    e_hh.wait(dve, u, 0)
                    e_hl.up(nc.vector.tensor_tensor(lo, tmp[:, u % 2, :], f32(hi), ALU.subtract))
                else:
                    e_hh.wait(dve, u, 0)
                    e_hl.up(nc.vector.tensor_tensor(lo, banks[u][:, 0:GL], f32(hi), ALU.subtract))
            wt.hi.wait(dve, 1, 0)
            wt.lo.up(weight_lo(nc, wt, 1))
            for u, (g, half) in enumerate(keys):
                e_kh.wait(dve, u, 0)
                cols = slice(half * GL, (half + 1) * GL)
                e_kc.up(add_lo(nc, Kl[:, g, cols], Kh[:, g, cols], banks[(NT + u) % 8][:, 0:GL],
                               None if bk is None else bk[:, g:g + 1]))
                if u % 2:
                    later.hi.wait(dve, u // 2, 0)
                    later.lo.up(weight_lo(nc, later, u // 2))

        @block.gpsimd
        def _(pool):
            if ln:
                e_pw.up(nc.gpsimd.memset(power[:, :, :], -0.5))
                e_mv.wait(pool, B - 1, 0)
                e_ve.up(nc.gpsimd.tensor_scalar(ve[:, :, 0], mv[:, :, 1], EPS, 1.0, ALU.add, ALU.mult))
                e_ve.wait(pool, 0, 0)
                e_pw.wait(pool, 0, 0)
                e_rs.up(nc.gpsimd.tensor_tensor(rs[:, :, 0], ve[:, :, 0], power[:, :, 0], ALU.pow))

        @block.scalar
        def _(act):
            cst.wait_cols(act)
            wt.full[0].wait(act, 0, 0)
            wt.hi.up(weight_hi(nc, wt, 0))
            for u, (half, c) in enumerate(tiles):
                hi = cTh[:, c, half * GL:(half + 1) * GL]
                if ln:
                    e_hf.wait(act, u, 0)
                    e_hh.up(nc.scalar.activation(hi, tmp[:, u % 2, :], ACT.Copy))
                else:
                    e_t.wait(act, u, 0)
                    e_hh.up(nc.scalar.activation(hi, banks[u][:, 0:GL], ACT.Copy))
            wt.full[1].wait(act, 0, 0)
            wt.hi.up(weight_hi(nc, wt, 1))
            for u, (g, half) in enumerate(keys):
                e_k.wait(act, u, 0)
                e_kh.up(add_hi(nc, Kh[:, g, half * GL:(half + 1) * GL], banks[(NT + u) % 8][:, 0:GL],
                               None if bk is None else bk[:, g:g + 1]))
                if u % 2:
                    i = u // 2
                    later.full[i % later.ns].wait(act, i // later.ns, 0)
                    later.hi.up(weight_hi(nc, later, i))
            for b in range(B):
                e_v.wait(act, b, 0)
                e_vc.up(nc.scalar.activation(V[:, b, :], banks[(NT + NK + b) % 8][0:L, :], ACT.Copy))

        @block.tensor
        def _(pe):
            cst.wait_ident(pe)
            e_x.wait(pe, 0, 0)
            if ln:
                e_xn.wait(pe, B - 1, 0)
            for u, (half, c) in enumerate(tiles):
                for i in range(4):
                    last = nc.tensor.transpose(banks[u][:, i * L:(i + 1) * L], x[:, half * 4 + i, c * P:(c + 1) * P],
                                               cst.ident[0:L, 0:L])
                e_t.up(last)
            e_hl.wait(pe, NT - 1, 0)
            wt.lo.wait(pe, 1, 0)
            for u, (g, half) in enumerate(keys):
                gs, hs = slice(g * P, (g + 1) * P), slice(half * GL, (half + 1) * GL)
                for c in range(CT):
                    last = product(nc, banks[(NT + u) % 8][:, 0:GL], W[0][0][:, c, gs], W[0][1][:, c, gs],
                                   cTh[:, c, hs], cTl[:, c, hs], c == 0, c == CT - 1)
                e_k.up(last)
            for b in range(B):
                e_kc.wait(pe, b, 0)
                ls = slice(b * L, (b + 1) * L)
                for c in range(CT):
                    last = product(nc, banks[(NT + NK + b) % 8][0:L, :], cTh[:, c, ls], cTl[:, c, ls],
                                   W[1][0][:, c, :], W[1][1][:, c, :], c == 0, c == CT - 1)
                e_v.up(last)


def cross_attention(nc, name, cst, x_in, x_out, ctx_in, ln_w, ln_b, ctx_ln, wq, bq, wk, bk, wv, bv, wo, bo_row):
    with ExitStack() as ctx:
        ph = Phase(nc, ctx, name)
        Kh, Kl = (ph.sb(n, [P, G, B * L], F32R) for n in ("Kh", "Kl"))
        Vall = ph.sb("Vall", [L, B, D])
        W = {n: (ph.sb(f"{n}h", [P, KT, D], F32R), ph.sb(f"{n}l", [P, KT, D], F32R)) for n in ("wq", "wo")}
        stage = ph.sb("stage", [P, 2, 2 * D])
        wt = weight_staging(ph, [stage[:, i, :] for i in range(2)])
        add_matrix(wt, wq, *W["wq"], SCALE)
        add_matrix(wt, wo, *W["wo"])
        context_kv(nc, name + "_kv", cst, ctx_in, ctx_ln, wk, bk, wv, Kh, Kl, Vall, wt)

        Kbh, Kbl = (ph.sb(n, [P, 2, G, 4, L], F32R) for n in ("Kbh", "Kbl"))
        Vbh, Vbl = (ph.sb(n, [P, G, 4, P], F32R) for n in ("Vbh", "Vbl"))
        qTh, qTl = ph.sb("qTh", [P, G, S], F32R), ph.sb("qTl", [P, G, S], F32R)
        Pr = ph.sb("Pr", [P, G, TT, GL])
        PTh, PTl = (ph.sb(n, [L, 2, S], F32R) for n in ("PTh", "PTl"))
        nmax, rsum, rinv = (ph.sb(n, [P, G, TT, 4]) for n in ("nmax", "rsum", "rinv"))
        bqs = ph.sb("bqs", [P, KT])
        oTh, oTl = ph.sb("oTh", [P, G, S], F32R), ph.sb("oTl", [P, G, S], F32R)
        x = token_buffers(ph, ln_w, ln_b, residual=stage[:, :, :].rearrange("p a (b d) -> p (a b) d", b=2))
        x_old, x_new = token_tiles(x_in), token_tiles(x_out)
        TILES = G * TT
        pj, s_bank, t_bank, o_bank = ph.banks("pj", 2), ph.banks("s", 2), ph.banks("t", 2), ph.banks("o", 2)

        xr_full = [ph.events(f"xr_full{t}", 1, 16) for t in range(TT)]
        e_zero = ph.events("zero", 4)
        e_bqs = ph.events("bqs_set")
        e_kb = ph.events("kb", 1, 16 * 8)
        e_vb = ph.events("vb", 8)
        e_q = ph.events("q", G)
        e_qh, e_ql = ph.events("qh", G), ph.events("ql", G)
        e_s = ph.events("s", TILES)
        e_mx = ph.events("mx", TILES)
        e_ex = ph.events("ex", TILES)
        e_ri = ph.events("ri", TILES)
        e_pn = ph.events("pn", TILES)
        e_tp = ph.events("tp", H)
        e_ph, e_pl = ph.events("ph", H), ph.events("pl", H)
        e_pv = ph.events("pv", H)
        e_oh, e_ol = ph.events("oh", G), ph.events("ol", G)
        e_out = ph.events("out", TT)

        LEAD, LAG, S_BANKS = 6, 2, 2
        JOBS = [(("Q", 0, 3), [0, 0, 1, 1]), (("T", 1, 0), [2]), (("T", 1, 1), [3]),
                (("O", -1, 0), [4, 4, 4, 4]), (("T", 1, 2), [5]), (("O", -1, 1), [5, 5, 5, 5]), (("T", 1, 3), [6]),
                (("O", -1, 2), [6, 6, 6, 6]), (("O", -1, 3), [7, 7, 7, 7]),
                (("Q", 1, 0), [8, 8, 8, 8]), (("Q", 1, 1), [9, 10, 11, 11]), (("Q", 1, 2), [12, 13, 14, 15])]
        OUT = {2: (-1, 3), 8: (0, 0), 10: (0, 1), 14: (0, 2)}

        def jobs(b, v, actions):
            for (kind, ahead, which), steps in JOBS:
                if steps[-1] == v and kind in actions and exists(b + ahead):
                    actions[kind](b + ahead, which)

        def tile(b, s):
            return (b, s) if s < TILES else (b + 1, s - TILES)

        def has_tile(last, s):
            return s < TILES or not last

        block = ctx.enter_context(nc.Block())

        @block.sync
        def _(sp):
            def load(n, t):
                x.full[t].up(sp.dma_start(x.xs[:, t, :], x_old[n, t]))

            def load_again(b):
                for t in range(TT):
                    x.stored[t].wait(sp, b - 1, 0, ph.passed)
                    xr_full[t].up(sp.dma_start(x.xr[:, t, :], x_old[b, t]))

            def place_k(n, par):
                e_s.wait(sp, n - 2, TILES - 1, ph.passed)
                e_kb.wait(sp, n - 1, 0, ph.passed)
                for dst, src in ((Kbh, Kh), (Kbl, Kl)):
                    for j in range(4):
                        rows = slice(HD * j, HD * (j + 1))
                        sp.dma_start(f32(dst[rows, par, :, j, :]), f32(src[rows, :, bass.ds(n * L, L)]))\
                          .then_inc(e_kb.sem, 16)

            def store(b, tiles):
                for t in tiles:
                    x.e_res.wait(sp, b, t, ph.passed)
                    x.stored[t].up(sp.dma_start(x_new[b, t], x.xr[:, t, :]))

            def pro():
                for t in range(TT):
                    load(0, t)
                x.bias_in.up(sp.dma_start(x.bias[:, :], bo_row.partition_broadcast(P)))
                e_zero.wait(sp, 0, 3)
                place_k(0, 0)
                x.e_tr.wait(sp, 0, KT - 1)
                for t in range(TT):
                    load(1, t)
                load_again(0)
                place_k(1, 1)

            def body(b, par, last):
                if not static(b, 0):
                    store(b - 1, (0, 1))
                if exists(b + 2):
                    x.e_tr.wait(sp, b + 1, KT - 1, ph.passed)
                    for t in range(TT):
                        load(b + 2, t)
                if not static(b, 0):
                    store(b - 1, (2, 3))
                    load_again(b)
                if exists(b + 2):
                    place_k(b + 2, par)
            pairs(sp, pro, body)
            store(B - 1, range(TT))
            for t in range(TT):
                x.stored[t].wait(sp, B - 1, 0)

        @block.tensor
        def _(pe):
            def T(n, c, _=0):
                x.e_xn.wait(pe, n, TT - 1)
                if c < 2:
                    e_ql.wait(pe, n - 1, 2 + c)
                elif not (static(n, 0) or static(n, 1)):
                    x.e_res.wait(pe, n - 2, c - 2)
                else:
                    x.e_hf.wait(pe, n, c - 2)
                x.e_tr.up(ln_transpose(nc, x, pj[c % 2], c, cst.ident[:, :]))

            def Q(n, g, c):
                if c:
                    pass
                elif g < 2:
                    if not (static(n, 0) or static(n, 1)):
                        x.e_res.wait(pe, n - 2, 2 + g)
                    x.e_hl.wait(pe, n, KT - 1)
                else:
                    e_ql.wait(pe, n, g - 2)
                wh, wl = W["wq"]
                gs = slice(g * P, (g + 1) * P)
                last = product(nc, pj[g % 2][:, :], wh[:, c, gs], wl[:, c, gs], x.hTh[:, 0, c, :], x.hTl[:, 0, c, :],
                               c == 0, c == KT - 1)
                if c == KT - 1:
                    e_q.up(last)

            def scores(b, par, s):
                g, qt = s // TT, s % TT
                if qt == 0:
                    e_ql.wait(pe, b, g)
                if s == 0:
                    e_kb.wait(pe, b, 0)
                e_ex.wait(pe, b, s - S_BANKS)
                qs = slice(qt * P, (qt + 1) * P)
                kh, kl = (k[:, par, g, :, :].rearrange("p j l -> p (j l)") for k in (Kbh, Kbl))
                e_s.up(product(nc, s_bank[s % S_BANKS][:, 0:GL], qTh[:, g, qs], qTl[:, g, qs], kh, kl, True, True))

            def P_transposed(b, h):
                g, j = h // 4, h % 4
                if j == 0:
                    e_pn.wait(pe, b, g * TT + TT - 1)
                e_pl.wait(pe, b, h - 2)
                for qt in range(TT):
                    last = nc.tensor.transpose(t_bank[j % 2][0:L, qt * P:(qt + 1) * P],
                                               Pr[:, g, qt, j * L:(j + 1) * L], cst.ident[:, :])
                e_tp.up(last)

            def PV(b, h):
                g, j = h // 4, h % 4
                if j == 0:
                    e_ol.wait(pe, b, g - 2)
                    e_vb.wait(pe, b, 2 * g + 1)
                e_pl.wait(pe, b, h)
                e_pv.up(product(nc, o_bank[g % 2][:, :], Vbh[0:L, g, j, :], Vbl[0:L, g, j, :], PTh[:, j % 2, :],
                                PTl[:, j % 2, :], j == 0, j == 3))

            def O(b, t, c):
                if t == 0 and c == 0:
                    e_ol.wait(pe, b, G - 1)
                if c:
                    pass
                elif exists(b + 2):
                    x.e_hf.wait(pe, b + 2, t)
                elif t < 2 and exists(b + 1):
                    e_ql.wait(pe, b + 1, 2 + t)
                elif t < 2:
                    x.e_res.wait(pe, b - 1, 2 + t)
                else:
                    x.e_res.wait(pe, b, t - 2)
                ts = slice(t * P, (t + 1) * P)
                wh, wl = W["wo"]
                last = product(nc, pj[t % 2][:, :], oTh[:, c, ts], oTl[:, c, ts], wh[:, c, :], wl[:, c, :],
                               c == 0, c == KT - 1)
                if c == KT - 1:
                    e_out.up(last)

            def pro():
                for c in range(KT):
                    T(0, c)
                for g in range(3):
                    for c in range(KT):
                        Q(0, g, c)
                for s in range(LEAD):
                    scores(0, 0, s)

            def body(b, par, last):
                for v in range(H):
                    for (kind, ahead, which), steps in JOBS:
                        for c in range(len(steps)):
                            if steps[c] == v and exists(b + ahead):
                                {"Q": Q, "O": O, "T": T}[kind](b + ahead, which, c)
                    if has_tile(last, v + LEAD):
                        n, s = tile(b, v + LEAD)
                        scores(n, par if v + LEAD < TILES else 1 - par, s)
                    P_transposed(b, v)
                    if v >= LAG:
                        PV(b, v - LAG)
                    elif not static(b, 0):
                        PV(b - 1, v - LAG + H)
                if last:
                    for h in range(H - LAG, H):
                        PV(b, h)
                    for t in range(TT):
                        for c in range(KT):
                            O(b, t, c)
            pairs(pe, pro, body)

        @block.scalar
        def _(act):
            def q_hi(n, g):
                e_q.wait(act, n, g)
                e_qh.up(add_hi(nc, qTh[:, g, :], pj[g % 2][:, :], None if bq is None else bqs[:, g:g + 1]))

            def exp(b, s):
                g, qt = s // TT, s % TT
                e_mx.wait(act, b, s)
                e_tp.wait(act, b - 1, 4 * g + 3)
                for j in range(4):
                    keys = slice(j * L, (j + 1) * L)
                    last = nc.scalar.activation(Pr[:, g, qt, keys], s_bank[s % S_BANKS][:, keys], ACT.Exp,
                                                bias=nmax[:, g, qt, j:j + 1], accum_out=rsum[:, g, qt, j:j + 1])
                e_ex.up(last)

            def p_hi(b, h):
                e_tp.wait(act, b, h)
                e_pv.wait(act, b, h - 2)
                e_ph.up(add_hi(nc, PTh[:, h % 2, :], t_bank[h % 2][0:L, :], None))

            def o_hi(b, g):
                e_pv.wait(act, b, 4 * g + 3)
                e_out.wait(act, b, -1)
                e_oh.up(add_hi(nc, oTh[:, g, :], o_bank[g % 2][:, :], None if bv is None else bv[:, g:g + 1]))

            def whole(n, c):
                x.e_tr.wait(act, n, c)
                x.e_hl.wait(act, n, c - x.temps)
                x.e_hf.up(ln_whole(nc, x, pj[c % 2], c))

            def pro():
                for c in range(KT):
                    whole(0, c)
                if bq is not None:
                    e_bqs.wait(act, 0, 0)
                for g in range(3):
                    q_hi(0, g)
                for s in range(LEAD):
                    exp(0, s)

            def body(b, par, last):
                for v in range(H):
                    if v in OUT and exists(b + OUT[v][0]):
                        o_hi(b + OUT[v][0], OUT[v][1])
                    jobs(b, v, {"Q": q_hi, "T": whole})
                    p_hi(b, v)
                    if has_tile(last, v + LEAD):
                        exp(*tile(b, v + LEAD))
                if last:
                    o_hi(b, G - 1)
            pairs(act, pro, body)

        @block.vector
        def _(dve):
            def q_lo(n, g):
                e_qh.wait(dve, n, g)
                e_ql.up(add_lo(nc, qTl[:, g, :], qTh[:, g, :], pj[g % 2][:, :],
                               None if bq is None else bqs[:, g:g + 1]))

            def maximum(b, s):
                e_s.wait(dve, b, s)
                e_mx.up(nc.vector.reduce_max(nmax[:, s // TT, s % TT, :], s_bank[s % S_BANKS][:, 0:GL]
                                             .rearrange("p (j l) -> p j l", j=4), AX.X, negate=True))

            def inverse(b, s):
                e_ex.wait(dve, b, s)
                e_ri.up(nc.vector.reciprocal(rinv[:, s // TT, s % TT, :], rsum[:, s // TT, s % TT, :]))

            def p_lo(b, h):
                e_ph.wait(dve, b, h)
                e_pl.up(add_lo(nc, PTl[:, h % 2, :], PTh[:, h % 2, :], t_bank[h % 2][0:L, :], None))

            def o_lo(b, g):
                e_oh.wait(dve, b, g)
                e_ol.up(add_lo(nc, oTl[:, g, :], oTh[:, g, :], o_bank[g % 2][:, :],
                               None if bv is None else bv[:, g:g + 1]))

            def stat(n, t):
                x.full[t].wait(dve, n, 0)
                x.e_st.up(ln_stats(nc, x, t))

            def aggregate(n):
                for t in range(TT):
                    x.e_st.wait(dve, n, t, ph.passed)
                    x.e_mv.up(ln_mean(nc, x, t))

            def normalise(n, t):
                x.e_rs.wait(dve, n, 0)
                x.e_xn.up(ln_normalise(nc, x, t))

            def hi(n, c):
                x.e_hf.wait(dve, n, c)
                x.e_hh.up(ln_hi(nc, x, c))

            def add_output(b, t):
                x.e_xb.wait(dve, b, t)
                e_out.wait(dve, b, t)
                x.e_res.up(add_out(nc, x, pj[t % 2], t))

            def pro():
                if bq is not None:
                    e_bqs.up(nc.vector.tensor_scalar(bqs[:, :], bq, SCALE, None, ALU.mult))
                    e_bqs.wait(dve, 0, 0)
                for t in range(TT):
                    stat(0, t)
                aggregate(0)
                for t in range(TT):
                    normalise(0, t)
                for c in range(KT):
                    hi(0, c)
                for g in range(3):
                    q_lo(0, g)
                for s in range(LEAD):
                    maximum(0, s)
                    if s:
                        inverse(0, s - 1)
                for t in range(TT):
                    stat(1, t)
                aggregate(1)
                for t in range(TT):
                    normalise(1, t)

            def body(b, par, last):
                for v in range(H):
                    if v in OUT and exists(b + OUT[v][0]):
                        o_lo(b + OUT[v][0], OUT[v][1])
                    jobs(b, v, {"Q": q_lo, "O": add_output, "T": hi})
                    if has_tile(last, v + LEAD):
                        maximum(*tile(b, v + LEAD))
                    p_lo(b, v)
                    if has_tile(last, v + LEAD - 1):
                        inverse(*tile(b, v + LEAD - 1))
                    if exists(b + 2):
                        if 9 <= v < 13:
                            stat(b + 2, v - 9)
                        if v == 12:
                            aggregate(b + 2)
                        if v >= 14:
                            for t in range(2 * (v - 14), 2 * (v - 14) + 2):
                                normalise(b + 2, t)
                if last:
                    o_lo(b, G - 1)
                    for t in range(TT):
                        add_output(b, t)
            pairs(dve, pro, body)

        @block.gpsimd
        def _(pool):
            def place_v(n, g, before):
                src = Vall[:, n, P * g:P * (g + 1)].rearrange("p (j d) -> p j d", j=4)
                if before:
                    e_pn.wait(pool, *before, ph.passed)
                e_pv.wait(pool, n - 1, 4 * g + 3, ph.passed)
                e_vb.up(nc.gpsimd.tensor_copy(diagonal(Vbh[0:L, g, :, :]), src))
                e_vb.wait(pool, n, 2 * g, ph.passed)
                e_vb.up(nc.gpsimd.tensor_tensor(diagonal(Vbl[0:L, g, :, :]), src, f32(diagonal(Vbh[0:L, g, :, :])),
                                                ALU.subtract))
                e_vb.wait(pool, n, 2 * g + 1, ph.passed)

            def normal(b, s):
                e_ri.wait(pool, b, s, ph.passed)
                p = Pr[:, s // TT, s % TT, :].rearrange("p (j l) -> p j l", j=4)
                e_pn.up(nc.gpsimd.tensor_tensor(p, p, rinv[:, s // TT, s % TT, :].unsqueeze(2).broadcast_to([P, 4, L]),
                                                ALU.mult))

            def rsqrt(n):
                x.e_mv.wait(pool, n, TT - 1, ph.passed)
                x.e_ve.up(ln_eps(nc, x))
                x.e_ve.wait(pool, n, 0)
                x.e_rs.up(ln_rsqrt(nc, x))

            def lo(n, c):
                x.e_hh.wait(pool, n, c)
                x.e_hl.up(ln_lo(nc, x, c))

            def bias(b, t):
                xr_full[t].wait(pool, b, 0)
                x.e_xb.up(add_bias(nc, x, t))

            def pro():
                x.e_power.up(ln_power(nc, x))
                for z in (Kbh, Kbl):
                    e_zero.up(nc.gpsimd.memset(f32(z[:, :, :, :, :]), 0.0))
                for z in (Vbh, Vbl):
                    e_zero.up(nc.gpsimd.memset(f32(z[:, :, :, :]), 0.0))
                x.e_power.wait(pool, 0, 0)
                rsqrt(0)
                e_zero.wait(pool, 0, 3)
                x.e_rs.wait(pool, 0, 0)
                for g in range(3):
                    place_v(0, g, None)
                for c in range(KT):
                    lo(0, c)
                for s in range(LEAD - 1):
                    normal(0, s)
                rsqrt(1)
                x.bias_in.wait(pool, 0, 0)

            def body(b, par, last):
                for v in range(H):
                    before = None
                    if has_tile(last, v + LEAD - 1):
                        before = tile(b, v + LEAD - 1)
                        normal(*before)
                    if v == 2:
                        place_v(b, 3, before)
                    elif v % 4 == 2 and not last:
                        place_v(b + 1, v // 4 - 1, before)
                    if 10 <= v < 14:
                        bias(b, v - 10)
                    if v == 12 and exists(b + 2):
                        rsqrt(b + 2)
                    jobs(b, v, {"T": lo})
            pairs(pool, pro, body)


class Constants:

    def __init__(self, nc, ctx, cols):
        self.nc = nc
        self.ident = ctx.enter_context(nc.sbuf_tensor("ident", [P, P], F32))
        self.cols = ctx.enter_context(nc.sbuf_tensor("cols", [P, NCOL], F32))
        self.s_ident, self.s_cols = (ctx.enter_context(nc.semaphore(n)) for n in ("s_ident", "s_cols"))
        with nc.Block() as block:
            @block.gpsimd
            def _(pool):
                nc.gpsimd.memset(self.ident[:, :], 0.0).then_inc(self.s_ident, 1)
                pool.wait_ge(self.s_ident, 1)
                nc.gpsimd.affine_select(out=self.ident[:, :], in_=self.ident[:, :], compare_op=ALU.not_equal, fill=1.0,
                                        base=0, pattern=[[-1, P]], channel_multiplier=1).then_inc(self.s_ident, 1)

            @block.sync
            def _(sp):
                sp.dma_start(self.cols[:, :], cols).then_inc(self.s_cols, 16)

    def wait_ident(self, eng):
        eng.wait_ge(self.s_ident, 2)

    def wait_cols(self, eng):
        eng.wait_ge(self.s_cols, 16)

    def col(self, name):
        at, n = COL_AT[name]
        return self.cols[:, at:at + n]


def program(nc, a, out):
    with ExitStack() as ctx:
        cst = Constants(nc, ctx, a["cols"])
        c = cst.col
        x = [a["x"]] + [nc.dram_tensor(f"x_{i}", (B * S, D), F32).ap() for i in range(1, 5)] + [out]
        cross_attention(nc, "L0ca", cst, x[0], x[1], a["ctx"], c("L0_ln1_w"), c("L0_ln1_b"),
                        (c("L0_ln2_w"), c("L0_ln2_b")), a["L0_wq"], None, a["L0_wkv"][:, 0:D], None,
                        a["L0_wkv"][:, D:2 * D], None, a["L0_wo"], a["L0_bo"])
        feed_forward(nc, "L0ff", cst, x[1], x[2], c("L0_ln3_w"), c("L0_ln3_b"), a["L0_w1"], c("L0_b1"),
                     a["L0_w2"], a["L0_b2"])
        self_attention(nc, "L1sa", cst, x[2], x[3], c("L1_ln1_g"), c("L1_ln1_b"), a["L1_sa_wq"], c("L1_sa_bq"),
                       a["L1_sa_wk"], c("L1_sa_bk"), a["L1_sa_wv"], c("L1_sa_bv"), a["L1_sa_wo"], a["L1_sa_bo"])
        cross_attention(nc, "L1ca", cst, x[3], x[4], a["ctx"], c("L1_ln2_g"), c("L1_ln2_b"), None, a["L1_ca_wq"],
                        c("L1_ca_bq"), a["L1_ca_wk"], c("L1_ca_bk"), a["L1_ca_wv"], c("L1_ca_bv"), a["L1_ca_wo"],
                        a["L1_ca_bo"])
        feed_forward(nc, "L1ff", cst, x[4], x[5], c("L1_ln3_g"), c("L1_ln3_b"), a["L1_w1"], c("L1_mlp_b1"),
                     a["L1_w2"], a["L1_b2"])


def kernel(**inputs):
    import concourse.bacc as bacc
    from concourse.bass_utils import run_bass_kernel_spmd

    v = {k.replace("_xattn", ""): np.asarray(w) for k, w in inputs.items()}
    arrays = {
        "x": v["x"].reshape(B * S, D), "ctx": v["ctx_768"],
        "cols": np.concatenate([v[n].reshape(-1, P).T for n, _ in COLS], axis=1),
        "L0_wq": v["L0_Wq"], "L0_wkv": v["L0_Wkv"], "L0_wo": v["L0_Wproj"], "L0_w1": v["L0_W1"], "L0_w2": v["L0_W2"],
        "L0_bo": v["L0_bproj"], "L0_b2": v["L0_b2"], "L1_sa_bo": v["L1_sa_bo"], "L1_ca_bo": v["L1_ca_bo"],
        "L1_b2": v["L1_mlp_b2"],
        "L1_w1": v["L1_mlp_w1"].T, "L1_w2": v["L1_mlp_w2"].T,
    }
    for n in ("sa_wq", "sa_wk", "sa_wv", "sa_wo", "ca_wq", "ca_wk", "ca_wv", "ca_wo"):
        arrays[f"L1_{n}"] = v[f"L1_{n}"].T
    arrays = {k: np.ascontiguousarray(w) for k, w in arrays.items()}

    nc = bacc.Bacc("TRN2", target_bir_lowering=False, num_devices=1)
    aps = {k: nc.dram_tensor(f"in_{k}", w.shape, mybir.dt.from_np(w.dtype), kind="ExternalInput").ap()
           for k, w in arrays.items()}
    out = nc.dram_tensor("out", (B * S, D), F32, kind="ExternalOutput").ap()
    program(nc, aps, out)
    r = run_bass_kernel_spmd(nc, [{f"in_{k}": w for k, w in arrays.items()}], core_ids=[0])
    return r.results[0]["out"].reshape(B, S, D)
```
